# Optimizing a Trainium2 kernel written in Bass

```python
import numpy as np
import jax
import jax.numpy as jnp

def _softmax(x, axis=-1):
    return jax.nn.softmax(x, axis=axis)

def _gelu(x):
    return jax.nn.gelu(x, approximate=True)

def _silu(x):
    return jax.nn.silu(x)

def _sigmoid(x):
    return jax.nn.sigmoid(x)

def _layernorm(x, axis=-1, eps=1e-05):
    m = jnp.mean(x, axis=axis, keepdims=True)
    v = jnp.var(x, axis=axis, keepdims=True)
    return (x - m) / jnp.sqrt(v + eps)

def _scatter_add(tgt, idx, src, axis=0):
    return tgt.at[idx].add(src)

def _segment_sum(src, seg, n):
    return jax.ops.segment_sum(src, seg, n)
kernel_name = 'mk_xattn_ffn_d2_seqx_r8_9e40f2'

def setup_inputs(seed: int=0):
    np.random.seed(seed)
    _w = jnp.asarray

    def _rec_inputs():
        import jax
        import jax.numpy as jnp
        _rk = jax.random.key(seed)
        x = 7.22e-05 + 1 * jax.random.normal(jax.random.fold_in(_rk, 1), (8, 128, 512), jnp.float32)
        _lenS = 128 - jax.random.randint(jax.random.fold_in(_rk, 7), (8,), 0, max(1, 128 // 4) + 1, jnp.int32)
        _lenS2 = 128 - jax.random.randint(jax.random.fold_in(_rk, 8), (8,), 0, max(1, 128 // 4) + 1, jnp.int32)
        _ctx_4096P = jax.random.normal(jax.random.fold_in(_rk, 11), (8, 16, 512), jnp.float32)
        _ctx_4096c = jax.random.dirichlet(jax.random.fold_in(_rk, 511), 0.3 * jnp.ones((16,), jnp.float32), (8, 128))
        _ctx_4096t = jnp.einsum('bsk,bkd->bsd', _ctx_4096c, _ctx_4096P)
        _ctx_4096t = _ctx_4096t * jax.lax.rsqrt(jnp.mean(jnp.square(_ctx_4096t)) + 1e-12) * 0.953939
        ctx_4096 = 4.13588e-05 + 0.999923 * (_ctx_4096t + 0.3 * jax.random.normal(jax.random.fold_in(_rk, 611), (8, 128, 512), jnp.float32))
        _validS = jnp.arange(128)[None, :] < _lenS[:, None]
        _validS2 = jnp.arange(128)[None, :] < _lenS2[:, None]
        _causal = jnp.tril(jnp.ones((128, 128), dtype=bool))
        mask_BxSxS2_bk0 = jnp.logical_not(jnp.broadcast_to(_validS2[:, None, :], (8, 128, 128)))
        return (x, ctx_4096, mask_BxSxS2_bk0)
    x, ctx_4096, mask_BxSxS2_bk0 = _rec_inputs()

    def _L0_xattn_setup():
        import jax, jax.numpy as jnp
        import numpy as np
        B, LQ, LK, D, H, DH = (2, 128, 128, 512, 32, 128)
        EPS = 1e-05

        def _rmsnorm(x, weight):
            var = jnp.mean(jnp.square(x), axis=-1, keepdims=True)
            return x * jax.lax.rsqrt(var + EPS) * weight
        key = jax.random.key(seed)
        ks = jax.random.split(key, 8)
        scale = 0.02
        return {'hidden_states': jax.random.normal(ks[0], (B, LQ, D), jnp.float32), 'key_value_states': jax.random.normal(ks[1], (B, LK, D), jnp.float32), 'attention_mask': jax.random.randint(ks[2], (B, LQ, LK), 0, 2) > 0, 'position_bias': jax.random.normal(ks[3], (H, LQ, LK), jnp.float32), 'ln_weight': jnp.ones((D,), jnp.float32), 'w_q': jax.random.normal(ks[4], (H * DH, D), jnp.float32) * scale, 'w_k': jax.random.normal(ks[5], (H * DH, D), jnp.float32) * scale, 'w_v': jax.random.normal(ks[6], (H * DH, D), jnp.float32) * scale, 'w_out': jax.random.normal(ks[7], (D, H * DH), jnp.float32) * scale}
    _L0_xattn_all = _L0_xattn_setup()
    _L0_xattn_in = {k: v for k, v in _L0_xattn_all.items() if k in ('position_bias', 'ln_weight', 'w_q', 'w_k', 'w_v', 'w_out')}
    del _L0_xattn_all

    def _L0_ffn_setup():
        import jax, jax.numpy as jnp
        import numpy as np
        SCALING = 16.0 / 8.0
        GAMMA = 1.0
        EPS = 1e-12
        key = jax.random.key(seed)
        ks = jax.random.split(key, 8)
        B, T, H, O = (4, 256, 512, 512)
        E_tot, E_act, r = (16, 4, 8)
        return {'x': jax.random.normal(ks[0], (B, T, H), jnp.float32), 'W_base': jax.random.normal(ks[1], (O, H), jnp.float32) * 0.02, 'b_base': jax.random.normal(ks[2], (O,), jnp.float32) * 0.02, 'lora_A': jax.random.normal(ks[3], (E_tot, r, H), jnp.float32) * 0.02, 'lora_B': jax.random.normal(ks[4], (E_tot, O, r), jnp.float32) * 0.02, 'router_W': jax.random.normal(ks[5], (E_tot, H), jnp.float32) * 0.02, 'router_b': jax.random.normal(ks[6], (E_tot,), jnp.float32) * 0.02, 'domain_prior': jax.random.uniform(ks[7], (E_tot,), jnp.float32), 'active': jnp.arange(E_act, dtype=jnp.int32)}
    _L0_ffn_all = _L0_ffn_setup()
    _L0_ffn_in = {k: v for k, v in _L0_ffn_all.items() if k in ('W_base', 'b_base', 'lora_A', 'lora_B', 'router_W', 'router_b', 'domain_prior', 'active')}
    del _L0_ffn_all

    def _L1_xattn_setup():
        import jax, jax.numpy as jnp
        import numpy as np
        TEXT_DIM = 512
        FEATURE_DIM = 512

        def _xavier_uniform(key, shape):
            fan_in, fan_out = (shape[1], shape[0])
            limit = float(np.sqrt(6.0 / (fan_in + fan_out)))
            return jax.random.uniform(key, shape, jnp.float32, -limit, limit)
        key = jax.random.key(seed)
        k1, k2, k3, k4 = jax.random.split(key, 4)
        text = jax.random.normal(k1, (8, 256, TEXT_DIM), jnp.float32)
        features = jax.random.normal(k2, (8, 72, FEATURE_DIM), jnp.float32)
        Wq = _xavier_uniform(k3, (FEATURE_DIM, TEXT_DIM))
        bq = jnp.zeros((FEATURE_DIM,), jnp.float32)
        Wk = _xavier_uniform(k4, (FEATURE_DIM, FEATURE_DIM))
        bk = jnp.zeros((FEATURE_DIM,), jnp.float32)
        return {'text': text, 'features': features, 'Wq': Wq, 'bq': bq, 'Wk': Wk, 'bk': bk}
    _L1_xattn_all = _L1_xattn_setup()
    _L1_xattn_in = {k: v for k, v in _L1_xattn_all.items() if k in ('Wq', 'bq', 'Wk', 'bk')}
    del _L1_xattn_all

    def _L1_ffn_setup():
        import jax, jax.numpy as jnp
        import numpy as np
        IN_FEATURES = 512

        def _dequantize(qweight, scale, zero_point):
            N, K_packed = qweight.shape
            groups = K_packed // 3
            p = qweight.reshape(N, groups, 3)
            v0 = p[:, :, 0] & 63
            v1 = p[:, :, 0] >> 6 & 63
            v2 = p[:, :, 1] & 63
            v3 = p[:, :, 2] & 63
            unpacked = jnp.stack([v0, v1, v2, v3], axis=2).reshape(N, groups * 4)
            unpacked = unpacked[:, :IN_FEATURES]
            return (unpacked.astype(jnp.float32) - zero_point) * scale
        key = jax.random.key(seed)
        k1, k2, k3, k4, k5 = jax.random.split(key, 5)
        x = jax.random.normal(k1, (8, 256, 512), dtype=jnp.float32)
        qweight = jax.random.randint(k2, (512, 384), 0, 512, dtype=jnp.int32)
        weight_scale = jax.random.uniform(k3, (512, 1), dtype=jnp.float32) * 0.02 + 0.001
        weight_zero_point = jax.random.uniform(k4, (512, 1), dtype=jnp.float32) * 63.0
        bias = jax.random.normal(k5, (512,), dtype=jnp.float32)
        return {'x': x, 'qweight': qweight, 'weight_scale': weight_scale, 'weight_zero_point': weight_zero_point, 'bias': bias}
    _L1_ffn_all = _L1_ffn_setup()
    _L1_ffn_in = {k: v for k, v in _L1_ffn_all.items() if k in ('qweight', 'weight_scale', 'weight_zero_point', 'bias')}
    del _L1_ffn_all
    return {'x': x, 'ctx_4096': ctx_4096, 'mask_BxSxS2_bk0': mask_BxSxS2_bk0, 'L0_xattn_position_bias': _L0_xattn_in['position_bias'], 'L0_xattn_ln_weight': _L0_xattn_in['ln_weight'], 'L0_xattn_w_q': _L0_xattn_in['w_q'], 'L0_xattn_w_k': _L0_xattn_in['w_k'], 'L0_xattn_w_v': _L0_xattn_in['w_v'], 'L0_xattn_w_out': _L0_xattn_in['w_out'], 'L0_ffn_W_base': _L0_ffn_in['W_base'], 'L0_ffn_b_base': _L0_ffn_in['b_base'], 'L0_ffn_lora_A': _L0_ffn_in['lora_A'], 'L0_ffn_lora_B': _L0_ffn_in['lora_B'], 'L0_ffn_router_W': _L0_ffn_in['router_W'], 'L0_ffn_router_b': _L0_ffn_in['router_b'], 'L0_ffn_domain_prior': _L0_ffn_in['domain_prior'], 'L0_ffn_active': _L0_ffn_in['active'], 'L1_xattn_Wq': _L1_xattn_in['Wq'], 'L1_xattn_bq': _L1_xattn_in['bq'], 'L1_xattn_Wk': _L1_xattn_in['Wk'], 'L1_xattn_bk': _L1_xattn_in['bk'], 'L1_ffn_qweight': _L1_ffn_in['qweight'], 'L1_ffn_weight_scale': _L1_ffn_in['weight_scale'], 'L1_ffn_weight_zero_point': _L1_ffn_in['weight_zero_point'], 'L1_ffn_bias': _L1_ffn_in['bias']}

def reference(x, ctx_4096, mask_BxSxS2_bk0, L0_xattn_position_bias, L0_xattn_ln_weight, L0_xattn_w_q, L0_xattn_w_k, L0_xattn_w_v, L0_xattn_w_out, L0_ffn_W_base, L0_ffn_b_base, L0_ffn_lora_A, L0_ffn_lora_B, L0_ffn_router_W, L0_ffn_router_b, L0_ffn_domain_prior, L0_ffn_active, L1_xattn_Wq, L1_xattn_bq, L1_xattn_Wk, L1_xattn_bk, L1_ffn_qweight, L1_ffn_weight_scale, L1_ffn_weight_zero_point, L1_ffn_bias):
    import jax
    import jax.numpy as jnp

    def _L0_xattn_ref(hidden_states, key_value_states, attention_mask, position_bias, ln_weight, w_q, w_k, w_v, w_out):
        import jax, jax.numpy as jnp
        import numpy as np
        B, LQ, LK, D, H, DH = (2, 128, 128, 512, 32, 128)
        EPS = 1e-05

        def _rmsnorm(x, weight):
            var = jnp.mean(jnp.square(x), axis=-1, keepdims=True)
            return x * jax.lax.rsqrt(var + EPS) * weight
        x = _rmsnorm(hidden_states, ln_weight)
        b, lq, _ = x.shape
        lk = key_value_states.shape[1]
        h_q = (x @ w_q.T).reshape(b, lq, H, DH)
        h_k = (key_value_states @ w_k.T).reshape(b, lk, H, DH)
        h_v = (key_value_states @ w_v.T).reshape(b, lk, H, DH)
        score = jnp.einsum('bqhd,bkhd->bhqk', h_q, h_k)
        score = score + position_bias[None]
        m = attention_mask[:, None]
        score = jnp.where(m, score, -jnp.inf)
        score = jax.nn.softmax(score, axis=-1)
        score = jnp.where(m, score, 0.0)
        attn = jnp.einsum('bhqk,bkhd->bqhd', score, h_v).reshape(b, lq, H * DH)
        out = attn @ w_out.T
        return hidden_states + out

    def _L0_ffn_ref(x, W_base, b_base, lora_A, lora_B, router_W, router_b, domain_prior, active):
        import jax, jax.numpy as jnp
        import numpy as np
        SCALING = 16.0 / 8.0
        GAMMA = 1.0
        EPS = 1e-12
        y = jnp.einsum('bth,oh->bto', x, W_base) + b_base
        A = lora_A[active]
        Bm = lora_B[active]
        z = jnp.einsum('bth,erh->bter', x, A)
        contribs = jnp.einsum('bter,eor->bteo', z, Bm) * SCALING
        logits = jnp.einsum('bth,eh->bte', x, router_W) + router_b
        logits = logits[..., active]
        prior = domain_prior[active]
        alpha = jax.nn.softmax(jnp.log(prior + EPS) + logits / GAMMA, axis=-1)
        return y + jnp.einsum('bteo,bte->bto', contribs, alpha)

    def _L1_xattn_ref(text, features, Wq, bq, Wk, bk):
        import jax, jax.numpy as jnp
        import numpy as np
        TEXT_DIM = 512
        FEATURE_DIM = 512

        def _xavier_uniform(key, shape):
            fan_in, fan_out = (shape[1], shape[0])
            limit = float(np.sqrt(6.0 / (fan_in + fan_out)))
            return jax.random.uniform(key, shape, jnp.float32, -limit, limit)
        Q = jnp.einsum('btx,dx->btd', text, Wq) + bq
        K = jnp.einsum('bpx,dx->bpd', features, Wk) + bk
        scale = 1.0 / jnp.sqrt(jnp.asarray(K.shape[-1], K.dtype))
        scores = jnp.einsum('btd,bpd->btp', Q, K) * scale
        attn = jax.nn.softmax(scores, axis=-1)
        attended = jnp.einsum('btp,bpd->btd', attn, features)
        return attended

    def _L1_ffn_ref(x, qweight, weight_scale, weight_zero_point, bias):
        import jax, jax.numpy as jnp
        import numpy as np
        IN_FEATURES = 512

        def _dequantize(qweight, scale, zero_point):
            N, K_packed = qweight.shape
            groups = K_packed // 3
            p = qweight.reshape(N, groups, 3)
            v0 = p[:, :, 0] & 63
            v1 = p[:, :, 0] >> 6 & 63
            v2 = p[:, :, 1] & 63
            v3 = p[:, :, 2] & 63
            unpacked = jnp.stack([v0, v1, v2, v3], axis=2).reshape(N, groups * 4)
            unpacked = unpacked[:, :IN_FEATURES]
            return (unpacked.astype(jnp.float32) - zero_point) * scale
        w = _dequantize(qweight, weight_scale, weight_zero_point)
        return jnp.einsum('bsk,nk->bsn', x, w) + bias
    x = x + _L0_xattn_ref(_layernorm(x, axis=-1), ctx_4096, mask_BxSxS2_bk0, L0_xattn_position_bias, L0_xattn_ln_weight, L0_xattn_w_q, L0_xattn_w_k, L0_xattn_w_v, L0_xattn_w_out)
    x = x + _L0_ffn_ref(_layernorm(x, axis=-1), L0_ffn_W_base, L0_ffn_b_base, L0_ffn_lora_A, L0_ffn_lora_B, L0_ffn_router_W, L0_ffn_router_b, L0_ffn_domain_prior, L0_ffn_active)
    x = x + _L1_xattn_ref(_layernorm(x, axis=-1), ctx_4096, L1_xattn_Wq, L1_xattn_bq, L1_xattn_Wk, L1_xattn_bk)
    x = x + _L1_ffn_ref(_layernorm(x, axis=-1), L1_ffn_qweight, L1_ffn_weight_scale, L1_ffn_weight_zero_point, L1_ffn_bias)
    return x

_drawn_inputs = setup_inputs


def setup_inputs(seed=0):
    import zlib

    import numpy as np

    out = dict(_drawn_inputs(seed))
    spreads = {'L0_xattn_ln_weight': (1.0, 0.2), 'L1_xattn_bq': (0.0, 0.744), 'L1_xattn_bk': (0.0, 2.0)}
    factors = {'L0_ffn_b_base': 5.434,
     'L0_ffn_lora_A': 3.985,
     'L0_ffn_lora_B': 3.944,
     'L0_ffn_router_W': 8.0,
     'L0_ffn_router_b': 36.525,
     'L0_ffn_domain_prior': 8.0,
     'L1_ffn_weight_zero_point': 64.0}
    for name, (base, spread) in spreads.items():
        noise = np.random.default_rng([zlib.crc32(name.encode()), seed]).standard_normal(out[name].shape)
        drawn = base * np.exp(spread * noise) if base else spread * noise
        out[name] = jnp.asarray(drawn.astype(out[name].dtype))
    for name, factor in factors.items():
        out[name] = (out[name] * factor).astype(out[name].dtype)
    return out
```

```python
from contextlib import ExitStack

import concourse.bass as bass
from concourse import mybir

F32 = mybir.dt.float32
F32R = mybir.dt.float32r
I32 = mybir.dt.int32
U8 = mybir.dt.uint8
ALU = mybir.AluOpType
ACT = mybir.ActivationFunctionType
AX_X = mybir.AxisListType.X

P = 128
BATCH, D, HEADS = 8, 512, 32
NC = D // P
TOK = BATCH * P
HALF = TOK // 2
GROUPS = HEADS // 2
STEPS = 4 * GROUPS
LOOP_STEPS = 8
TURNS = STEPS // LOOP_STEPS
EXPERTS, ACTIVE, RANK = 16, 4, 8
ZL = ACTIVE * RANK + ACTIVE
LORA_SCALE = 16.0 / 8.0
EPS = 1e-5
PRIOR_EPS = 1e-12
MASKED = 3e38
SCORE_SCALE = float(D) ** -0.5


def wait_from(eng, sem, value):
    if not isinstance(value, int) or value > 0:
        eng.wait_ge(sem, value)


def build(nc, x, ctx_nat, ctx_t, mask, bias, ln_w, w_q, w_k, w_v, w_o, w_base, b_base, lora_a, lora_b,
          router_w, router_b, prior, active, wq1, bq1, wk1, bk1, qweight, w_scale, w_zero, ffn_bias, out):
    with ExitStack() as stack:
        top = [(nc.sbuf_base + 63) // 64 * 64]
        sizes = {F32: 4, F32R: 4, I32: 4, U8: 1}

        def place(name, shape, dt, at=None):
            size = sizes[dt]
            for n in shape[1:]:
                size *= n
            if at is None:
                at = top[0]
                top[0] += (size + 31) // 32 * 32
                assert top[0] <= nc.sbuf_usable_end, (name, top)
            return nc.alloc_sbuf_tensor_at(name, shape, dt, offset=at), at

        xt_hi, at_xt_hi = place("xt_hi", [P, NC, TOK], F32R)
        xt_lo, at_xt_lo = place("xt_lo", [P, NC, TOK], F32R)
        ct_hi, at_ct_hi = place("ct_hi", [P, NC, TOK], F32R)
        ct_lo, at_ct_lo = place("ct_lo", [P, NC, TOK], F32R)
        acc, _ = place("acc", [P, BATCH, D], F32)
        wq_hi, at_wq = place("wq_hi", [P, 2, NC, P], F32R)
        wq_lo, _ = place("wq_lo", [P, 2, NC, P], F32R)
        wk_hi, _ = place("wk_hi", [P, 2, NC, P], F32R)
        wk_lo, _ = place("wk_lo", [P, 2, NC, P], F32R)
        wv_hi, wv_lo, wo_hi, wo_lo, at_wv, at_wo = [0, 0], [0, 0], [0, 0], [0, 0], [0, 0], [0, 0]
        for n in range(2):
            wv_hi[n], at_wv[n] = place(f"wv_hi{n}", [P, NC, 2 * P], F32R)
            wv_lo[n], _ = place(f"wv_lo{n}", [P, NC, 2 * P], F32R)
            wo_hi[n], at_wo[n] = place(f"wo_hi{n}", [P, 2, D], F32R)
            wo_lo[n], _ = place(f"wo_lo{n}", [P, 2, D], F32R)
        raw_q, at_raw = place("raw_q", [P, 2, NC, P], F32)
        raw_k, _ = place("raw_k", [P, 2, NC, P], F32)
        raw_v, _ = place("raw_v", [P, NC, 2 * P], F32)
        raw_o, _ = place("raw_o", [P, 2, D], F32)
        qt, kt, vv, at_qkv = [0, 0], [0, 0], [0, 0], [0, 0]
        for n in range(2):
            qt[n], at_qkv[n] = place(f"qt{n}", [P, 2, HALF], F32)
            kt[n], _ = place(f"kt{n}", [P, 2, HALF], F32)
            vv[n], _ = place(f"vv{n}", [P, 4, 2 * P], F32)
        scores, probs, shift = [0, 0], [0, 0], [0, 0]
        for n in range(2):
            scores[n], _ = place(f"scores{n}", [P, 4, P], F32)
            probs[n], _ = place(f"probs{n}", [P, 4, P], F32)
            shift[n], _ = place(f"shift{n}", [P, 4, P], F32)
        probs_t, _ = place("probs_t", [P, 4, P], F32)
        att_hi, at_att_hi = place("att_hi", [P, 4, P], F32R)
        att_lo, _ = place("att_lo", [P, 4, P], F32R)
        bias_sb, _ = place("bias_sb", [P, 2, 2, P], F32)
        mask_sb, _ = place("mask_sb", [P, BATCH, P], F32)
        ident, _ = place("ident", [P, P], F32)
        ones, _ = place("ones", [P, P], F32)
        low_rank_in, _ = place("low_rank_in", [P, NC, ZL], F32)
        low_rank_out, _ = place("low_rank_out", [ACTIVE * RANK + 1, D], F32)
        normed, _ = place("normed", [P, 3, D], F32)
        row_max, _ = place("row_max", [P, 2, 4], F32)
        neg_max, _ = place("neg_max", [P, 2, 4], F32)
        row_sum, _ = place("row_sum", [P, 2, 4], F32)
        row_inv, _ = place("row_inv", [P, 2, 4], F32)
        row_fac, _ = place("row_fac", [P, 2, 4], F32)
        stats, _ = place("stats", [P, BATCH, 6], F32)
        mean_var, _ = place("mean_var", [P, BATCH, 2], F32)
        var_eps, _ = place("var_eps", [P, BATCH], F32)
        rstd, _ = place("rstd", [P, BATCH], F32)
        ms_a, _ = place("ms_a", [P, BATCH], F32)
        ms_b, _ = place("ms_b", [P, BATCH], F32)
        ms_eps, _ = place("ms_eps", [P, BATCH], F32)
        rms, _ = place("rms", [P, BATCH], F32)
        minus_half, _ = place("minus_half", [P, BATCH], F32)
        t_stats, _ = place("t_stats", [P, 3, BATCH, 6], F32)
        t_mv, _ = place("t_mv", [P, 3, BATCH, 2], F32)
        t_ve, _ = place("t_ve", [P, 3, BATCH], F32)
        t_rstd, _ = place("t_rstd", [P, 3, BATCH], F32)
        uw, _ = place("uw", [P, 9], F32)
        bqk, _ = place("bqk", [P, 2, NC], F32)
        bqk_mul, _ = place("bqk_mul", [P, NC], F32)
        bqk_sum, _ = place("bqk_sum", [P, 1], F32)
        act_i, _ = place("act_i", [1, ACTIVE], I32)
        act_f, _ = place("act_f", [1, 3, ACTIVE], F32)
        targets, _ = place("targets", [1, ZL], F32)
        iota_r, _ = place("iota_r", [1, RANK], I32)
        iota_p, _ = place("iota_p", [P, 1], I32)
        iota_rf, _ = place("iota_rf", [1, RANK], F32)
        iota_pf, _ = place("iota_pf", [P, 1], F32)
        select, _ = place("select", [P, ZL], F32)
        rb_sb, _ = place("rb_sb", [EXPERTS, 2], F32)
        logit_bias, _ = place("logit_bias", [P, 3, ACTIVE], F32)
        logits, _ = place("logits", [P, BATCH, ACTIVE], F32)
        l_max, _ = place("l_max", [P, BATCH, 2], F32)
        l_exp, _ = place("l_exp", [P, BATCH, ACTIVE], F32)
        l_sum, _ = place("l_sum", [P, BATCH, 2], F32)
        alpha, _ = place("alpha", [P, BATCH, ACTIVE], F32)
        z_mix, _ = place("z_mix", [P, 2, ACTIVE * RANK + 1], F32)
        b_max, _ = place("b_max", [P, BATCH, 2], F32)
        b_sum, _ = place("b_sum", [P, BATCH, 2], F32)
        x_sum, _ = place("x_sum", [P, BATCH, 2], F32)
        prior_eps, _ = place("prior_eps", [P, 1], F32)

        raw_ct = [place(f"raw_ct{n}", [P, NC, HALF], F32, at=at_wo[n])[0] for n in range(2)]
        mask_raw, _ = place("mask_raw", [P, BATCH, P], U8, at=at_qkv[1])
        ln_w_rows, _ = place("ln_w_rows", [P, D], F32, at=at_att_hi)
        rms_in = [place(f"rms_in{n}", [P, D], F32, at=at_qkv[1] + 4096 + 2048 * n)[0] for n in range(2)]

        wk1_raw, _ = place("wk1_raw", [P, NC, D], F32, at=at_raw)
        wq1_raw, _ = place("wq1_raw", [P, NC, D], F32, at=at_raw + 8192)
        wk1_hi, _ = place("wk1_hi", [P, NC, D], F32R, at=at_wv[0])
        wk1_lo, _ = place("wk1_lo", [P, NC, D], F32R, at=at_wo[0])
        wq1_hi, _ = place("wq1_hi", [P, NC, D], F32R, at=at_wq)
        wq1_lo, _ = place("wq1_lo", [P, NC, D], F32R, at=at_wq + 8192)
        mm_hi, _ = place("mm_hi", [P, NC, D], F32R, at=at_raw)
        mm_lo, _ = place("mm_lo", [P, NC, D], F32R, at=at_raw + 8192)
        gg, _ = place("gg", [P, NC, TOK], F32, at=at_xt_hi)
        base_hi, _ = place("base_hi", [P, NC, D], F32R, at=at_xt_lo)
        base_lo, _ = place("base_lo", [P, NC, D], F32R, at=at_xt_lo + 8192)
        base_raw, _ = place("base_raw", [P, NC, D], F32, at=at_qkv[0])
        r_row, _ = place("r_row", [P, TOK], F32, at=at_qkv[0] + 8192)
        lora_a_sb, _ = place("lora_a_sb", [P, D], F32, at=at_wv[1])
        lora_b_sb, _ = place("lora_b_sb", [P, D], F32, at=at_wv[1] + 2048)
        router_sb, _ = place("router_sb", [EXPERTS, D], F32, at=at_wv[1] + 4096)
        rb_cols, _ = place("rb_cols", [EXPERTS, 2, P], F32, at=at_wv[1] + 6144)
        ww_hi, _ = place("ww_hi", [P, NC, P], F32R, at=at_wo[1])
        ww_lo, _ = place("ww_lo", [P, NC, P], F32R, at=at_wo[1] + 2048)
        ww_f, _ = place("ww_f", [P, NC, P], F32, at=at_wo[1] + 4096)
        ctx_sb, _ = place("ctx_sb", [P, BATCH, D], F32, at=at_wv[0])
        codes, _ = place("codes", [P, NC, D], F32R, at=at_wq)
        packed, _ = place("packed", [P, 3, D], I32, at=at_wq + 8192)
        unpack, _ = place("unpack", [P, D], I32, at=at_wq + 8192 + 6144)
        zero_rows, _ = place("zero_rows", [P, D], F32, at=at_ct_lo)
        scale_rows, _ = place("scale_rows", [P, D], F32, at=at_ct_lo + 2048)
        bias_rows, _ = place("bias_rows", [P, D], F32, at=at_ct_lo + 4096)
        f_scr = [place(f"f_scr{n}", [P, D], F32, at=at_ct_lo + 6144 + 2048 * n)[0] for n in range(4)]
        a_hi, _ = place("a_hi", [P, NC, P], F32R, at=at_ct_hi)
        a_lo, _ = place("a_lo", [P, NC, P], F32R, at=at_ct_hi + 2048)
        a_full, _ = place("a_full", [P, NC, P], F32, at=at_ct_hi + 4096)
        b_full, _ = place("b_full", [P, NC, P], F32, at=at_ct_hi + 6144)
        c_hi, _ = place("c_hi", [P, NC, P], F32R, at=at_ct_hi + 8192)
        c_lo, _ = place("c_lo", [P, NC, P], F32R, at=at_ct_hi + 10240)
        b_probs, _ = place("b_probs", [P, P], F32, at=at_ct_hi + 12288)
        b_probs_t, _ = place("b_probs_t", [P, P], F32, at=at_ct_hi + 12800)
        z_mix_t, _ = place("z_mix_t", [ACTIVE * RANK + 1, P], F32, at=at_ct_hi + 13312)
        junk, _ = place("junk", [P, D], F32, at=at_ct_hi + 13824)

        def bank(name):
            return stack.enter_context(nc.psum_tensor(name, [P, D], F32))

        ps_s, ps_t, ps_pv, ps_q, ps_k, ps_v = (bank(f"ps_{n}") for n in "s t pv q k v".split())
        ps_o = [bank("ps_o0"), bank("ps_o1")]

        def blocks(t):
            return t[:].rearrange("p (n c) -> p n c", c=P)

        S = {}

        def sem(name):
            S[name] = stack.enter_context(nc.semaphore(name))
            return S[name]

        ct_in = [sem(f"ct_in{n}") for n in range(2)]
        x_in = [sem(f"x_in{n}") for n in range(2)]
        wq_in, wk_in, wv_in, wo_in = sem("wq_in"), sem("wk_in"), sem("wv_in"), sem("wo_in")
        bias_in = [sem("bias_in0"), sem("bias_in1")]
        mask_in, ln_in = sem("mask_in"), sem("ln_in")
        const_done, ident_zero, ident_done, mask_done = sem("const_done"), sem("ident_zero"), sem("ident_done"), sem("mask_done")
        ct_hi_done, ct_lo_done = sem("ct_hi_done"), sem("ct_lo_done")
        x_chain, x_ve, x_rstd, x_ms, x_rms = sem("x_chain"), sem("x_ve"), sem("x_rstd"), sem("x_ms"), sem("x_rms")
        x_normed, x_resid, x_h, x_t, x_hi, x_lo = (sem(n) for n in ("x_normed", "x_resid", "x_h", "x_t", "x_hi", "x_lo"))
        wq_hi_s, wq_lo_s, wk_hi_s, wk_lo_s = (sem(n) for n in ("wq_hi_s", "wq_lo_s", "wk_hi_s", "wk_lo_s"))
        wv_hi_s, wv_lo_s, wo_hi_s, wo_lo_s = (sem(n) for n in ("wv_hi_s", "wv_lo_s", "wo_hi_s", "wo_lo_s"))
        q_done, k_done, v_done, q_out, k_out, v_out = (sem(n) for n in ("q_done", "k_done", "v_done", "q_out", "k_out", "v_out"))
        s_done, s_shifted, s_max, s_neg, e_done, s_inv, s_fac, p_done = (
            sem(n) for n in ("s_done", "s_shifted", "s_max", "s_neg", "e_done", "s_inv", "s_fac", "p_done"))
        shift_done, pt_done, pt_out, pv_done, att_hi_s, att_lo_s, o_done, o_added = (
            sem(n) for n in ("shift_done", "pt_done", "pt_out", "pv_done", "att_hi_s", "att_lo_s", "o_done", "o_added"))
        w1_in = [sem("wk1_in"), sem("wq1_in")]
        w1_hi_s, w1_lo_s = sem("w1_hi_s"), sem("w1_lo_s")
        vec_in, vec_mul, vec_sum, vec_mm, vec_out = (sem(n) for n in ("vec_in", "vec_mul", "vec_sum", "vec_mm", "vec_out"))
        mm_done, mm_hi_s, mm_out = sem("mm_done"), sem("mm_hi_s"), sem("mm_out")
        g_done, g_out = sem("g_done"), sem("g_out")
        ww_s, ww_hi_s, ww_lo_s, r_done, r_out = (sem(n) for n in ("ww_s", "ww_hi_s", "ww_lo_s", "r_done", "r_out"))
        base_in, base_hi_s, base_lo_s = sem("base_in"), sem("base_hi_s"), sem("base_lo_s")
        act_in, lora_in, act_chain, iota_s, tgt_mm, sel_s, rbc_s = (
            sem(n) for n in ("act_in", "lora_in", "act_chain", "iota_s", "tgt_mm", "sel_s", "rbc_s"))
        lr_mm, lr_out, lb_mm, lb_out, lbias = (sem(n) for n in ("lr_mm", "lr_out", "lb_mm", "lb_out", "lbias"))
        ctx_in, packed_in, rows_in, unp, codes_s = (sem(n) for n in ("ctx_in", "packed_in", "rows_in", "unp", "codes_s"))
        n_st = [sem(f"n_st{k}") for k in range(3)]
        n_mv = [sem(f"n_mv{k}") for k in range(3)]
        n_ve = [sem(f"n_ve{k}") for k in range(3)]
        n_rs = [sem(f"n_rs{k}") for k in range(3)]
        n_xn = [sem(f"n_xn{k}") for k in range(3)]
        n_t = [sem(f"n_t{k}") for k in range(3)]
        a_full_s, a_hi_s, a_lo_s, z_mm, y_mm, zt_mm, zt_out, a_add = (
            sem(n) for n in ("a_full_s", "a_hi_s", "a_lo_s", "z_mm", "y_mm", "zt_mm", "zt_out", "a_add"))
        lg_c, lg_exp, z_mixed = sem("lg_c"), sem("lg_exp"), sem("z_mixed")
        b_full_s, bs_mm, b_c, b_exp, bt_mm, bt_out, at_mm, b_inv, b_add = (
            sem(n) for n in ("b_full_s", "bs_mm", "b_c", "b_exp", "bt_mm", "bt_out", "at_mm", "b_inv", "b_add"))
        c_hi_s, c_lo_s, c_sum, c_neg, c_mm, c_zero, c_scaled, c_bias, c_add = (
            sem(n) for n in ("c_hi_s", "c_lo_s", "c_sum", "c_neg", "c_mm", "c_zero", "c_scaled", "c_bias", "c_add"))
        stored = sem("stored")

        block = stack.enter_context(nc.Block())

        def three(pe, dst, hi_l, lo_l, hi_r, lo_r, first, last):
            pe.matmul(dst, hi_l, hi_r, start=first, stop=False)
            pe.matmul(dst, hi_l, lo_r, start=False, stop=False)
            return pe.matmul(dst, lo_l, hi_r, start=False, stop=last)

        @block.sync
        def _(sp):
            def halves(t):
                return t.rearrange("(b p) d -> p b d", p=P)

            sp.dma_start(raw_ct[0][:], ctx_t[:, :, 0:HALF]).then_inc(ct_in[0], 16)
            sp.dma_start(raw_k[:].rearrange("p h c d -> p (h c d)"), w_k[0]).then_inc(wk_in, 16)
            sp.dma_start(acc[:, 0:4, :], halves(x)[:, 0:4, :]).then_inc(x_in[0], 16)
            sp.dma_start(raw_v[:].rearrange("p c d -> p (c d)"), w_v[0]).then_inc(wv_in, 16)
            sp.dma_start(raw_q[:].rearrange("p h c d -> p (h c d)"), w_q[0]).then_inc(wq_in, 16)
            sp.dma_start(raw_ct[1][:], ctx_t[:, :, HALF:TOK]).then_inc(ct_in[1], 16)
            sp.dma_start(acc[:, 4:8, :], halves(x)[:, 4:8, :]).then_inc(x_in[1], 16)
            sp.dma_start(raw_o[:].rearrange("p h d -> p (h d)"), w_o[0]).then_inc(wo_in, 16)
            sp.wait_ge(wv_lo_s, 1)
            sp.dma_start(raw_v[:].rearrange("p c d -> p (c d)"), w_v[1]).then_inc(wv_in, 16)

            def load_group(g, more, parity):
                sp.wait_ge(wq_lo_s, 2 * g)
                sp.dma_start(raw_q[:].rearrange("p h c d -> p (h c d)"), w_q[g]).then_inc(wq_in, 16)
                sp.wait_ge(wk_lo_s, 2 * g)
                sp.dma_start(raw_k[:].rearrange("p h c d -> p (h c d)"), w_k[g]).then_inc(wk_in, 16)
                wait_from(sp, shift_done, 4 * g - 4)
                sp.dma_start(bias_sb[:, parity], bias[g]).then_inc(bias_in[parity], 16)
                sp.wait_ge(wo_lo_s, g)
                sp.dma_start(raw_o[:].rearrange("p h d -> p (h d)"), w_o[g]).then_inc(wo_in, 16)
                if more:
                    sp.wait_ge(wv_lo_s, g + 1)
                    sp.dma_start(raw_v[:].rearrange("p c d -> p (c d)"), w_v[g + 1]).then_inc(wv_in, 16)

            load_group(1, True, 1)
            with sp.Fori(1, TURNS - 1) as i:
                load_group(2 * i, True, 0)
                load_group(2 * i + 1, True, 1)
            load_group(GROUPS - 2, True, 0)
            load_group(GROUPS - 1, False, 1)

            sp.wait_ge(wq_lo_s, 2 * GROUPS)
            sp.wait_ge(wk_lo_s, 2 * GROUPS)
            sp.dma_start(wk1_raw[:], wk1).then_inc(w1_in[0], 16)
            sp.wait_ge(wv_lo_s, GROUPS)
            sp.wait_ge(wo_lo_s, GROUPS)
            sp.dma_start(wq1_raw[:], wq1).then_inc(w1_in[1], 16)
            sp.wait_ge(v_done, STEPS)
            sp.dma_start(lora_a_sb[:], lora_a).then_inc(lora_in, 16)
            sp.dma_start(lora_b_sb[:], lora_b).then_inc(lora_in, 16)
            sp.dma_start(router_sb[:], router_w).then_inc(lora_in, 16)
            sp.wait_ge(pv_done, STEPS - 2)
            sp.dma_start(base_raw[:], w_base).then_inc(base_in, 16)
            sp.wait_ge(mm_done, NC)
            sp.dma_start(packed[:], qweight).then_inc(packed_in, 16)
            sp.dma_start(ctx_sb[:], ctx_nat.rearrange("(b p) d -> p b d", p=P)).then_inc(ctx_in, 16)
            sp.wait_ge(g_done, 2 * NC)
            sp.wait_ge(r_done, 2)
            sp.dma_start(zero_rows[:], w_zero.broadcast_to([P, D])).then_inc(rows_in, 16)
            sp.dma_start(scale_rows[:], w_scale.broadcast_to([P, D])).then_inc(rows_in, 16)
            sp.dma_start(bias_rows[:], ffn_bias.broadcast_to([P, D])).then_inc(rows_in, 16)
            for b in range(BATCH):
                sp.wait_ge(c_add, b + 1)
                sp.dma_start(out[b * P:(b + 1) * P, :], acc[:, b, :]).then_inc(stored, 16)
            sp.wait_ge(stored, 16 * BATCH)

        @block.scalar
        def _(act):
            act.dma_start(ln_w_rows[:], ln_w.broadcast_to([P, D])).then_inc(ln_in, 16)
            act.dma_start(bias_sb[:, 0], bias[0]).then_inc(bias_in[0], 16)
            act.dma_start(mask_raw[:], mask).then_inc(mask_in, 16)
            act.dma_start(act_i[:], active).then_inc(act_in, 16)
            act.dma_start(rb_sb[:, 0:1], router_b).then_inc(act_in, 16)
            act.dma_start(rb_sb[:, 1:2], prior).then_inc(act_in, 16)
            act.dma_start(low_rank_out[ACTIVE * RANK:ACTIVE * RANK + 1, :], b_base).then_inc(act_in, 16)
            act.dma_start(bqk[:, 0, :], bq1).then_inc(vec_in, 16)
            act.dma_start(bqk[:, 1, :], bk1).then_inc(vec_in, 16)

            def split_ct(half):
                act.wait_ge(ct_in[half], 16)
                for c in range(NC):
                    act.copy(ct_hi[:, c, half * HALF:(half + 1) * HALF], raw_ct[half][:, c, :]).then_inc(ct_hi_done, 1)

            def split_qk(g, head):
                wait_from(act, wq_in, 16 * (g + 1))
                wait_from(act, q_done, 4 * g - 1 + head)
                act.copy(wq_hi[:, head], raw_q[:, head]).then_inc(wq_hi_s, 1)
                wait_from(act, wk_in, 16 * (g + 1))
                wait_from(act, k_done, 4 * g - 1 + head)
                act.copy(wk_hi[:, head], raw_k[:, head]).then_inc(wk_hi_s, 1)

            def split_v(g, n):
                wait_from(act, wv_in, 16 * (g + 1))
                wait_from(act, v_done, 4 * g - 4)
                act.copy(wv_hi[n][:], raw_v[:]).then_inc(wv_hi_s, 1)

            def split_o(g, n):
                wait_from(act, wo_in, 16 * (g + 1))
                wait_from(act, o_done, 8 * g - 8)
                act.copy(wo_hi[n][:], raw_o[:]).then_inc(wo_hi_s, 1)

            def k_evac(t, n, part):
                wait_from(act, k_done, t + 1)
                act.copy(kt[n][:, part, :], ps_k[:]).then_inc(k_out, 1)

            def q_evac(t, n, part):
                wait_from(act, q_done, t + 1)
                act.copy(qt[n][:, part, :], ps_q[:]).then_inc(q_out, 1)

            def x_high(b):
                act.wait_ge(x_t, b + 1)
                act.copy(xt_hi[:, :, b * P:(b + 1) * P], blocks(ps_o[b % 2])).then_inc(x_hi, 1)

            split_ct(0)
            act.wait_ge(wk_in, 16)
            act.copy(wk_hi[:, 0], raw_k[:, 0]).then_inc(wk_hi_s, 1)
            act.copy(wk_hi[:, 1], raw_k[:, 1]).then_inc(wk_hi_s, 1)
            split_v(0, 0)
            k_evac(0, 0, 0)
            k_evac(1, 0, 1)
            act.wait_ge(wq_in, 16)
            act.copy(wq_hi[:, 0], raw_q[:, 0]).then_inc(wq_hi_s, 1)
            act.copy(wq_hi[:, 1], raw_q[:, 1]).then_inc(wq_hi_s, 1)
            for b in range(4):
                x_high(b)
            split_ct(1)
            q_evac(0, 0, 0)
            q_evac(1, 0, 1)
            for b in range(4, 8):
                x_high(b)
            act.wait_ge(ct_lo_done, NC)
            split_o(0, 0)
            split_v(1, 1)

            def attention_high(s):
                wait_from(act, pv_done, s + 1)
                act.copy(att_hi[:], blocks(ps_pv)).then_inc(att_hi_s, 1)

            def exponentials(s, n):
                act.wait_ge(s_neg, s + 1)
                wait_from(act, pt_done, s - 1)
                for m in range(4):
                    e = act.activation(probs[n][:, m, :], scores[n][:, m, :], ACT.Exp,
                                       bias=neg_max[:, n, m:m + 1], accum_out=row_sum[:, n, m:m + 1])
                e.then_inc(e_done, 1)

            def pt_evac(s):
                act.wait_ge(pt_done, s + 1)
                act.copy(probs_t[:], blocks(ps_t)).then_inc(pt_out, 1)

            def step(i, c):
                s = LOOP_STEPS * i + c
                g = 2 * i + c // 4
                n = c % 2
                if c > 0 or not isinstance(i, int) or i > 0:
                    attention_high(s - 1)
                exponentials(s, n)
                q_evac(s + 2, (c // 2 + 1) % 2, n)
                k_evac(s + 2, (c // 2 + 1) % 2, n)
                pt_evac(s)
                last = isinstance(i, int) and i == TURNS - 1
                if c % 4 < 2 and not (last and c >= 4):
                    split_qk(g + 1, c % 4)
                if c % 4 == 2 and not (last and c >= 4):
                    split_o(g + 1, (c // 4 + 1) % 2)
                if c % 4 == 3 and not last:
                    split_v(g + 2, (c // 4) % 2)

            for c in range(LOOP_STEPS):
                step(0, c)
            with act.Fori(1, TURNS - 1) as i:
                for c in range(LOOP_STEPS):
                    step(i, c)
            for c in range(LOOP_STEPS - 4):
                step(TURNS - 1, c)
            step(TURNS - 1, 4)
            step(TURNS - 1, 5)
            attention_high(STEPS - 3)
            act.wait_ge(w1_in[0], 16)
            act.wait_ge(v_done, 4 * (GROUPS - 1))
            for c in range(NC):
                act.copy(wk1_hi[:, c, :], wk1_raw[:, c, :]).then_inc(w1_hi_s, 1)
            act.wait_ge(w1_in[1], 16)
            act.wait_ge(q_done, STEPS)
            act.wait_ge(k_done, STEPS)
            for c in range(NC):
                act.copy(wq1_hi[:, c, :], wq1_raw[:, c, :]).then_inc(w1_hi_s, 1)

            def mm_high(m):
                act.wait_ge(mm_done, m + 1)
                if m == 0:
                    act.wait_ge(w1_lo_s, 2 * NC)
                    act.wait_ge(vec_mm, 1)
                act.copy(mm_hi[:, m, :], (ps_q, ps_k)[m % 2][:]).then_inc(mm_hi_s, 1)

            exponentials(STEPS - 2, 0)
            mm_high(0)
            pt_evac(STEPS - 2)
            mm_high(1)
            mm_high(2)
            attention_high(STEPS - 2)
            act.wait_ge(lr_mm, 1)
            act.activation(logit_bias[:, 0, :], ps_v[:, 148:152], ACT.Ln, bias=prior_eps[:, 0:1]).then_inc(lbias, 1)
            mm_high(3)
            exponentials(STEPS - 1, 1)
            act.wait_ge(base_in, 16)
            for c in range(NC):
                act.copy(base_hi[:, c, :], base_raw[:, c, :]).then_inc(base_hi_s, 1)
            pt_evac(STEPS - 1)
            attention_high(STEPS - 1)
            act.wait_ge(ww_s, NC)
            act.wait_ge(o_done, 2 * STEPS)
            act.copy(ww_hi[:], ww_f[:]).then_inc(ww_hi_s, 1)
            for v in range(4):
                act.wait_ge(unp, v + 1)
                act.copy(codes[:, v, :], unpack[:]).then_inc(codes_s, 1)

            act.wait_ge(g_done, 2 * NC)
            act.wait_ge(r_done, 2)

            def stage_a(b):
                act.wait_ge(n_t[0], b + 1)
                wait_from(act, z_mm, b)
                act.copy(a_full[:], blocks(ps_s)).then_inc(a_full_s, 1)
                wait_from(act, y_mm, b)
                act.copy(a_hi[:], blocks(ps_s)).then_inc(a_hi_s, 1)

            def stage_a_exp(b):
                act.wait_ge(lg_c, 3 * b + 3)
                act.activation(l_exp[:, b, :], logits[:, b, :], ACT.Exp, bias=l_max[:, b, 1:2],
                               accum_out=l_sum[:, b, 0:1]).then_inc(lg_exp, 1)

            def stage_a_zt(b):
                act.wait_ge(zt_mm, b + 1)
                wait_from(act, y_mm, b)
                act.copy(z_mix_t[:], ps_k[0:ACTIVE * RANK + 1, P:2 * P]).then_inc(zt_out, 1)

            def stage_b(b):
                act.wait_ge(n_t[1], b + 1)
                wait_from(act, bs_mm, b)
                act.copy(b_full[:], blocks(ps_t)).then_inc(b_full_s, 1)

            def stage_b_exp(b):
                act.wait_ge(b_c, 2 * b + 2)
                wait_from(act, bt_mm, b)
                act.activation(b_probs[:], ps_v[:, 0:P], ACT.Exp, bias=b_max[:, b, 1:2], scale=SCORE_SCALE,
                               accum_out=b_sum[:, b, 0:1]).then_inc(b_exp, 1)

            def stage_b_pt(b):
                act.wait_ge(bt_mm, b + 1)
                wait_from(act, at_mm, b)
                act.copy(b_probs_t[:], ps_v[:, 2 * P:3 * P]).then_inc(bt_out, 1)

            def stage_c(b):
                act.wait_ge(n_xn[2], b + 1)
                wait_from(act, c_sum, b)
                act.activation(junk[:], normed[:, 2, :], ACT.Copy, accum_out=x_sum[:, b, 0:1]).then_inc(c_sum, 1)
                act.wait_ge(n_t[2], b + 1)
                wait_from(act, c_mm, b)
                act.copy(c_hi[:], blocks(ps_pv)).then_inc(c_hi_s, 1)

            for w in range(BATCH + 2):
                a, b, c = w, w - 1, w - 2
                if a < BATCH:
                    stage_a(a)
                if 0 <= b < BATCH:
                    stage_b(b)
                if 0 <= c < BATCH:
                    stage_c(c)
                if a < BATCH:
                    stage_a_exp(a)
                if 0 <= b < BATCH:
                    stage_b_exp(b)
                if a < BATCH:
                    stage_a_zt(a)
                if 0 <= b < BATCH:
                    stage_b_pt(b)

        @block.gpsimd
        def _(pool):
            pool.memset(ident[:], 0.0).then_inc(ident_zero, 1)
            pool.memset(ones[:], 1.0).then_inc(const_done, 1)
            pool.memset(minus_half[:], -0.5).then_inc(const_done, 1)
            pool.memset(prior_eps[:], PRIOR_EPS).then_inc(const_done, 1)
            pool.memset(z_mix[:, :, ACTIVE * RANK:ACTIVE * RANK + 1], 1.0).then_inc(const_done, 1)
            pool.iota(iota_r[:], pattern=[[1, RANK]], base=0, channel_multiplier=0).then_inc(iota_s, 1)
            pool.iota(iota_p[:], pattern=[[1, 1]], base=0, channel_multiplier=1).then_inc(iota_s, 1)
            pool.wait_ge(ident_zero, 1)
            pool.affine_select(out=ident[:], in_=ident[:], compare_op=ALU.not_equal, fill=1.0, base=0,
                               pattern=[[-1, P]], channel_multiplier=1).then_inc(ident_done, 1)

            def rest_qk(head, g):
                wait_from(pool, wq_hi_s, 2 * g + head + 1)
                pool.tensor_tensor(wq_lo[:, head], raw_q[:, head], wq_hi[:, head].bitcast(F32),
                                   ALU.subtract).then_inc(wq_lo_s, 1)
                wait_from(pool, wk_hi_s, 2 * g + head + 1)
                pool.tensor_tensor(wk_lo[:, head], raw_k[:, head], wk_hi[:, head].bitcast(F32),
                                   ALU.subtract).then_inc(wk_lo_s, 1)

            def rest_v(g, n):
                wait_from(pool, wv_hi_s, g + 1)
                pool.tensor_tensor(wv_lo[n][:], raw_v[:], wv_hi[n][:].bitcast(F32), ALU.subtract).then_inc(wv_lo_s, 1)

            def rest_o(g, n):
                wait_from(pool, wo_hi_s, g + 1)
                pool.tensor_tensor(wo_lo[n][:], raw_o[:], wo_hi[n][:].bitcast(F32), ALU.subtract).then_inc(wo_lo_s, 1)

            def make_shift(s, c):
                n = c % 2
                first = 4 * (c // 2 % 2) + 2 * n
                wait_from(pool, s_shifted, s - 1)
                bias_b = bias_sb[:, c // 4 % 2].unsqueeze(1).broadcast_to([P, 2, 2, P])
                mask_b = mask_sb[:, first:first + 2, :].unsqueeze(2).broadcast_to([P, 2, 2, P])
                pool.tensor_tensor(shift[n][:].rearrange("p (b h) k -> p b h k", b=2), bias_b, mask_b,
                                   ALU.add).then_inc(shift_done, 1)

            def x_scale(half):
                cols = slice(4 * half, 4 * half + 4)
                pool.wait_ge(x_ve, half + 1)
                pool.tensor_tensor(rstd[:, cols], var_eps[:, cols], minus_half[:, 0:4], ALU.pow).then_inc(x_rstd, 1)
                pool.wait_ge(x_ms, half + 1)
                pool.tensor_tensor(rms[:, cols], ms_eps[:, cols], minus_half[:, 0:4], ALU.pow).then_inc(x_rms, 1)

            def x_residual(b):
                pool.wait_ge(x_normed, b + 1)
                pool.tensor_tensor(acc[:, b, :], acc[:, b, :], normed[:, b % 2, :], ALU.add).then_inc(x_resid, 1)

            pool.wait_ge(const_done, 2)
            pool.wait_ge(wk_hi_s, 1)
            pool.tensor_tensor(wk_lo[:, 0], raw_k[:, 0], wk_hi[:, 0].bitcast(F32), ALU.subtract).then_inc(wk_lo_s, 1)
            pool.wait_ge(wk_hi_s, 2)
            pool.tensor_tensor(wk_lo[:, 1], raw_k[:, 1], wk_hi[:, 1].bitcast(F32), ALU.subtract).then_inc(wk_lo_s, 1)
            x_scale(0)
            rest_v(0, 0)
            for b in range(2):
                x_residual(b)
            pool.wait_ge(wq_hi_s, 1)
            pool.tensor_tensor(wq_lo[:, 0], raw_q[:, 0], wq_hi[:, 0].bitcast(F32), ALU.subtract).then_inc(wq_lo_s, 1)
            pool.wait_ge(wq_hi_s, 2)
            pool.tensor_tensor(wq_lo[:, 1], raw_q[:, 1], wq_hi[:, 1].bitcast(F32), ALU.subtract).then_inc(wq_lo_s, 1)
            for b in range(2, 4):
                x_residual(b)
            x_scale(1)
            pool.wait_ge(mask_done, 1)
            pool.wait_ge(bias_in[0], 16)
            make_shift(0, 0)
            for b in range(4, 8):
                x_residual(b)
            rest_o(0, 0)
            rest_v(1, 1)

            def step(i, c):
                s = LOOP_STEPS * i + c
                g = 2 * i + c // 4
                last = isinstance(i, int) and i == TURNS - 1
                if not (last and c == LOOP_STEPS - 1):
                    if c == 3:
                        pool.wait_ge(bias_in[1], 16 * (i + 1))
                    if c == 7:
                        pool.wait_ge(bias_in[0], 16 * (i + 2))
                    make_shift(s + 1, (c + 1) % LOOP_STEPS)
                if c % 4 < 2 and not (last and c >= 4):
                    rest_qk(c % 4, g + 1)
                if c % 4 == 2 and not (last and c >= 4):
                    rest_o(g + 1, (c // 4 + 1) % 2)
                if c % 4 == 3 and not last:
                    rest_v(g + 2, (c // 4) % 2)

            for c in range(LOOP_STEPS):
                step(0, c)
            with pool.Fori(1, TURNS - 1) as i:
                for c in range(LOOP_STEPS):
                    step(i, c)
            for c in range(LOOP_STEPS):
                step(TURNS - 1, c)
            for c in range(NC):
                pool.wait_ge(base_hi_s, c + 1)
                pool.tensor_tensor(base_lo[:, c, :], base_raw[:, c, :], base_hi[:, c, :].bitcast(F32),
                                   ALU.subtract).then_inc(base_lo_s, 1)
            pool.wait_ge(ww_hi_s, 1)
            pool.tensor_tensor(ww_lo[:], ww_f[:], ww_hi[:].bitcast(F32), ALU.subtract).then_inc(ww_lo_s, 1)

            def inv_std(stage, b):
                pool.wait_ge(n_ve[stage], b + 1)
                pool.tensor_tensor(t_rstd[:, stage, b:b + 1], t_ve[:, stage, b:b + 1], minus_half[:, 0:1],
                                   ALU.pow).then_inc(n_rs[stage], 1)

            pool.wait_ge(rows_in, 48)
            for w in range(BATCH + 2):
                a, b, c = w, w - 1, w - 2
                if a < BATCH:
                    inv_std(0, a)
                if 0 <= b < BATCH:
                    inv_std(1, b)
                if 0 <= c < BATCH:
                    inv_std(2, c)
                    wait_from(pool, c_add, c - 1)
                    pool.wait_ge(b_add, c + 1)
                    pool.tensor_tensor(f_scr[c % 2][:], acc[:, c, :], bias_rows[:], ALU.add).then_inc(c_bias, 1)
                    pool.wait_ge(c_zero, c + 1)
                    pool.tensor_tensor(f_scr[2 + c % 2][:], f_scr[2 + c % 2][:], scale_rows[:],
                                       ALU.mult).then_inc(c_scaled, 1)

        @block.vector
        def _(dve):
            def ct_rest(half):
                for c in range(NC):
                    cols = slice(half * HALF, (half + 1) * HALF)
                    dve.wait_ge(ct_hi_done, NC * half + c + 1)
                    dve.tensor_tensor(ct_lo[:, c, cols], raw_ct[half][:, c, :], ct_hi[:, c, cols].bitcast(F32),
                                      ALU.subtract).then_inc(ct_lo_done, 1)

            def x_statistics(half):
                dve.wait_ge(x_in[half], 16)
                tiles = range(4 * half, 4 * half + 4)
                at = 11 * half
                for b in tiles:
                    dve.bn_stats(stats[:, b, :], acc[:, b, :]).then_inc(x_chain, 1)
                for n, b in enumerate(tiles):
                    dve.wait_ge(x_chain, at + n + 1)
                    dve.bn_aggr(mean_var[:, b, :], stats[:, b, :]).then_inc(x_chain, 1)
                cols = slice(4 * half, 4 * half + 4)
                var = mean_var[:, cols, 1]
                dve.wait_ge(x_chain, at + 8)
                dve.tensor_scalar(var_eps[:, cols], var, EPS, None, ALU.add).then_inc(x_ve, 1)
                dve.wait_ge(x_rstd, half + 1)
                dve.tensor_tensor(ms_a[:, cols], var, rstd[:, cols], ALU.mult).then_inc(x_chain, 1)
                dve.wait_ge(x_chain, at + 9)
                dve.tensor_tensor(ms_b[:, cols], ms_a[:, cols], rstd[:, cols], ALU.mult).then_inc(x_chain, 1)
                dve.wait_ge(x_chain, at + 10)
                dve.tensor_scalar(ms_eps[:, cols], ms_b[:, cols], EPS, None, ALU.add).then_inc(x_ms, 1)
                dve.sem_inc(x_chain, 1)

            def x_tile(b):
                if b % 4 == 0:
                    dve.wait_ge(x_rms, b // 4 + 1)
                wait_from(dve, x_resid, b - 1)
                dve.tensor_scalar(normed[:, b % 2, :], acc[:, b, :], mean_var[:, b, 0:1], rstd[:, b:b + 1],
                                  ALU.subtract, ALU.mult).then_inc(x_normed, 1)
                dve.wait_ge(x_normed, b + 1)
                wait_from(dve, x_t, b - 1)
                dve.scalar_tensor_tensor(rms_in[b % 2][:], normed[:, b % 2, :], rms[:, b:b + 1], ln_w_rows[:],
                                         ALU.mult, ALU.mult).then_inc(x_h, 1)

            def x_rest(b):
                dve.wait_ge(x_hi, b + 1)
                cols = slice(b * P, (b + 1) * P)
                dve.tensor_tensor(xt_lo[:, :, cols], blocks(ps_o[b % 2]), xt_hi[:, :, cols].bitcast(F32),
                                  ALU.subtract).then_inc(x_lo, 1)

            def v_evac(t, n, part):
                wait_from(dve, v_done, t + 1)
                dve.tensor_copy(vv[n][:, 2 * part:2 * part + 2, :],
                                ps_v[:].rearrange("p (b c) -> p b c", b=2)).then_inc(v_out, 1)

            ct_rest(0)
            dve.wait_ge(mask_in, 16)
            dve.tensor_scalar(mask_sb[:], mask_raw[:], 1.0, MASKED, ALU.subtract, ALU.mult).then_inc(mask_done, 1)
            x_statistics(0)
            v_evac(0, 0, 0)
            dve.wait_ge(ln_in, 16)
            for b in range(4):
                x_tile(b)
                if b > 0:
                    x_rest(b - 1)
            x_rest(3)
            ct_rest(1)
            x_statistics(1)
            for b in range(4, 8):
                x_tile(b)
                if b > 4:
                    x_rest(b - 1)
            x_rest(7)

            def attention_rest(s):
                wait_from(dve, att_hi_s, s + 1)
                dve.tensor_tensor(att_lo[:], blocks(ps_pv), att_hi[:].bitcast(F32), ALU.subtract).then_inc(att_lo_s, 1)

            def add_output(s, c):
                for j in range(2):
                    b = 4 * (c // 2 % 2) + 2 * (c % 2) + j
                    wait_from(dve, o_done, 2 * s + j + 1)
                    if isinstance(s, int) and s < 4:
                        dve.wait_ge(x_resid, b + 1)
                    else:
                        dve.wait_ge(o_added, 2 * s - 6)
                    dve.tensor_tensor(acc[:, b, :], ps_o[j][:], acc[:, b, :], ALU.add).then_inc(o_added, 1)

            def step(i, c, drain=False):
                s = LOOP_STEPS * i + c
                n = c % 2
                start = isinstance(i, int) and i == 0 and c == 0
                if not start and not drain:
                    attention_rest(s - 1)
                dve.wait_ge(s_done, s + 1)
                dve.wait_ge(shift_done, s + 1)
                wait_from(dve, e_done, s - 1)
                dve.tensor_tensor(scores[n][:], blocks(ps_s), shift[n][:], ALU.add).then_inc(s_shifted, 1)
                dve.wait_ge(s_shifted, s + 1)
                dve.tensor_reduce(row_max[:, n, :], scores[n][:], AX_X, ALU.max).then_inc(s_max, 1)
                dve.wait_ge(s_max, s + 1)
                dve.tensor_scalar(neg_max[:, n, :], row_max[:, n, :], -1.0, None, ALU.mult).then_inc(s_neg, 1)
                if not drain:
                    v_evac(s + 1, ((c + 1) // 2) % 2, (c + 1) % 2)
                dve.wait_ge(e_done, s + 1)
                dve.reciprocal(row_inv[:, n, :], row_sum[:, n, :]).then_inc(s_inv, 1)
                dve.wait_ge(s_inv, s + 1)
                dve.scalar_tensor_tensor(row_fac[:, n, :], row_max[:, n, :], -MASKED / 3.0, row_inv[:, n, :],
                                         ALU.is_gt, ALU.mult).then_inc(s_fac, 1)
                dve.wait_ge(s_fac, s + 1)
                dve.tensor_tensor(probs[n][:], probs[n][:], row_fac[:, n, :].unsqueeze(2).broadcast_to([P, 4, P]),
                                  ALU.mult).then_inc(p_done, 1)
                if not start:
                    add_output(s - 1, (c - 1) % LOOP_STEPS)

            for c in range(LOOP_STEPS):
                step(0, c)
            with dve.Fori(1, TURNS - 1) as i:
                for c in range(LOOP_STEPS):
                    step(i, c)
            for c in range(6):
                step(TURNS - 1, c)

            attention_rest(STEPS - 3)
            v_evac(STEPS - 1, 1, 1)

            dve.wait_ge(act_in, 64)
            dve.wait_ge(iota_s, 2)
            dve.tensor_copy(act_f[:, 0, :], act_i[:]).then_inc(act_chain, 1)
            dve.tensor_copy(iota_rf[:], iota_r[:]).then_inc(act_chain, 1)
            dve.tensor_copy(iota_pf[:], iota_p[:]).then_inc(act_chain, 1)
            dve.wait_ge(act_chain, 3)
            dve.tensor_scalar(act_f[:, 1, :], act_f[:, 0, :], 0.0, float(EXPERTS), ALU.is_lt, ALU.mult).then_inc(act_chain, 1)
            dve.wait_ge(act_chain, 4)
            dve.tensor_tensor(act_f[:, 2, :], act_f[:, 0, :], act_f[:, 1, :], ALU.add).then_inc(act_chain, 1)
            dve.wait_ge(act_chain, 5)
            dve.tensor_scalar(targets[:, ACTIVE * RANK:ZL], act_f[:, 2, :], 0.0, float(EXPERTS - 1), ALU.max,
                              ALU.min).then_inc(act_chain, 1)
            dve.wait_ge(act_chain, 6)
            for j in range(ACTIVE):
                dve.scalar_tensor_tensor(targets[:, j * RANK:(j + 1) * RANK],
                                         targets[:, ACTIVE * RANK + j:ACTIVE * RANK + j + 1].broadcast_to([1, RANK]),
                                         float(RANK), iota_rf[:], ALU.mult, ALU.add).then_inc(act_chain, 1)
            dve.wait_ge(vec_in, 32)
            dve.tensor_tensor(bqk_mul[:], bqk[:, 0, :], bqk[:, 1, :], ALU.mult).then_inc(vec_mul, 1)
            dve.wait_ge(vec_mul, 1)
            dve.tensor_reduce(bqk_sum[:], bqk_mul[:], AX_X, ALU.add).then_inc(vec_sum, 1)

            dve.wait_ge(o_done, 2 * (STEPS - 4))
            for c in range(NC):
                dve.wait_ge(w1_hi_s, c + 1)
                dve.tensor_tensor(wk1_lo[:, c, :], wk1_raw[:, c, :], wk1_hi[:, c, :].bitcast(F32),
                                  ALU.subtract).then_inc(w1_lo_s, 1)
            for c in range(NC):
                dve.wait_ge(w1_hi_s, NC + c + 1)
                dve.tensor_tensor(wq1_lo[:, c, :], wq1_raw[:, c, :], wq1_hi[:, c, :].bitcast(F32),
                                  ALU.subtract).then_inc(w1_lo_s, 1)

            def mm_rest(m):
                dve.wait_ge(mm_hi_s, m + 1)
                dve.tensor_tensor(mm_lo[:, m, :], (ps_q, ps_k)[m % 2][:], mm_hi[:, m, :].bitcast(F32),
                                  ALU.subtract).then_inc(mm_out, 1)

            def g_evac(m, half):
                n = 2 * m + half
                dve.wait_ge(g_done, n + 1)
                dve.tensor_scalar(gg[:, m, half * HALF:(half + 1) * HALF], (ps_q, ps_k)[n % 2][:],
                                  uw[:, m:m + 1], None, ALU.add).then_inc(g_out, 1)

            dve.wait_ge(vec_mm, 1)
            dve.tensor_copy(uw[:], ps_v[:, 0:9]).then_inc(vec_out, 1)
            dve.wait_ge(tgt_mm, 1)
            dve.wait_ge(act_chain, 10)
            dve.tensor_scalar(select[:], ps_v[:, 0:ZL], iota_pf[:, 0:1], None, ALU.is_equal).then_inc(sel_s, 1)
            dve.wait_ge(v_done, STEPS)
            for n in range(2):
                dve.tensor_scalar(rb_cols[:, n, :], ones[0:EXPERTS, :], rb_sb[:, n:n + 1], None,
                                  ALU.mult).then_inc(rbc_s, 1)
            step(TURNS - 1, 6, drain=True)
            mm_rest(0)
            mm_rest(1)
            mm_rest(2)
            attention_rest(STEPS - 2)
            dve.wait_ge(lr_mm, 1)
            dve.wait_ge(lbias, 1)
            dve.tensor_copy(low_rank_in[:], ps_v[:, 0:NC * ZL].rearrange("p (c z) -> p c z", z=ZL)).then_inc(lr_out, 1)
            dve.wait_ge(lr_out, 1)
            dve.tensor_tensor(logit_bias[:, 1, :], logit_bias[:, 0, :], ps_v[:, 144:148], ALU.add).then_inc(lr_out, 1)
            mm_rest(3)
            step(TURNS - 1, 7, drain=True)
            dve.wait_ge(lb_mm, 1)
            dve.tensor_copy(low_rank_out[0:ACTIVE * RANK, :], ps_v[0:ACTIVE * RANK, :]).then_inc(lb_out, 1)
            g_evac(0, 0)
            g_evac(0, 1)
            attention_rest(STEPS - 1)
            g_evac(1, 0)
            g_evac(1, 1)
            add_output(STEPS - 1, LOOP_STEPS - 1)
            dve.wait_ge(vec_out, 1)
            dve.wait_ge(o_done, 2 * STEPS)
            for c in range(NC):
                dve.tensor_scalar(ww_f[:, c, :], ones[:], uw[:, NC + c:NC + c + 1], None, ALU.mult).then_inc(ww_s, 1)
            g_evac(2, 0)
            g_evac(2, 1)
            dve.wait_ge(packed_in, 16)
            for v, (word, down) in enumerate(((0, 0), (0, 6), (1, 0), (2, 0))):
                wait_from(dve, codes_s, v)
                dve.tensor_scalar(unpack[:], packed[:, word, :], down, 63, ALU.logical_shift_right,
                                  ALU.bitwise_and).then_inc(unp, 1)
            g_evac(3, 0)
            g_evac(3, 1)
            for half in range(2):
                dve.wait_ge(r_done, half + 1)
                dve.tensor_scalar(r_row[:, half * HALF:(half + 1) * HALF], ps_v[:], uw[:, 2 * NC:2 * NC + 1],
                                  None, ALU.add).then_inc(r_out, 1)

            def normalise(stage, b, before, count):
                dve.wait_ge(before, count)
                dve.bn_stats(t_stats[:, stage, b, :], acc[:, b, :]).then_inc(n_st[stage], 1)
                dve.wait_ge(n_st[stage], b + 1)
                dve.bn_aggr(t_mv[:, stage, b, :], t_stats[:, stage, b, :]).then_inc(n_mv[stage], 1)
                dve.wait_ge(n_mv[stage], b + 1)
                dve.tensor_scalar(t_ve[:, stage, b:b + 1], t_mv[:, stage, b, 1:2], EPS, None,
                                  ALU.add).then_inc(n_ve[stage], 1)

            def normalise_end(stage, b):
                dve.wait_ge(n_rs[stage], b + 1)
                wait_from(dve, n_t[stage], b)
                if stage == 2:
                    wait_from(dve, c_sum, b)
                dve.tensor_scalar(normed[:, stage, :], acc[:, b, :], t_mv[:, stage, b, 0:1],
                                  t_rstd[:, stage, b:b + 1], ALU.subtract, ALU.mult).then_inc(n_xn[stage], 1)

            def a_rest(b):
                dve.wait_ge(a_hi_s, b + 1)
                dve.tensor_tensor(a_lo[:], blocks(ps_s), a_hi[:].bitcast(F32), ALU.subtract).then_inc(a_lo_s, 1)

            def a_route(b):
                dve.wait_ge(z_mm, b + 1)
                dve.tensor_tensor(logits[:, b, :], ps_k[:, ACTIVE * RANK:ZL], logit_bias[:, 1, :],
                                  ALU.add).then_inc(lg_c, 1)
                dve.wait_ge(lg_c, 3 * b + 1)
                dve.tensor_reduce(l_max[:, b, 0:1], logits[:, b, :], AX_X, ALU.max).then_inc(lg_c, 1)
                dve.wait_ge(lg_c, 3 * b + 2)
                dve.tensor_scalar(l_max[:, b, 1:2], l_max[:, b, 0:1], -1.0, None, ALU.mult).then_inc(lg_c, 1)

            def a_mix(b):
                dve.wait_ge(lg_exp, b + 1)
                dve.reciprocal(l_sum[:, b, 1:2], l_sum[:, b, 0:1]).then_inc(z_mixed, 1)
                dve.wait_ge(z_mixed, 3 * b + 1)
                dve.tensor_scalar(alpha[:, b, :], l_exp[:, b, :], l_sum[:, b, 1:2], LORA_SCALE, ALU.mult,
                                  ALU.mult).then_inc(z_mixed, 1)
                dve.wait_ge(z_mixed, 3 * b + 2)
                wait_from(dve, zt_mm, b - 1)
                dve.tensor_tensor(z_mix[:, b % 2, 0:ACTIVE * RANK].rearrange("p (e r) -> p e r", r=RANK),
                                  ps_k[:, 0:ACTIVE * RANK].rearrange("p (e r) -> p e r", r=RANK),
                                  alpha[:, b, :].unsqueeze(2).broadcast_to([P, ACTIVE, RANK]),
                                  ALU.mult).then_inc(z_mixed, 1)

            def a_finish(b):
                dve.wait_ge(y_mm, b + 1)
                dve.wait_ge(n_xn[0], b + 1)
                dve.tensor_tensor(acc[:, b, :], ps_q[:], acc[:, b, :], ALU.add).then_inc(a_add, 1)

            def b_softmax(b):
                dve.wait_ge(bs_mm, b + 1)
                dve.tensor_reduce(b_max[:, b, 0:1], ps_v[:, 0:P], AX_X, ALU.max).then_inc(b_c, 1)
                dve.wait_ge(b_c, 2 * b + 1)
                dve.tensor_scalar(b_max[:, b, 1:2], b_max[:, b, 0:1], -SCORE_SCALE, None, ALU.mult).then_inc(b_c, 1)

            def b_finish(b):
                dve.wait_ge(b_exp, b + 1)
                dve.reciprocal(b_sum[:, b, 1:2], b_sum[:, b, 0:1]).then_inc(b_inv, 1)
                dve.wait_ge(b_inv, b + 1)
                dve.wait_ge(at_mm, b + 1)
                dve.scalar_tensor_tensor(acc[:, b, :], ps_o[0][:], b_sum[:, b, 1:2], acc[:, b, :], ALU.mult,
                                         ALU.add).then_inc(b_add, 1)

            def c_rest(b):
                dve.wait_ge(c_hi_s, b + 1)
                dve.tensor_tensor(c_lo[:], blocks(ps_pv), c_hi[:].bitcast(F32), ALU.subtract).then_inc(c_lo_s, 1)
                dve.wait_ge(c_sum, b + 1)
                dve.tensor_scalar(x_sum[:, b, 1:2], x_sum[:, b, 0:1], -1.0, None, ALU.mult).then_inc(c_neg, 1)

            def c_zero_point(b):
                dve.wait_ge(c_neg, b + 1)
                dve.wait_ge(c_mm, b + 1)
                wait_from(dve, c_add, b - 1)
                dve.scalar_tensor_tensor(f_scr[2 + b % 2][:], zero_rows[:], x_sum[:, b, 1:2], ps_o[1][:], ALU.mult,
                                         ALU.add).then_inc(c_zero, 1)

            def c_finish(b):
                dve.wait_ge(c_scaled, b + 1)
                dve.wait_ge(c_bias, b + 1)
                dve.tensor_tensor(acc[:, b, :], f_scr[2 + b % 2][:], f_scr[b % 2][:], ALU.add).then_inc(c_add, 1)

            dve.wait_ge(rows_in, 48)
            for w in range(BATCH + 2):
                a, b, c = w, w - 1, w - 2
                has_a, has_b, has_c = a < BATCH, 0 <= b < BATCH, 0 <= c < BATCH
                if has_a:
                    normalise(0, a, o_added, 2 * STEPS)
                if has_b:
                    normalise(1, b, a_add, b + 1)
                if has_c:
                    normalise(2, c, b_add, c + 1)
                if has_a:
                    normalise_end(0, a)
                if has_b:
                    normalise_end(1, b)
                if has_c:
                    normalise_end(2, c)
                if has_a:
                    a_rest(a)
                if has_c:
                    c_rest(c)
                if has_a:
                    a_route(a)
                if has_b:
                    b_softmax(b)
                if has_a:
                    a_mix(a)
                if has_c:
                    c_zero_point(c)
                if has_b:
                    b_finish(b)
                if has_a:
                    a_finish(a)
                if has_c:
                    c_finish(c)

        @block.tensor
        def _(pe):
            def project_k(t, c):
                head, half = c % 2, c // 2 % 2
                cols = slice(half * HALF, (half + 1) * HALF)
                for m in range(NC):
                    last = three(pe, ps_k[:], wk_hi[:, head, m, :], wk_lo[:, head, m, :], ct_hi[:, m, cols],
                                 ct_lo[:, m, cols], m == 0, m == NC - 1)
                last.then_inc(k_done, 1)

            def project_q(t, c):
                head, half = c % 2, c // 2 % 2
                cols = slice(half * HALF, (half + 1) * HALF)
                for m in range(NC):
                    last = three(pe, ps_q[:], wq_hi[:, head, m, :], wq_lo[:, head, m, :], xt_hi[:, m, cols],
                                 xt_lo[:, m, cols], m == 0, m == NC - 1)
                last.then_inc(q_done, 1)

            def project_v(t, c):
                n, first = c // 4 % 2, 4 * (c // 2 % 2) + 2 * (c % 2)
                for j in range(2):
                    cols = slice((first + j) * P, (first + j + 1) * P)
                    for m in range(NC):
                        last = three(pe, ps_v[:, j * 2 * P:(j + 1) * 2 * P], ct_hi[:, m, cols], ct_lo[:, m, cols],
                                     wv_hi[n][:, m, :], wv_lo[n][:, m, :], m == 0, m == NC - 1)
                last.then_inc(v_done, 1)

            def x_transpose(b):
                pe.wait_ge(x_h, b + 1)
                wait_from(pe, x_lo, b - 1)
                for m in range(NC):
                    last = pe.transpose(ps_o[b % 2][:, m * P:(m + 1) * P], rms_in[b % 2][:, m * P:(m + 1) * P], ident[:])
                last.then_inc(x_t, 1)

            pe.wait_ge(ct_lo_done, NC)
            pe.wait_ge(wk_lo_s, 1)
            project_k(0, 0)
            pe.wait_ge(wk_lo_s, 2)
            pe.wait_ge(k_out, 1)
            project_k(1, 1)
            pe.wait_ge(wv_lo_s, 1)
            project_v(0, 0)
            pe.wait_ge(v_out, 1)
            project_v(1, 1)
            pe.wait_ge(ident_done, 1)
            for b in range(4):
                x_transpose(b)
            pe.wait_ge(x_lo, 4)
            pe.wait_ge(wq_lo_s, 1)
            project_q(0, 0)
            pe.wait_ge(wq_lo_s, 2)
            pe.wait_ge(q_out, 1)
            project_q(1, 1)
            for b in range(4, 8):
                x_transpose(b)
            pe.wait_ge(ct_lo_done, 2 * NC)
            pe.wait_ge(x_lo, 8)

            def output(s, c, g=None):
                wait_from(pe, att_lo_s, s + 1)
                if g is not None:
                    pe.wait_ge(wo_lo_s, g + 1)
                n = c // 4 % 2
                for j in range(2):
                    wait_from(pe, o_added, 2 * s + j - 1)
                    for h in range(2):
                        last = three(pe, ps_o[j][:], att_hi[:, 2 * j + h, :], att_lo[:, 2 * j + h, :],
                                     wo_hi[n][:, h, :], wo_lo[n][:, h, :], h == 0, h == 1)
                    last.then_inc(o_done, 1)

            def step_scores(s, c):
                u0 = s - c % 2
                pe.wait_ge(q_out, u0 + 2)
                pe.wait_ge(k_out, u0 + 2)
                wait_from(pe, s_shifted, s)
                n = c // 2 % 2
                for j in range(2):
                    cols = slice((2 * (c % 2) + j) * P, (2 * (c % 2) + j + 1) * P)
                    for h in range(2):
                        m = 2 * j + h
                        last = pe.matmul(ps_s[:, m * P:(m + 1) * P], qt[n][:, h, cols], kt[n][:, h, cols],
                                         start=True, stop=True)
                last.then_inc(s_done, 1)

            def step_transpose(s, c):
                pe.wait_ge(p_done, s + 1)
                wait_from(pe, pt_out, s)
                for m in range(4):
                    last = pe.transpose(ps_t[:, m * P:(m + 1) * P], probs[c % 2][:, m, :], ident[:])
                last.then_inc(pt_done, 1)

            def step_values(s, c):
                pe.wait_ge(pt_out, s + 1)
                pe.wait_ge(v_out, s - c % 2 + 2)
                wait_from(pe, att_lo_s, s)
                n = c // 2 % 2
                for j in range(2):
                    for h in range(2):
                        m = 2 * j + h
                        last = pe.matmul(ps_pv[:, m * P:(m + 1) * P], vv[n][:, 2 * (c % 2) + j, h * P:(h + 1) * P],
                                         probs_t[:, m, :], start=True, stop=True)
                last.then_inc(pv_done, 1)

            def step(i, c):
                s = LOOP_STEPS * i + c
                t, tc = s + 2, (c + 2) % LOOP_STEPS
                gt = 2 * i + (c + 2) // 4
                step_scores(s, c)
                pe.wait_ge(wq_lo_s, 2 * gt + c % 2 + 1)
                pe.wait_ge(q_out, t)
                project_q(t, tc)
                if c > 0 or not isinstance(i, int) or i > 0:
                    output(s - 1, (c - 1) % LOOP_STEPS, 2 * i + c // 4 if c % 4 == 1 else None)
                pe.wait_ge(wk_lo_s, 2 * gt + c % 2 + 1)
                pe.wait_ge(k_out, t)
                project_k(t, tc)
                step_transpose(s, c)
                pe.wait_ge(wv_lo_s, gt + 1)
                pe.wait_ge(v_out, t)
                project_v(t, tc)
                step_values(s, c)

            for c in range(LOOP_STEPS):
                step(0, c)
            with pe.Fori(1, TURNS - 1) as i:
                for c in range(LOOP_STEPS):
                    step(i, c)
            for c in range(6):
                step(TURNS - 1, c)

            def product_m(m):
                if m == 0:
                    pe.wait_ge(w1_lo_s, 2 * NC)
                    pe.wait_ge(q_out, STEPS)
                    pe.wait_ge(k_out, STEPS)
                wait_from(pe, mm_out, m - 1)
                cols = slice(m * P, (m + 1) * P)
                for c in range(NC):
                    last = three(pe, (ps_q, ps_k)[m % 2][:], wk1_hi[:, c, cols], wk1_lo[:, c, cols], wq1_hi[:, c, :],
                                 wq1_lo[:, c, :], c == 0, c == NC - 1)
                last.then_inc(mm_done, 1)

            def product_g(m, half):
                n = 2 * m + half
                if n == 0:
                    pe.wait_ge(mm_out, NC)
                wait_from(pe, g_out, n - 1)
                cols, rows = slice(m * P, (m + 1) * P), slice(half * HALF, (half + 1) * HALF)
                for c in range(NC):
                    last = three(pe, (ps_q, ps_k)[n % 2][:], mm_hi[:, c, cols], mm_lo[:, c, cols], ct_hi[:, c, rows],
                                 ct_lo[:, c, rows], c == 0, c == NC - 1)
                last.then_inc(g_done, 1)

            s = STEPS - 2
            step_scores(s, 6)
            pe.wait_ge(v_out, STEPS)
            pe.wait_ge(w1_in[0], 16)
            pe.wait_ge(w1_in[1], 16)
            pe.wait_ge(vec_in, 32)
            pe.wait_ge(vec_sum, 1)
            pe.wait_ge(const_done, 4)
            for k, (w_raw, vec) in enumerate(((wq1_raw, 1), (wk1_raw, 0))):
                for m in range(NC):
                    for c in range(NC):
                        pe.matmul(ps_v[:, NC * k + m:NC * k + m + 1], w_raw[:, c, m * P:(m + 1) * P],
                                  bqk[:, vec, c:c + 1], start=(c == 0), stop=(c == NC - 1))
            pe.matmul(ps_v[:, 2 * NC:2 * NC + 1], ones[:], bqk_sum[:], start=True, stop=True).then_inc(vec_mm, 1)
            product_m(0)
            output(s - 1, 5)
            pe.wait_ge(vec_out, 1)
            pe.wait_ge(act_chain, 10)
            pe.matmul(ps_v[:, 0:ZL], ones[0:1, :], targets[:], start=True, stop=True).then_inc(tgt_mm, 1)
            product_m(1)
            step_transpose(s, 6)
            product_m(2)
            step_values(s, 6)
            pe.wait_ge(sel_s, 1)
            pe.wait_ge(rbc_s, 2)
            pe.wait_ge(lora_in, 48)
            for c in range(NC):
                cols = slice(c * P, (c + 1) * P)
                pe.matmul(ps_v[:, c * ZL:c * ZL + ACTIVE * RANK], lora_a_sb[:, cols], select[:, 0:ACTIVE * RANK],
                          start=True, stop=True)
                pe.matmul(ps_v[:, c * ZL + ACTIVE * RANK:(c + 1) * ZL], router_sb[:, cols],
                          select[0:EXPERTS, ACTIVE * RANK:ZL], start=True, stop=True)
            for n in range(2):
                last = pe.matmul(ps_v[:, NC * ZL + ACTIVE * n:NC * ZL + ACTIVE * (n + 1)], rb_cols[:, n, :],
                                 select[0:EXPERTS, ACTIVE * RANK:ZL], start=True, stop=True)
            last.then_inc(lr_mm, 1)
            product_m(3)
            s = STEPS - 1
            step_scores(s, 7)
            output(s - 1, 6)
            pe.wait_ge(lr_out, 2)
            pe.matmul(ps_v[0:ACTIVE * RANK, :], select[:, 0:ACTIVE * RANK], lora_b_sb[:], start=True,
                      stop=True).then_inc(lb_mm, 1)
            product_g(0, 0)
            step_transpose(s, 7)
            product_g(0, 1)
            step_values(s, 7)
            product_g(1, 0)
            product_g(1, 1)
            output(s, 7)
            for m in range(2, NC):
                for half in range(2):
                    product_g(m, half)
            pe.wait_ge(ww_lo_s, 1)
            pe.wait_ge(lb_out, 1)
            for half in range(2):
                wait_from(pe, r_out, half)
                rows = slice(half * HALF, (half + 1) * HALF)
                for c in range(NC):
                    last = three(pe, ps_v[:], ww_hi[:, c, :], ww_lo[:, c, :], ct_hi[:, c, rows], ct_lo[:, c, rows],
                                 c == 0, c == NC - 1)
                last.then_inc(r_done, 1)

            banks = (ps_s, ps_t, ps_pv)

            def transpose(stage, b, freed):
                pe.wait_ge(n_xn[stage], b + 1)
                wait_from(pe, freed, b)
                if b == 0 and stage == 0:
                    pe.wait_ge(s_shifted, STEPS)
                if b == 0 and stage == 1:
                    pe.wait_ge(pt_out, STEPS)
                if b == 0 and stage == 2:
                    pe.wait_ge(att_lo_s, STEPS)
                for m in range(NC):
                    src = normed[:, stage, m * P:(m + 1) * P] if stage < 2 else normed[:, stage, m:D:NC]
                    last = pe.transpose(banks[stage][:, m * P:(m + 1) * P], src, ident[:])
                last.then_inc(n_t[stage], 1)

            def a_low_rank(b):
                pe.wait_ge(a_full_s, b + 1)
                wait_from(pe, zt_out, b)
                wait_from(pe, z_mixed, 3 * b)
                for c in range(NC):
                    last = pe.matmul(ps_k[:, 0:ZL], a_full[:, c, :], low_rank_in[:, c, :], start=(c == 0),
                                     stop=(c == NC - 1))
                last.then_inc(z_mm, 1)

            def a_base(b):
                pe.wait_ge(a_lo_s, b + 1)
                if b == 0:
                    pe.wait_ge(base_lo_s, NC)
                    pe.wait_ge(g_out, 2 * NC)
                wait_from(pe, a_add, b)
                for c in range(NC):
                    three(pe, ps_q[:], a_hi[:, c, :], a_lo[:, c, :], base_hi[:, c, :], base_lo[:, c, :], c == 0, False)

            def a_mix_t(b):
                pe.wait_ge(z_mixed, 3 * b + 3)
                pe.transpose(ps_k[0:ACTIVE * RANK + 1, P:2 * P], z_mix[:, b % 2, :], ident[:]).then_inc(zt_mm, 1)

            def a_end(b):
                pe.wait_ge(zt_out, b + 1)
                pe.matmul(ps_q[:], z_mix_t[:], low_rank_out[:], start=False, stop=True).then_inc(y_mm, 1)

            def b_scores(b):
                pe.wait_ge(b_full_s, b + 1)
                wait_from(pe, bt_out, b)
                if b == 0:
                    pe.wait_ge(r_out, 2)
                cols = slice(b * P, (b + 1) * P)
                for c in range(NC):
                    pe.matmul(ps_v[:, 0:P], b_full[:, c, :], gg[:, c, cols], start=(c == 0), stop=False)
                pe.matmul(ps_v[:, 0:P], ones[0:1, :], r_row[0:1, cols], start=False, stop=True).then_inc(bs_mm, 1)

            def b_transpose(b):
                pe.wait_ge(b_exp, b + 1)
                pe.transpose(ps_v[:, 2 * P:3 * P], b_probs[:], ident[:]).then_inc(bt_mm, 1)

            def b_attend(b):
                pe.wait_ge(bt_out, b + 1)
                if b == 0:
                    pe.wait_ge(ctx_in, 16)
                    pe.wait_ge(o_added, 2 * STEPS)
                wait_from(pe, b_add, b)
                pe.matmul(ps_o[0][:], b_probs_t[:], ctx_sb[:, b, :], start=True, stop=True).then_inc(at_mm, 1)

            def c_product(b):
                pe.wait_ge(c_lo_s, b + 1)
                if b == 0:
                    pe.wait_ge(codes_s, 4)
                    pe.wait_ge(o_added, 2 * STEPS)
                wait_from(pe, c_zero, b)
                for c in range(NC):
                    pe.matmul(ps_o[1][:], c_hi[:, c, :], codes[:, c, :], start=(c == 0), stop=False)
                    last = pe.matmul(ps_o[1][:], c_lo[:, c, :], codes[:, c, :], start=False, stop=(c == NC - 1))
                last.then_inc(c_mm, 1)

            for w in range(BATCH + 2):
                a, b, c = w, w - 1, w - 2
                has_a, has_b, has_c = a < BATCH, 0 <= b < BATCH, 0 <= c < BATCH
                if has_a:
                    transpose(0, a, a_lo_s)
                if has_b:
                    transpose(1, b, b_full_s)
                if has_c:
                    transpose(2, c, c_lo_s)
                if has_a:
                    a_low_rank(a)
                if has_b:
                    b_scores(b)
                if has_a:
                    a_base(a)
                if has_c:
                    c_product(c)
                if has_a:
                    a_mix_t(a)
                if has_b:
                    b_transpose(b)
                    b_attend(b)
                if has_a:
                    a_end(a)


def kernel(**inputs):
    import numpy as np
    import concourse.bacc as bacc
    from concourse.bass_utils import run_bass_kernel_spmd

    def get(name):
        return np.asarray(inputs[name])

    def keep(a):
        return np.ascontiguousarray(a)

    g = GROUPS
    arrays = {
        "x": keep(get("x").reshape(TOK, D)),
        "ctx_nat": keep(get("ctx_4096").reshape(TOK, D)),
        "ctx_t": keep(get("ctx_4096").reshape(TOK, NC, P).transpose(2, 1, 0)),
        "mask": keep(get("mask_BxSxS2_bk0").transpose(1, 0, 2)),
        "bias": keep(get("L0_xattn_position_bias").reshape(g, 2, P, P).transpose(0, 2, 1, 3)),
        "ln_w": keep(get("L0_xattn_ln_weight").reshape(1, D)),
        "w_q": keep(get("L0_xattn_w_q").reshape(g, 2, P, NC, P).transpose(0, 4, 1, 3, 2).reshape(g, P, 2 * D)),
        "w_k": keep(get("L0_xattn_w_k").reshape(g, 2, P, NC, P).transpose(0, 4, 1, 3, 2).reshape(g, P, 2 * D)),
        "w_v": keep(get("L0_xattn_w_v").reshape(g, 2 * P, NC, P).transpose(0, 3, 2, 1).reshape(g, P, 2 * D)),
        "w_o": keep(get("L0_xattn_w_out").reshape(D, g, 2, P).transpose(1, 3, 2, 0).reshape(g, P, 2 * D)),
        "w_base": keep(get("L0_ffn_W_base").reshape(D, NC, P).transpose(2, 1, 0)),
        "b_base": keep(get("L0_ffn_b_base").reshape(1, D)),
        "lora_a": keep(get("L0_ffn_lora_A").reshape(EXPERTS * RANK, D)),
        "lora_b": keep(get("L0_ffn_lora_B").transpose(0, 2, 1).reshape(EXPERTS * RANK, D)),
        "router_w": keep(get("L0_ffn_router_W")),
        "router_b": keep(get("L0_ffn_router_b").reshape(EXPERTS, 1)),
        "prior": keep(get("L0_ffn_domain_prior").reshape(EXPERTS, 1)),
        "active": keep(get("L0_ffn_active").reshape(1, ACTIVE)),
        "wq1": keep(get("L1_xattn_Wq").reshape(NC, P, D).transpose(1, 0, 2)),
        "bq1": keep(get("L1_xattn_bq").reshape(NC, P).T),
        "wk1": keep(get("L1_xattn_Wk").reshape(NC, P, D).transpose(1, 0, 2)),
        "bk1": keep(get("L1_xattn_bk").reshape(NC, P).T),
        "qweight": keep(get("L1_ffn_qweight").reshape(D, P, 3).transpose(1, 2, 0)),
        "w_scale": keep(get("L1_ffn_weight_scale").reshape(1, D)),
        "w_zero": keep(get("L1_ffn_weight_zero_point").reshape(1, D)),
        "ffn_bias": keep(get("L1_ffn_bias").reshape(1, D)),
    }
    nc = bacc.Bacc("TRN2", target_bir_lowering=False, num_devices=1)
    args = [nc.dram_tensor(f"in_{name}", a.shape, mybir.dt.from_np(a.dtype), kind="ExternalInput").ap()
            for name, a in arrays.items()]
    args.append(nc.dram_tensor("out_x", (TOK, D), F32, kind="ExternalOutput").ap())
    build(nc, *args)
    done = run_bass_kernel_spmd(nc, [{f"in_{name}": a for name, a in arrays.items()}], core_ids=[0])
    return done.results[0]["out_x"].reshape(BATCH, P, D)
```

```python
from contextlib import ExitStack

import concourse.bass as bass
from concourse import mybir

F32 = mybir.dt.float32
F32R = mybir.dt.float32r
I32 = mybir.dt.int32
U8 = mybir.dt.uint8
ALU = mybir.AluOpType
ACT = mybir.ActivationFunctionType
AX_X = mybir.AxisListType.X

P = 128
BATCH, D, HEADS = 8, 512, 32
NC = D // P
TOK = BATCH * P
HALF = TOK // 2
GROUPS = HEADS // 2
STEPS = 4 * GROUPS
LOOP_STEPS = 8
TURNS = STEPS // LOOP_STEPS
EXPERTS, ACTIVE, RANK = 16, 4, 8
ZL = ACTIVE * RANK + ACTIVE
LORA_SCALE = 16.0 / 8.0
EPS = 1e-5
PRIOR_EPS = 1e-12
MASKED = 3e38
SCORE_SCALE = float(D) ** -0.5


def wait_from(eng, sem, value):
    if not isinstance(value, int) or value > 0:
        eng.wait_ge(sem, value)


def build(nc, x, ctx_nat, ctx_t, mask, bias, ln_w, w_q, w_k, w_v, w_o, w_base, b_base, lora_a, lora_b,
          router_w, router_b, prior, active, wq1, bq1, wk1, bk1, qweight, w_scale, w_zero, ffn_bias, out):
    with ExitStack() as stack:
        top = [(nc.sbuf_base + 63) // 64 * 64]
        sizes = {F32: 4, F32R: 4, I32: 4, U8: 1}

        def place(name, shape, dt, at=None):
            size = sizes[dt]
            for n in shape[1:]:
                size *= n
            if at is None:
                at = top[0]
                top[0] += (size + 31) // 32 * 32
                assert top[0] <= nc.sbuf_usable_end, (name, top)
            return nc.alloc_sbuf_tensor_at(name, shape, dt, offset=at), at

        xt_hi, at_xt_hi = place("xt_hi", [P, NC, TOK], F32R)
        xt_lo, at_xt_lo = place("xt_lo", [P, NC, TOK], F32R)
        ct_hi, at_ct_hi = place("ct_hi", [P, NC, TOK], F32R)
        ct_lo, at_ct_lo = place("ct_lo", [P, NC, TOK], F32R)
        acc, _ = place("acc", [P, BATCH, D], F32)
        wq_hi, at_wq = place("wq_hi", [P, 2, NC, P], F32R)
        wq_lo, _ = place("wq_lo", [P, 2, NC, P], F32R)
        wk_hi, _ = place("wk_hi", [P, 2, NC, P], F32R)
        wk_lo, _ = place("wk_lo", [P, 2, NC, P], F32R)
        wv_hi, wv_lo, wo_hi, wo_lo, at_wv, at_wo = [0, 0], [0, 0], [0, 0], [0, 0], [0, 0], [0, 0]
        for n in range(2):
            wv_hi[n], at_wv[n] = place(f"wv_hi{n}", [P, NC, 2 * P], F32R)
            wv_lo[n], _ = place(f"wv_lo{n}", [P, NC, 2 * P], F32R)
            wo_hi[n], at_wo[n] = place(f"wo_hi{n}", [P, 2, D], F32R)
            wo_lo[n], _ = place(f"wo_lo{n}", [P, 2, D], F32R)
        raw_q, at_raw = place("raw_q", [P, 2, NC, P], F32)
        raw_k, _ = place("raw_k", [P, 2, NC, P], F32)
        raw_v, _ = place("raw_v", [P, NC, 2 * P], F32)
        raw_o, _ = place("raw_o", [P, 2, D], F32)
        qt, kt, vv, at_qkv = [0, 0], [0, 0], [0, 0], [0, 0]
        for n in range(2):
            qt[n], at_qkv[n] = place(f"qt{n}", [P, 2, HALF], F32)
            kt[n], _ = place(f"kt{n}", [P, 2, HALF], F32)
            vv[n], _ = place(f"vv{n}", [P, 4, 2 * P], F32)
        scores, probs, shift, at_scores, at_probs = [0, 0], [0, 0], [0, 0], [0, 0], [0, 0]
        for n in range(2):
            scores[n], at_scores[n] = place(f"scores{n}", [P, 4, P], F32)
            probs[n], at_probs[n] = place(f"probs{n}", [P, 4, P], F32)
            shift[n], _ = place(f"shift{n}", [P, 4, P], F32)
        probs_t, _ = place("probs_t", [P, 4, P], F32)
        att_hi, at_att_hi = place("att_hi", [P, 4, P], F32R)
        att_lo, _ = place("att_lo", [P, 4, P], F32R)
        bias_sb, _ = place("bias_sb", [P, 2, 2, P], F32)
        mask_sb, _ = place("mask_sb", [P, BATCH, P], F32)
        ident, _ = place("ident", [P, P], F32)
        ones, _ = place("ones", [P, P], F32)
        low_rank_in, _ = place("low_rank_in", [P, NC, ZL], F32)
        low_rank_out, _ = place("low_rank_out", [ACTIVE * RANK + 1, D], F32)
        normed, _ = place("normed", [P, 3, D], F32)
        row_max, _ = place("row_max", [P, 2, 4], F32)
        neg_max, _ = place("neg_max", [P, 2, 4], F32)
        row_sum, _ = place("row_sum", [P, 2, 4], F32)
        row_inv, _ = place("row_inv", [P, 2, 4], F32)
        row_fac, _ = place("row_fac", [P, 2, 4], F32)
        stats, _ = place("stats", [P, BATCH, 6], F32)
        mean_var, _ = place("mean_var", [P, BATCH, 2], F32)
        var_eps, _ = place("var_eps", [P, BATCH], F32)
        rstd, _ = place("rstd", [P, BATCH], F32)
        ms_a, _ = place("ms_a", [P, BATCH], F32)
        ms_b, _ = place("ms_b", [P, BATCH], F32)
        ms_eps, _ = place("ms_eps", [P, BATCH], F32)
        rms, _ = place("rms", [P, BATCH], F32)
        minus_half, _ = place("minus_half", [P, BATCH], F32)
        t_stats, _ = place("t_stats", [P, 3, BATCH, 6], F32)
        t_mv, _ = place("t_mv", [P, 3, BATCH, 2], F32)
        t_ve, _ = place("t_ve", [P, 3, BATCH], F32)
        t_rstd, _ = place("t_rstd", [P, 3, BATCH], F32)
        uw, _ = place("uw", [P, 9], F32)
        bqk, _ = place("bqk", [P, 2, NC], F32)
        bqk_mul, _ = place("bqk_mul", [P, NC], F32)
        bqk_sum, _ = place("bqk_sum", [P, 1], F32)
        act_i, _ = place("act_i", [1, ACTIVE], I32)
        act_f, _ = place("act_f", [1, 3, ACTIVE], F32)
        targets, _ = place("targets", [1, ZL], F32)
        iota_r, _ = place("iota_r", [1, RANK], I32)
        iota_p, _ = place("iota_p", [P, 1], I32)
        iota_rf, _ = place("iota_rf", [1, RANK], F32)
        iota_pf, _ = place("iota_pf", [P, 1], F32)
        select, _ = place("select", [P, ZL], F32)
        rb_sb, _ = place("rb_sb", [EXPERTS, 2], F32)
        logit_bias, _ = place("logit_bias", [P, 3, ACTIVE], F32)
        logits, _ = place("logits", [P, BATCH, ACTIVE], F32)
        l_max, _ = place("l_max", [P, BATCH, 2], F32)
        l_exp, _ = place("l_exp", [P, BATCH, ACTIVE], F32)
        l_sum, _ = place("l_sum", [P, BATCH, 2], F32)
        alpha, _ = place("alpha", [P, BATCH, ACTIVE], F32)
        z_mix, _ = place("z_mix", [P, 2, ACTIVE * RANK + 1], F32)
        b_max, _ = place("b_max", [P, BATCH, 2], F32)
        b_sum, _ = place("b_sum", [P, BATCH, 2], F32)
        x_sum, _ = place("x_sum", [P, BATCH, 2], F32)
        prior_eps, _ = place("prior_eps", [P, 1], F32)

        raw_ct = [place(f"raw_ct{n}", [P, NC, HALF], F32, at=at_wo[n])[0] for n in range(2)]
        mask_raw, _ = place("mask_raw", [P, BATCH, P], U8, at=at_scores[0])
        ln_w_rows, _ = place("ln_w_rows", [P, D], F32, at=at_att_hi)
        rms_in = [place(f"rms_in{n}", [P, D], F32, at=at_probs[n])[0] for n in range(2)]

        wk1_raw, _ = place("wk1_raw", [P, NC, D], F32, at=at_raw)
        wq1_raw, _ = place("wq1_raw", [P, NC, D], F32, at=at_raw + 8192)
        wk1_hi, _ = place("wk1_hi", [P, NC, D], F32R, at=at_wv[0])
        wk1_lo, _ = place("wk1_lo", [P, NC, D], F32R, at=at_wo[0])
        wq1_hi, _ = place("wq1_hi", [P, NC, D], F32R, at=at_wq)
        wq1_lo, _ = place("wq1_lo", [P, NC, D], F32R, at=at_wq + 8192)
        mm_hi, _ = place("mm_hi", [P, NC, D], F32R, at=at_raw)
        mm_lo, _ = place("mm_lo", [P, NC, D], F32R, at=at_raw + 8192)
        gg, _ = place("gg", [P, NC, TOK], F32, at=at_xt_hi)
        base_hi, _ = place("base_hi", [P, NC, D], F32R, at=at_xt_lo)
        base_lo, _ = place("base_lo", [P, NC, D], F32R, at=at_xt_lo + 8192)
        base_raw, _ = place("base_raw", [P, NC, D], F32, at=at_qkv[0])
        r_row, _ = place("r_row", [P, TOK], F32, at=at_qkv[0] + 8192)
        lora_a_sb, _ = place("lora_a_sb", [P, D], F32, at=at_wv[1])
        lora_b_sb, _ = place("lora_b_sb", [P, D], F32, at=at_wv[1] + 2048)
        router_sb, _ = place("router_sb", [EXPERTS, D], F32, at=at_wv[1] + 4096)
        rb_cols, _ = place("rb_cols", [EXPERTS, 2, P], F32, at=at_wv[1] + 6144)
        ww_hi, _ = place("ww_hi", [P, NC, P], F32R, at=at_wo[1])
        ww_lo, _ = place("ww_lo", [P, NC, P], F32R, at=at_wo[1] + 2048)
        ww_f, _ = place("ww_f", [P, NC, P], F32, at=at_wo[1] + 4096)
        ctx_sb, _ = place("ctx_sb", [P, BATCH, D], F32, at=at_wv[0])
        codes, _ = place("codes", [P, NC, D], F32R, at=at_wq)
        packed, _ = place("packed", [P, 3, D], I32, at=at_wq + 8192)
        unpack, _ = place("unpack", [P, D], I32, at=at_wq + 8192 + 6144)
        zero_rows, _ = place("zero_rows", [P, D], F32, at=at_ct_lo)
        scale_rows, _ = place("scale_rows", [P, D], F32, at=at_ct_lo + 2048)
        bias_rows, _ = place("bias_rows", [P, D], F32, at=at_ct_lo + 4096)
        f_scr = [place(f"f_scr{n}", [P, D], F32, at=at_ct_lo + 6144 + 2048 * n)[0] for n in range(4)]
        a_hi, _ = place("a_hi", [P, NC, P], F32R, at=at_qkv[1])
        a_lo, _ = place("a_lo", [P, NC, P], F32R, at=at_qkv[1] + 2048)
        a_full, _ = place("a_full", [P, NC, P], F32, at=at_qkv[1] + 4096)
        b_full, _ = place("b_full", [P, NC, P], F32, at=at_qkv[1] + 6144)
        c_hi, _ = place("c_hi", [P, NC, P], F32R, at=at_qkv[1] + 8192)
        c_lo, _ = place("c_lo", [P, NC, P], F32R, at=at_qkv[1] + 10240)
        b_probs, _ = place("b_probs", [P, P], F32, at=at_scores[0])
        b_probs_t, _ = place("b_probs_t", [P, P], F32, at=at_scores[0] + 512)
        z_mix_t, _ = place("z_mix_t", [ACTIVE * RANK + 1, P], F32, at=at_scores[0] + 1024)
        junk, _ = place("junk", [P, D], F32, at=at_scores[1])

        def bank(name):
            return stack.enter_context(nc.psum_tensor(name, [P, D], F32))

        ps_s, ps_t, ps_pv, ps_q, ps_k, ps_v = (bank(f"ps_{n}") for n in "s t pv q k v".split())
        ps_o = [bank("ps_o0"), bank("ps_o1")]

        def blocks(t):
            return t[:].rearrange("p (n c) -> p n c", c=P)

        g_banks = (ps_q, ps_k, ps_v, ps_t, ps_pv, ps_o[1], ps_pv, ps_o[1])
        r_banks = (ps_v, ps_pv)

        S = {}

        def sem(name):
            S[name] = stack.enter_context(nc.semaphore(name))
            return S[name]

        ct_in = [sem(f"ct_in{n}") for n in range(NC + 1)]
        x_in = [sem(f"x_in{n}") for n in range(2)]
        wq_in, wk_in, wv_in, wo_in = sem("wq_in"), sem("wk_in"), sem("wv_in"), sem("wo_in")
        bias_in = [sem("bias_in0"), sem("bias_in1")]
        mask_in, ln_in = sem("mask_in"), sem("ln_in")
        const_done, ident_zero, ident_done, mask_done = sem("const_done"), sem("ident_zero"), sem("ident_done"), sem("mask_done")
        ct_hi_done, ct_lo_done = sem("ct_hi_done"), sem("ct_lo_done")
        x_stats, x_mean = sem("x_stats"), sem("x_mean")
        x_chain, x_ve, x_rstd, x_ms, x_rms = sem("x_chain"), sem("x_ve"), sem("x_rstd"), sem("x_ms"), sem("x_rms")
        x_normed, x_resid, x_h, x_t, x_hi, x_lo = (sem(n) for n in ("x_normed", "x_resid", "x_h", "x_t", "x_hi", "x_lo"))
        wq_hi_s, wq_lo_s, wk_hi_s, wk_lo_s = (sem(n) for n in ("wq_hi_s", "wq_lo_s", "wk_hi_s", "wk_lo_s"))
        wv_hi_s, wv_lo_s, wo_hi_s, wo_lo_s = (sem(n) for n in ("wv_hi_s", "wv_lo_s", "wo_hi_s", "wo_lo_s"))
        q_done, k_done, v_done, q_out, k_out, v_out = (sem(n) for n in ("q_done", "k_done", "v_done", "q_out", "k_out", "v_out"))
        s_done, s_shifted, s_max, s_neg, e_done, s_inv, s_fac, p_done = (
            sem(n) for n in ("s_done", "s_shifted", "s_max", "s_neg", "e_done", "s_inv", "s_fac", "p_done"))
        shift_done, pt_done, pt_out, pv_done, att_hi_s, att_lo_s, o_done, o_added = (
            sem(n) for n in ("shift_done", "pt_done", "pt_out", "pv_done", "att_hi_s", "att_lo_s", "o_done", "o_added"))
        w1_in = [sem("wk1_in"), sem("wq1_in")]
        w1_hi_s, w1_lo_s = sem("w1_hi_s"), sem("w1_lo_s")
        vec_in, vec_mul, vec_sum, vec_acc, vec_mm, vec_out = (
            sem(n) for n in ("vec_in", "vec_mul", "vec_sum", "vec_acc", "vec_mm", "vec_out"))
        mm_done, mm_hi_s, mm_out = sem("mm_done"), sem("mm_hi_s"), sem("mm_out")
        g_done, g_out = sem("g_done"), sem("g_out")
        ww_s, ww_hi_s, ww_lo_s, r_done, r_out = (sem(n) for n in ("ww_s", "ww_hi_s", "ww_lo_s", "r_done", "r_out"))
        base_in, base_hi_s, base_lo_s = sem("base_in"), sem("base_hi_s"), sem("base_lo_s")
        act_in, lora_in, act_chain, iota_s, tgt_mm, sel_s, rbc_s = (
            sem(n) for n in ("act_in", "lora_in", "act_chain", "iota_s", "tgt_mm", "sel_s", "rbc_s"))
        lr_mm, lr_out, lb_mm, lb_out, lbias = (sem(n) for n in ("lr_mm", "lr_out", "lb_mm", "lb_out", "lbias"))
        ctx_in, packed_in, rows_in, unp, codes_s = (sem(n) for n in ("ctx_in", "packed_in", "rows_in", "unp", "codes_s"))
        n_st = [sem(f"n_st{k}") for k in range(3)]
        n_mv = [sem(f"n_mv{k}") for k in range(3)]
        n_ve = [sem(f"n_ve{k}") for k in range(3)]
        n_rs = [sem(f"n_rs{k}") for k in range(3)]
        n_xn = [sem(f"n_xn{k}") for k in range(3)]
        n_t = [sem(f"n_t{k}") for k in range(3)]
        a_full_s, a_hi_s, a_lo_s, z_mm, y_mm, zt_mm, zt_out, a_add = (
            sem(n) for n in ("a_full_s", "a_hi_s", "a_lo_s", "z_mm", "y_mm", "zt_mm", "zt_out", "a_add"))
        lg_c, lg_exp, z_mixed = sem("lg_c"), sem("lg_exp"), sem("z_mixed")
        b_full_s, bs_mm, b_c, b_exp, bt_mm, bt_out, at_mm, b_inv, b_add = (
            sem(n) for n in ("b_full_s", "bs_mm", "b_c", "b_exp", "bt_mm", "bt_out", "at_mm", "b_inv", "b_add"))
        c_hi_s, c_lo_s, c_sum, c_neg, c_mm, c_zero, c_scaled, c_bias, c_add = (
            sem(n) for n in ("c_hi_s", "c_lo_s", "c_sum", "c_neg", "c_mm", "c_zero", "c_scaled", "c_bias", "c_add"))
        stored = sem("stored")

        block = stack.enter_context(nc.Block())

        def three(pe, dst, hi_l, lo_l, hi_r, lo_r, first, last):
            pe.matmul(dst, hi_l, hi_r, start=first, stop=False)
            pe.matmul(dst, hi_l, lo_r, start=False, stop=False)
            return pe.matmul(dst, lo_l, hi_r, start=False, stop=last)

        @block.sync
        def _(sp):
            def halves(t):
                return t.rearrange("(b p) d -> p b d", p=P)

            sp.dma_start(raw_k[:].rearrange("p h c d -> p (h c d)"), w_k[0]).then_inc(wk_in, 16)
            for c in range(NC):
                sp.dma_start(raw_ct[0][:, c, :], ctx_t[:, c, 0:HALF]).then_inc(ct_in[c], 16)
            sp.dma_start(raw_v[:].rearrange("p c d -> p (c d)"), w_v[0]).then_inc(wv_in, 16)
            sp.dma_start(acc[:, 0:4, :], halves(x)[:, 0:4, :]).then_inc(x_in[0], 16)
            sp.dma_start(raw_ct[1][:], ctx_t[:, :, HALF:TOK]).then_inc(ct_in[NC], 16)
            sp.dma_start(ln_w_rows[:], ln_w.broadcast_to([P, D])).then_inc(ln_in, 16)
            sp.dma_start(acc[:, 4:8, :], halves(x)[:, 4:8, :]).then_inc(x_in[1], 16)
            sp.dma_start(raw_q[:].rearrange("p h c d -> p (h c d)"), w_q[0]).then_inc(wq_in, 16)
            sp.dma_start(mask_raw[:], mask).then_inc(mask_in, 16)
            sp.dma_start(bias_sb[:, 0], bias[0]).then_inc(bias_in[0], 16)
            sp.dma_start(raw_o[:].rearrange("p h d -> p (h d)"), w_o[0]).then_inc(wo_in, 16)
            sp.dma_start(act_i[:], active).then_inc(act_in, 16)
            sp.dma_start(rb_sb[:, 0:1], router_b).then_inc(act_in, 16)
            sp.dma_start(rb_sb[:, 1:2], prior).then_inc(act_in, 16)
            sp.dma_start(low_rank_out[ACTIVE * RANK:ACTIVE * RANK + 1, :], b_base).then_inc(act_in, 16)
            sp.dma_start(bqk[:, 0, :], bq1).then_inc(vec_in, 16)
            sp.dma_start(bqk[:, 1, :], bk1).then_inc(vec_in, 16)
            sp.wait_ge(wv_lo_s, 1)
            sp.dma_start(raw_v[:].rearrange("p c d -> p (c d)"), w_v[1]).then_inc(wv_in, 16)

            def load_group(g, more, parity):
                sp.wait_ge(wq_lo_s, 2 * g)
                sp.dma_start(raw_q[:].rearrange("p h c d -> p (h c d)"), w_q[g]).then_inc(wq_in, 16)
                sp.wait_ge(wk_lo_s, 2 * g)
                sp.dma_start(raw_k[:].rearrange("p h c d -> p (h c d)"), w_k[g]).then_inc(wk_in, 16)
                wait_from(sp, shift_done, 4 * g - 4)
                sp.dma_start(bias_sb[:, parity], bias[g]).then_inc(bias_in[parity], 16)
                sp.wait_ge(wo_lo_s, g)
                sp.dma_start(raw_o[:].rearrange("p h d -> p (h d)"), w_o[g]).then_inc(wo_in, 16)
                if more:
                    sp.wait_ge(wv_lo_s, g + 1)
                    sp.dma_start(raw_v[:].rearrange("p c d -> p (c d)"), w_v[g + 1]).then_inc(wv_in, 16)

            load_group(1, True, 1)
            with sp.Fori(1, TURNS - 1) as i:
                load_group(2 * i, True, 0)
                load_group(2 * i + 1, True, 1)
            load_group(GROUPS - 2, True, 0)
            load_group(GROUPS - 1, False, 1)

            sp.wait_ge(wq_lo_s, 2 * GROUPS)
            sp.wait_ge(wk_lo_s, 2 * GROUPS)
            sp.dma_start(wk1_raw[:], wk1).then_inc(w1_in[0], 16)
            sp.wait_ge(wv_lo_s, GROUPS)
            sp.wait_ge(wo_lo_s, GROUPS)
            sp.dma_start(wq1_raw[:], wq1).then_inc(w1_in[1], 16)
            sp.wait_ge(v_done, STEPS)
            sp.dma_start(lora_a_sb[:], lora_a).then_inc(lora_in, 16)
            sp.dma_start(lora_b_sb[:], lora_b).then_inc(lora_in, 16)
            sp.dma_start(router_sb[:], router_w).then_inc(lora_in, 16)
            sp.wait_ge(pv_done, STEPS - 2)
            sp.dma_start(base_raw[:], w_base).then_inc(base_in, 16)
            sp.wait_ge(mm_done, NC)
            sp.dma_start(packed[:], qweight).then_inc(packed_in, 16)
            sp.dma_start(ctx_sb[:], ctx_nat.rearrange("(b p) d -> p b d", p=P)).then_inc(ctx_in, 16)
            sp.wait_ge(g_done, 2 * NC)
            sp.wait_ge(r_done, 2)
            sp.dma_start(zero_rows[:], w_zero.broadcast_to([P, D])).then_inc(rows_in, 16)
            sp.dma_start(scale_rows[:], w_scale.broadcast_to([P, D])).then_inc(rows_in, 16)
            sp.dma_start(bias_rows[:], ffn_bias.broadcast_to([P, D])).then_inc(rows_in, 16)
            for b in range(BATCH):
                sp.wait_ge(c_add, b + 1)
                sp.dma_start(out[b * P:(b + 1) * P, :], acc[:, b, :]).then_inc(stored, 16)
            sp.wait_ge(stored, 16 * BATCH)

        @block.scalar
        def _(act):
            def split_ct(half, c):
                act.wait_ge(ct_in[NC if half else c], 16)
                act.copy(ct_hi[:, c, half * HALF:(half + 1) * HALF], raw_ct[half][:, c, :]).then_inc(ct_hi_done, 1)

            def split_qk(g, head):
                wait_from(act, wq_in, 16 * (g + 1))
                wait_from(act, q_done, 4 * g - 1 + head)
                act.copy(wq_hi[:, head], raw_q[:, head]).then_inc(wq_hi_s, 1)
                wait_from(act, wk_in, 16 * (g + 1))
                wait_from(act, k_done, 4 * g - 1 + head)
                act.copy(wk_hi[:, head], raw_k[:, head]).then_inc(wk_hi_s, 1)

            def split_v(g, n):
                wait_from(act, wv_in, 16 * (g + 1))
                wait_from(act, v_done, 4 * g - 4)
                act.copy(wv_hi[n][:], raw_v[:]).then_inc(wv_hi_s, 1)

            def split_o(g, n):
                wait_from(act, wo_in, 16 * (g + 1))
                wait_from(act, o_done, 8 * g - 8)
                act.copy(wo_hi[n][:], raw_o[:]).then_inc(wo_hi_s, 1)

            def k_evac(t, n, part):
                wait_from(act, k_done, t + 1)
                act.copy(kt[n][:, part, :], ps_k[:]).then_inc(k_out, 1)

            def q_evac(t, n, part):
                wait_from(act, q_done, t + 1)
                act.copy(qt[n][:, part, :], ps_q[:]).then_inc(q_out, 1)

            def x_high(b):
                act.wait_ge(x_t, b + 1)
                act.copy(xt_hi[:, :, b * P:(b + 1) * P], blocks(ps_o[b % 2])).then_inc(x_hi, 1)

            act.wait_ge(wk_in, 16)
            act.copy(wk_hi[:, 0], raw_k[:, 0]).then_inc(wk_hi_s, 1)
            for c in range(NC):
                split_ct(0, c)
            act.copy(wk_hi[:, 1], raw_k[:, 1]).then_inc(wk_hi_s, 1)
            split_v(0, 0)
            k_evac(0, 0, 0)
            k_evac(1, 0, 1)
            for c in range(NC):
                split_ct(1, c)
            k_evac(2, 1, 0)
            x_high(0)
            x_high(1)
            act.wait_ge(wq_in, 16)
            act.copy(wq_hi[:, 0], raw_q[:, 0]).then_inc(wq_hi_s, 1)
            act.copy(wq_hi[:, 1], raw_q[:, 1]).then_inc(wq_hi_s, 1)
            k_evac(3, 1, 1)
            for b in range(2, 6):
                x_high(b)
            q_evac(0, 0, 0)
            x_high(6)
            q_evac(1, 0, 1)
            x_high(7)
            act.wait_ge(ct_lo_done, NC)
            split_o(0, 0)
            split_v(1, 1)

            def attention_high(s):
                wait_from(act, pv_done, s + 1)
                act.copy(att_hi[:], blocks(ps_pv)).then_inc(att_hi_s, 1)

            def exponentials(s, n):
                act.wait_ge(s_neg, s + 1)
                wait_from(act, pt_done, s - 1)
                for m in range(4):
                    e = act.activation(probs[n][:, m, :], scores[n][:, m, :], ACT.Exp,
                                       bias=neg_max[:, n, m:m + 1], accum_out=row_sum[:, n, m:m + 1])
                e.then_inc(e_done, 1)

            def pt_evac(s):
                act.wait_ge(pt_done, s + 1)
                act.copy(probs_t[:], blocks(ps_t)).then_inc(pt_out, 1)

            def step(i, c):
                s = LOOP_STEPS * i + c
                g = 2 * i + c // 4
                n = c % 2
                if c > 0 or not isinstance(i, int) or i > 0:
                    attention_high(s - 1)
                exponentials(s, n)
                q_evac(s + 2, (c // 2 + 1) % 2, n)
                if not isinstance(i, int) or s > 1:
                    k_evac(s + 2, (c // 2 + 1) % 2, n)
                pt_evac(s)
                last = isinstance(i, int) and i == TURNS - 1
                if c % 4 < 2 and not (last and c >= 4):
                    split_qk(g + 1, c % 4)
                if c % 4 == 2 and not (last and c >= 4):
                    split_o(g + 1, (c // 4 + 1) % 2)
                if c % 4 == 3 and not last:
                    split_v(g + 2, (c // 4) % 2)

            for c in range(LOOP_STEPS):
                step(0, c)
            with act.Fori(1, TURNS - 1) as i:
                for c in range(LOOP_STEPS):
                    step(i, c)
            for c in range(LOOP_STEPS - 4):
                step(TURNS - 1, c)
            step(TURNS - 1, 4)
            act.wait_ge(w1_in[0], 16)
            act.wait_ge(v_done, 4 * (GROUPS - 1))
            for c in range(NC):
                act.copy(wk1_hi[:, c, :], wk1_raw[:, c, :]).then_inc(w1_hi_s, 1)
            attention_high(STEPS - 4)
            exponentials(STEPS - 3, 1)
            q_evac(STEPS - 1, 1, 1)
            act.wait_ge(w1_in[1], 16)
            for c in range(NC):
                act.copy(wq1_hi[:, c, :], wq1_raw[:, c, :]).then_inc(w1_hi_s, 1)
            k_evac(STEPS - 1, 1, 1)
            pt_evac(STEPS - 3)
            attention_high(STEPS - 3)

            def mm_high(m):
                act.wait_ge(mm_done, m + 1)
                if m == 0:
                    act.wait_ge(w1_lo_s, 2 * NC)
                    act.wait_ge(vec_mm, 1)
                act.copy(mm_hi[:, m, :], (ps_q, ps_k)[m % 2][:]).then_inc(mm_hi_s, 1)

            exponentials(STEPS - 2, 0)
            mm_high(0)
            pt_evac(STEPS - 2)
            mm_high(1)
            mm_high(2)
            attention_high(STEPS - 2)
            act.wait_ge(lr_mm, 1)
            act.activation(logit_bias[:, 0, :], ps_v[:, 148:152], ACT.Ln, bias=prior_eps[:, 0:1]).then_inc(lbias, 1)
            mm_high(3)
            exponentials(STEPS - 1, 1)
            act.wait_ge(base_in, 16)
            for c in range(NC):
                act.copy(base_hi[:, c, :], base_raw[:, c, :]).then_inc(base_hi_s, 1)
            pt_evac(STEPS - 1)
            attention_high(STEPS - 1)
            act.wait_ge(ww_s, NC)
            act.wait_ge(o_done, 2 * STEPS)
            act.copy(ww_hi[:], ww_f[:]).then_inc(ww_hi_s, 1)

            def code(v):
                act.wait_ge(unp, v + 1)
                act.copy(codes[:, v, :], unpack[:]).then_inc(codes_s, 1)

            def stage_a(b):
                act.wait_ge(n_t[0], b + 1)
                wait_from(act, z_mm, b)
                act.copy(a_full[:], blocks(ps_s)).then_inc(a_full_s, 1)
                wait_from(act, y_mm, b)
                act.copy(a_hi[:], blocks(ps_s)).then_inc(a_hi_s, 1)

            def stage_a_exp(b):
                act.wait_ge(lg_c, 3 * b + 3)
                act.activation(l_exp[:, b, :], logits[:, b, :], ACT.Exp, bias=l_max[:, b, 1:2],
                               accum_out=l_sum[:, b, 0:1]).then_inc(lg_exp, 1)

            def stage_a_zt(b):
                act.wait_ge(zt_mm, b + 1)
                wait_from(act, y_mm, b)
                act.copy(z_mix_t[:], ps_k[0:ACTIVE * RANK + 1, P:2 * P]).then_inc(zt_out, 1)

            def stage_b(b):
                act.wait_ge(n_t[1], b + 1)
                wait_from(act, bs_mm, b)
                act.copy(b_full[:], blocks(ps_t)).then_inc(b_full_s, 1)

            def stage_b_exp(b):
                act.wait_ge(b_c, 2 * b + 2)
                wait_from(act, bt_mm, b)
                act.activation(b_probs[:], ps_v[:, 0:P], ACT.Exp, bias=b_max[:, b, 1:2], scale=SCORE_SCALE,
                               accum_out=b_sum[:, b, 0:1]).then_inc(b_exp, 1)

            def stage_b_pt(b):
                act.wait_ge(bt_mm, b + 1)
                wait_from(act, at_mm, b)
                act.copy(b_probs_t[:], ps_v[:, 2 * P:3 * P]).then_inc(bt_out, 1)

            def stage_c_sum(b):
                act.wait_ge(n_xn[2], b + 1)
                wait_from(act, c_sum, b)
                act.activation(junk[:], normed[:, 2, :], ACT.Copy, accum_out=x_sum[:, b, 0:1]).then_inc(c_sum, 1)

            def stage_c(b):
                act.wait_ge(n_t[2], b + 1)
                wait_from(act, c_mm, b)
                act.copy(c_hi[:], blocks(ps_pv)).then_inc(c_hi_s, 1)

            for w in range(BATCH + 5):
                a, b, b_end, c = w, w - 1, w - 2, w - 3
                if 0 <= b_end < BATCH:
                    stage_b_pt(b_end)
                if a < BATCH:
                    stage_a(a)
                    stage_a_exp(a)
                if w < 2:
                    code(2 * w)
                if 0 <= c < BATCH:
                    stage_c_sum(c)
                if 0 <= b < BATCH:
                    stage_b(b)
                if 0 <= c < BATCH:
                    stage_c(c)
                if a < BATCH:
                    stage_a_zt(a)
                if 0 <= b < BATCH:
                    stage_b_exp(b)
                if w < 2:
                    code(2 * w + 1)

        @block.gpsimd
        def _(pool):
            pool.memset(ident[:], 0.0).then_inc(ident_zero, 1)
            pool.memset(ones[:], 1.0).then_inc(const_done, 1)
            pool.memset(minus_half[:], -0.5).then_inc(const_done, 1)
            pool.memset(prior_eps[:], PRIOR_EPS).then_inc(const_done, 1)
            pool.memset(z_mix[:, :, ACTIVE * RANK:ACTIVE * RANK + 1], 1.0).then_inc(const_done, 1)
            pool.iota(iota_r[:], pattern=[[1, RANK]], base=0, channel_multiplier=0).then_inc(iota_s, 1)
            pool.iota(iota_p[:], pattern=[[1, 1]], base=0, channel_multiplier=1).then_inc(iota_s, 1)
            pool.wait_ge(ident_zero, 1)
            pool.affine_select(out=ident[:], in_=ident[:], compare_op=ALU.not_equal, fill=1.0, base=0,
                               pattern=[[-1, P]], channel_multiplier=1).then_inc(ident_done, 1)

            def rest_qk(head, g):
                wait_from(pool, wq_hi_s, 2 * g + head + 1)
                pool.tensor_tensor(wq_lo[:, head], raw_q[:, head], wq_hi[:, head].bitcast(F32),
                                   ALU.subtract).then_inc(wq_lo_s, 1)
                wait_from(pool, wk_hi_s, 2 * g + head + 1)
                pool.tensor_tensor(wk_lo[:, head], raw_k[:, head], wk_hi[:, head].bitcast(F32),
                                   ALU.subtract).then_inc(wk_lo_s, 1)

            def rest_v(g, n):
                wait_from(pool, wv_hi_s, g + 1)
                pool.tensor_tensor(wv_lo[n][:], raw_v[:], wv_hi[n][:].bitcast(F32), ALU.subtract).then_inc(wv_lo_s, 1)

            def rest_o(g, n):
                wait_from(pool, wo_hi_s, g + 1)
                pool.tensor_tensor(wo_lo[n][:], raw_o[:], wo_hi[n][:].bitcast(F32), ALU.subtract).then_inc(wo_lo_s, 1)

            def make_shift(s, c):
                n = c % 2
                first = 4 * (c // 2 % 2) + 2 * n
                wait_from(pool, s_shifted, s - 1)
                bias_b = bias_sb[:, c // 4 % 2].unsqueeze(1).broadcast_to([P, 2, 2, P])
                mask_b = mask_sb[:, first:first + 2, :].unsqueeze(2).broadcast_to([P, 2, 2, P])
                pool.tensor_tensor(shift[n][:].rearrange("p (b h) k -> p b h k", b=2), bias_b, mask_b,
                                   ALU.add).then_inc(shift_done, 1)

            def x_scale(half):
                cols = slice(4 * half, 4 * half + 4)
                pool.wait_ge(x_ve, half + 1)
                pool.tensor_tensor(rstd[:, cols], var_eps[:, cols], minus_half[:, 0:4], ALU.pow).then_inc(x_rstd, 1)
                pool.wait_ge(x_ms, half + 1)
                pool.tensor_tensor(rms[:, cols], ms_eps[:, cols], minus_half[:, 0:4], ALU.pow).then_inc(x_rms, 1)

            def x_residual(b):
                pool.wait_ge(x_normed, b + 1)
                pool.tensor_tensor(acc[:, b, :], acc[:, b, :], normed[:, b % 3, :], ALU.add).then_inc(x_resid, 1)

            pool.wait_ge(const_done, 2)
            rest_v(0, 0)
            x_scale(0)
            x_residual(0)
            x_residual(1)
            x_scale(1)
            pool.wait_ge(wq_hi_s, 1)
            pool.tensor_tensor(wq_lo[:, 0], raw_q[:, 0], wq_hi[:, 0].bitcast(F32), ALU.subtract).then_inc(wq_lo_s, 1)
            x_residual(2)
            x_residual(3)
            pool.wait_ge(wq_hi_s, 2)
            pool.tensor_tensor(wq_lo[:, 1], raw_q[:, 1], wq_hi[:, 1].bitcast(F32), ALU.subtract).then_inc(wq_lo_s, 1)
            x_residual(4)
            x_residual(5)
            pool.wait_ge(mask_done, 1)
            pool.wait_ge(bias_in[0], 16)
            make_shift(0, 0)
            x_residual(6)
            x_residual(7)
            rest_o(0, 0)
            rest_v(1, 1)

            def step(i, c):
                s = LOOP_STEPS * i + c
                g = 2 * i + c // 4
                last = isinstance(i, int) and i == TURNS - 1
                if not (last and c == LOOP_STEPS - 1):
                    if c == 3:
                        pool.wait_ge(bias_in[1], 16 * (i + 1))
                    if c == 7:
                        pool.wait_ge(bias_in[0], 16 * (i + 2))
                    make_shift(s + 1, (c + 1) % LOOP_STEPS)
                if c % 4 < 2 and not (last and c >= 4):
                    rest_qk(c % 4, g + 1)
                if c % 4 == 2 and not (last and c >= 4):
                    rest_o(g + 1, (c // 4 + 1) % 2)
                if c % 4 == 3 and not last:
                    rest_v(g + 2, (c // 4) % 2)

            for c in range(LOOP_STEPS):
                step(0, c)
            with pool.Fori(1, TURNS - 1) as i:
                for c in range(LOOP_STEPS):
                    step(i, c)
            for c in range(LOOP_STEPS):
                step(TURNS - 1, c)
            for c in range(NC):
                pool.wait_ge(base_hi_s, c + 1)
                pool.tensor_tensor(base_lo[:, c, :], base_raw[:, c, :], base_hi[:, c, :].bitcast(F32),
                                   ALU.subtract).then_inc(base_lo_s, 1)

            def inv_std(stage, b):
                pool.wait_ge(n_ve[stage], b + 1)
                pool.tensor_tensor(t_rstd[:, stage, b:b + 1], t_ve[:, stage, b:b + 1], minus_half[:, 0:1],
                                   ALU.pow).then_inc(n_rs[stage], 1)

            inv_std(0, 0)
            pool.wait_ge(ww_hi_s, 1)
            pool.tensor_tensor(ww_lo[:], ww_f[:], ww_hi[:].bitcast(F32), ALU.subtract).then_inc(ww_lo_s, 1)
            for w in range(BATCH + 5):
                b, c, c_end = w - 1, w - 3, w - 4
                if 0 <= b < BATCH:
                    inv_std(1, b)
                if 0 <= c < BATCH:
                    inv_std(2, c)
                if 0 <= c_end < BATCH:
                    if c_end == 0:
                        pool.wait_ge(rows_in, 48)
                    wait_from(pool, c_add, c_end - 1)
                    pool.wait_ge(b_add, c_end + 1)
                    pool.tensor_tensor(f_scr[c_end % 2][:], acc[:, c_end, :], bias_rows[:], ALU.add).then_inc(c_bias, 1)
                    pool.wait_ge(c_zero, c_end + 1)
                    pool.tensor_tensor(f_scr[2 + c_end % 2][:], f_scr[2 + c_end % 2][:], scale_rows[:],
                                       ALU.mult).then_inc(c_scaled, 1)
                if w + 1 < BATCH:
                    inv_std(0, w + 1)

        @block.vector
        def _(dve):
            def ct_rest(half, c):
                cols = slice(half * HALF, (half + 1) * HALF)
                dve.wait_ge(ct_hi_done, NC * half + c + 1)
                dve.tensor_tensor(ct_lo[:, c, cols], raw_ct[half][:, c, :], ct_hi[:, c, cols].bitcast(F32),
                                  ALU.subtract).then_inc(ct_lo_done, 1)

            def x_statistics(half):
                dve.wait_ge(x_in[half], 16)
                tiles = range(4 * half, 4 * half + 4)
                for b in tiles:
                    dve.bn_stats(stats[:, b, :], acc[:, b, :]).then_inc(x_stats, 1)
                for b in tiles:
                    dve.wait_ge(x_stats, b + 1)
                    dve.bn_aggr(mean_var[:, b, :], stats[:, b, :]).then_inc(x_mean, 1)
                cols = slice(4 * half, 4 * half + 4)
                dve.wait_ge(x_mean, 4 * half + 4)
                dve.tensor_scalar(var_eps[:, cols], mean_var[:, cols, 1], EPS, None, ALU.add).then_inc(x_ve, 1)

            def x_mean_square(half):
                cols = slice(4 * half, 4 * half + 4)
                dve.wait_ge(x_rstd, half + 1)
                dve.tensor_tensor(ms_a[:, cols], mean_var[:, cols, 1], rstd[:, cols], ALU.mult).then_inc(x_chain, 1)
                dve.wait_ge(x_chain, 2 * half + 1)
                dve.tensor_tensor(ms_b[:, cols], ms_a[:, cols], rstd[:, cols], ALU.mult).then_inc(x_chain, 1)
                dve.wait_ge(x_chain, 2 * half + 2)
                dve.tensor_scalar(ms_eps[:, cols], ms_b[:, cols], EPS, None, ALU.add).then_inc(x_ms, 1)

            def x_tile(b):
                if b % 4 == 0:
                    dve.wait_ge(x_rms, b // 4 + 1)
                wait_from(dve, x_resid, b - 2)
                dve.tensor_scalar(normed[:, b % 3, :], acc[:, b, :], mean_var[:, b, 0:1], rstd[:, b:b + 1],
                                  ALU.subtract, ALU.mult).then_inc(x_normed, 1)
                dve.wait_ge(x_normed, b + 1)
                wait_from(dve, x_t, b - 1)
                dve.scalar_tensor_tensor(rms_in[b % 2][:], normed[:, b % 3, :], rms[:, b:b + 1], ln_w_rows[:],
                                         ALU.mult, ALU.mult).then_inc(x_h, 1)

            def x_rest(b):
                dve.wait_ge(x_hi, b + 1)
                cols = slice(b * P, (b + 1) * P)
                dve.tensor_tensor(xt_lo[:, :, cols], blocks(ps_o[b % 2]), xt_hi[:, :, cols].bitcast(F32),
                                  ALU.subtract).then_inc(x_lo, 1)

            def v_evac(t, n, part):
                wait_from(dve, v_done, t + 1)
                dve.tensor_copy(vv[n][:, 2 * part:2 * part + 2, :],
                                ps_v[:].rearrange("p (b c) -> p b c", b=2)).then_inc(v_out, 1)

            def wk_rest(head):
                dve.wait_ge(wk_hi_s, head + 1)
                dve.tensor_tensor(wk_lo[:, head], raw_k[:, head], wk_hi[:, head].bitcast(F32),
                                  ALU.subtract).then_inc(wk_lo_s, 1)

            wk_rest(0)
            for c in range(NC):
                ct_rest(0, c)
            wk_rest(1)
            x_statistics(0)
            v_evac(0, 0, 0)
            ct_rest(1, 0)
            x_mean_square(0)
            ct_rest(1, 1)
            ct_rest(1, 2)
            dve.wait_ge(ln_in, 16)
            x_tile(0)
            ct_rest(1, 3)
            x_tile(1)
            v_evac(1, 0, 1)
            x_statistics(1)
            x_rest(0)
            x_tile(2)
            x_rest(1)
            x_tile(3)
            x_mean_square(1)
            x_rest(2)
            x_tile(4)
            x_rest(3)
            x_tile(5)
            v_evac(2, 1, 0)
            x_rest(4)
            x_tile(6)
            v_evac(3, 1, 1)
            x_rest(5)
            x_tile(7)
            x_rest(6)
            dve.wait_ge(mask_in, 16)
            dve.tensor_scalar(mask_sb[:], mask_raw[:], 1.0, MASKED, ALU.subtract, ALU.mult).then_inc(mask_done, 1)
            x_rest(7)

            def attention_rest(s):
                wait_from(dve, att_hi_s, s + 1)
                dve.tensor_tensor(att_lo[:], blocks(ps_pv), att_hi[:].bitcast(F32), ALU.subtract).then_inc(att_lo_s, 1)

            def add_output(s, c):
                for j in range(2):
                    b = 4 * (c // 2 % 2) + 2 * (c % 2) + j
                    wait_from(dve, o_done, 2 * s + j + 1)
                    if isinstance(s, int) and s < 4:
                        dve.wait_ge(x_resid, b + 1)
                    else:
                        dve.wait_ge(o_added, 2 * s - 6)
                    dve.tensor_tensor(acc[:, b, :], ps_o[j][:], acc[:, b, :], ALU.add).then_inc(o_added, 1)

            def step(i, c, drain=False):
                s = LOOP_STEPS * i + c
                n = c % 2
                start = isinstance(i, int) and i == 0 and c == 0
                if not start and not drain:
                    attention_rest(s - 1)
                dve.wait_ge(s_done, s + 1)
                dve.wait_ge(shift_done, s + 1)
                wait_from(dve, e_done, s - 1)
                dve.tensor_tensor(scores[n][:], blocks(ps_s), shift[n][:], ALU.add).then_inc(s_shifted, 1)
                dve.wait_ge(s_shifted, s + 1)
                dve.tensor_reduce(row_max[:, n, :], scores[n][:], AX_X, ALU.max).then_inc(s_max, 1)
                dve.wait_ge(s_max, s + 1)
                dve.tensor_scalar(neg_max[:, n, :], row_max[:, n, :], -1.0, None, ALU.mult).then_inc(s_neg, 1)
                if not drain and (not isinstance(i, int) or s > 2):
                    v_evac(s + 1, ((c + 1) // 2) % 2, (c + 1) % 2)
                dve.wait_ge(e_done, s + 1)
                dve.reciprocal(row_inv[:, n, :], row_sum[:, n, :]).then_inc(s_inv, 1)
                dve.wait_ge(s_inv, s + 1)
                dve.scalar_tensor_tensor(row_fac[:, n, :], row_max[:, n, :], -MASKED / 3.0, row_inv[:, n, :],
                                         ALU.is_gt, ALU.mult).then_inc(s_fac, 1)
                dve.wait_ge(s_fac, s + 1)
                dve.tensor_tensor(probs[n][:], probs[n][:], row_fac[:, n, :].unsqueeze(2).broadcast_to([P, 4, P]),
                                  ALU.mult).then_inc(p_done, 1)
                if not start:
                    add_output(s - 1, (c - 1) % LOOP_STEPS)

            for c in range(LOOP_STEPS):
                step(0, c)
            dve.wait_ge(act_in, 64)
            dve.wait_ge(iota_s, 2)
            dve.tensor_copy(act_f[:, 0, :], act_i[:]).then_inc(act_chain, 1)
            dve.tensor_copy(iota_rf[:], iota_r[:]).then_inc(act_chain, 1)
            dve.tensor_copy(iota_pf[:], iota_p[:]).then_inc(act_chain, 1)
            dve.wait_ge(act_chain, 3)
            dve.tensor_scalar(act_f[:, 1, :], act_f[:, 0, :], 0.0, float(EXPERTS), ALU.is_lt, ALU.mult).then_inc(act_chain, 1)
            dve.wait_ge(act_chain, 4)
            dve.tensor_tensor(act_f[:, 2, :], act_f[:, 0, :], act_f[:, 1, :], ALU.add).then_inc(act_chain, 1)
            dve.wait_ge(act_chain, 5)
            dve.tensor_scalar(targets[:, ACTIVE * RANK:ZL], act_f[:, 2, :], 0.0, float(EXPERTS - 1), ALU.max,
                              ALU.min).then_inc(act_chain, 1)
            dve.wait_ge(act_chain, 6)
            for j in range(ACTIVE):
                dve.scalar_tensor_tensor(targets[:, j * RANK:(j + 1) * RANK],
                                         targets[:, ACTIVE * RANK + j:ACTIVE * RANK + j + 1].broadcast_to([1, RANK]),
                                         float(RANK), iota_rf[:], ALU.mult, ALU.add).then_inc(act_chain, 1)
            dve.wait_ge(vec_in, 32)
            dve.tensor_tensor(bqk_mul[:], bqk[:, 0, :], bqk[:, 1, :], ALU.mult).then_inc(vec_mul, 1)
            dve.wait_ge(vec_mul, 1)
            dve.tensor_reduce(bqk_sum[:], bqk_mul[:], AX_X, ALU.add).then_inc(vec_sum, 1)

            with dve.Fori(1, TURNS - 1) as i:
                for c in range(LOOP_STEPS):
                    step(i, c)
            for c in range(5):
                step(TURNS - 1, c)

            def weighted_rows(k, w_raw, vec):
                dve.tensor_scalar(normed[:, k, :], w_raw[:, 0, :], bqk[:, vec, 0:1], None, ALU.mult).then_inc(vec_acc, 1)
                for c in range(1, NC):
                    dve.wait_ge(vec_acc, NC * (1 - k) + c)
                    dve.scalar_tensor_tensor(normed[:, k, :], w_raw[:, c, :], bqk[:, vec, c:c + 1], normed[:, k, :],
                                             ALU.mult, ALU.add).then_inc(vec_acc, 1)

            dve.wait_ge(w1_in[0], 16)
            weighted_rows(1, wk1_raw, 0)
            dve.wait_ge(o_done, 2 * (STEPS - 4))
            for c in range(NC):
                dve.wait_ge(w1_hi_s, c + 1)
                dve.tensor_tensor(wk1_lo[:, c, :], wk1_raw[:, c, :], wk1_hi[:, c, :].bitcast(F32),
                                  ALU.subtract).then_inc(w1_lo_s, 1)
            step(TURNS - 1, 5)
            dve.wait_ge(w1_in[1], 16)
            weighted_rows(0, wq1_raw, 1)
            dve.wait_ge(k_done, STEPS)
            for c in range(NC):
                dve.wait_ge(w1_hi_s, NC + c + 1)
                dve.tensor_tensor(wq1_lo[:, c, :], wq1_raw[:, c, :], wq1_hi[:, c, :].bitcast(F32),
                                  ALU.subtract).then_inc(w1_lo_s, 1)

            def mm_rest(m):
                dve.wait_ge(mm_hi_s, m + 1)
                dve.tensor_tensor(mm_lo[:, m, :], (ps_q, ps_k)[m % 2][:], mm_hi[:, m, :].bitcast(F32),
                                  ALU.subtract).then_inc(mm_out, 1)

            def g_evac(n):
                dve.wait_ge(g_done, n + 1)
                m, half = n % NC, n // NC
                dve.tensor_scalar(gg[:, m, half * HALF:(half + 1) * HALF], g_banks[n][:], uw[:, m:m + 1], None,
                                  ALU.add).then_inc(g_out, 1)

            def r_evac(half):
                dve.wait_ge(r_done, half + 1)
                dve.tensor_scalar(r_row[:, half * HALF:(half + 1) * HALF], r_banks[half][:], uw[:, 2 * NC:2 * NC + 1],
                                  None, ALU.add).then_inc(r_out, 1)

            def unpack_code(v):
                word, down = ((0, 0), (0, 6), (1, 0), (2, 0))[v]
                dve.wait_ge(packed_in, 16)
                wait_from(dve, codes_s, v)
                dve.tensor_scalar(unpack[:], packed[:, word, :], down, 63, ALU.logical_shift_right,
                                  ALU.bitwise_and).then_inc(unp, 1)

            v_evac(STEPS - 1, 1, 1)
            attention_rest(STEPS - 3)
            step(TURNS - 1, 6, drain=True)
            dve.wait_ge(vec_mm, 1)
            dve.tensor_copy(uw[:], ps_v[:, 0:9]).then_inc(vec_out, 1)
            mm_rest(0)
            dve.wait_ge(tgt_mm, 1)
            dve.wait_ge(act_chain, 10)
            dve.tensor_scalar(select[:], ps_v[:, 0:ZL], iota_pf[:, 0:1], None, ALU.is_equal).then_inc(sel_s, 1)
            for n in range(2):
                dve.tensor_scalar(rb_cols[:, n, :], ones[0:EXPERTS, :], rb_sb[:, n:n + 1], None,
                                  ALU.mult).then_inc(rbc_s, 1)
            mm_rest(1)
            mm_rest(2)
            attention_rest(STEPS - 2)
            dve.wait_ge(lr_mm, 1)
            dve.wait_ge(lbias, 1)
            dve.tensor_copy(low_rank_in[:], ps_v[:, 0:NC * ZL].rearrange("p (c z) -> p c z", z=ZL)).then_inc(lr_out, 1)
            dve.wait_ge(lr_out, 1)
            dve.tensor_tensor(logit_bias[:, 1, :], logit_bias[:, 0, :], ps_v[:, 144:148], ALU.add).then_inc(lr_out, 1)
            mm_rest(3)
            step(TURNS - 1, 7, drain=True)
            dve.wait_ge(lb_mm, 1)
            dve.tensor_copy(low_rank_out[0:ACTIVE * RANK, :], ps_v[0:ACTIVE * RANK, :]).then_inc(lb_out, 1)

            def normalise(stage, b, before, count):
                dve.wait_ge(before, count)
                dve.bn_stats(t_stats[:, stage, b, :], acc[:, b, :]).then_inc(n_st[stage], 1)
                dve.wait_ge(n_st[stage], b + 1)
                dve.bn_aggr(t_mv[:, stage, b, :], t_stats[:, stage, b, :]).then_inc(n_mv[stage], 1)
                dve.wait_ge(n_mv[stage], b + 1)
                dve.tensor_scalar(t_ve[:, stage, b:b + 1], t_mv[:, stage, b, 1:2], EPS, None,
                                  ALU.add).then_inc(n_ve[stage], 1)

            def normalise_end(stage, b):
                dve.wait_ge(n_rs[stage], b + 1)
                wait_from(dve, n_t[stage], b)
                if stage == 2:
                    wait_from(dve, c_sum, b)
                dve.tensor_scalar(normed[:, stage, :], acc[:, b, :], t_mv[:, stage, b, 0:1],
                                  t_rstd[:, stage, b:b + 1], ALU.subtract, ALU.mult).then_inc(n_xn[stage], 1)

            def a_rest(b):
                dve.wait_ge(a_hi_s, b + 1)
                dve.tensor_tensor(a_lo[:], blocks(ps_s), a_hi[:].bitcast(F32), ALU.subtract).then_inc(a_lo_s, 1)

            def a_route(b):
                dve.wait_ge(z_mm, b + 1)
                dve.tensor_tensor(logits[:, b, :], ps_k[:, ACTIVE * RANK:ZL], logit_bias[:, 1, :],
                                  ALU.add).then_inc(lg_c, 1)
                dve.wait_ge(lg_c, 3 * b + 1)
                dve.tensor_reduce(l_max[:, b, 0:1], logits[:, b, :], AX_X, ALU.max).then_inc(lg_c, 1)
                dve.wait_ge(lg_c, 3 * b + 2)
                dve.tensor_scalar(l_max[:, b, 1:2], l_max[:, b, 0:1], -1.0, None, ALU.mult).then_inc(lg_c, 1)

            def a_mix(b):
                dve.wait_ge(lg_exp, b + 1)
                dve.reciprocal(l_sum[:, b, 1:2], l_sum[:, b, 0:1]).then_inc(z_mixed, 1)
                dve.wait_ge(z_mixed, 3 * b + 1)
                dve.tensor_scalar(alpha[:, b, :], l_exp[:, b, :], l_sum[:, b, 1:2], LORA_SCALE, ALU.mult,
                                  ALU.mult).then_inc(z_mixed, 1)
                dve.wait_ge(z_mixed, 3 * b + 2)
                wait_from(dve, zt_mm, b - 1)
                dve.tensor_tensor(z_mix[:, b % 2, 0:ACTIVE * RANK].rearrange("p (e r) -> p e r", r=RANK),
                                  ps_k[:, 0:ACTIVE * RANK].rearrange("p (e r) -> p e r", r=RANK),
                                  alpha[:, b, :].unsqueeze(2).broadcast_to([P, ACTIVE, RANK]),
                                  ALU.mult).then_inc(z_mixed, 1)

            def a_finish(b):
                dve.wait_ge(y_mm, b + 1)
                dve.wait_ge(n_xn[0], b + 1)
                dve.tensor_tensor(acc[:, b, :], ps_q[:], acc[:, b, :], ALU.add).then_inc(a_add, 1)

            def b_softmax(b):
                dve.wait_ge(bs_mm, b + 1)
                dve.tensor_reduce(b_max[:, b, 0:1], ps_v[:, 0:P], AX_X, ALU.max).then_inc(b_c, 1)
                dve.wait_ge(b_c, 2 * b + 1)
                dve.tensor_scalar(b_max[:, b, 1:2], b_max[:, b, 0:1], -SCORE_SCALE, None, ALU.mult).then_inc(b_c, 1)

            def b_finish(b):
                dve.wait_ge(b_exp, b + 1)
                dve.reciprocal(b_sum[:, b, 1:2], b_sum[:, b, 0:1]).then_inc(b_inv, 1)
                dve.wait_ge(b_inv, b + 1)
                dve.wait_ge(at_mm, b + 1)
                dve.scalar_tensor_tensor(acc[:, b, :], ps_o[0][:], b_sum[:, b, 1:2], acc[:, b, :], ALU.mult,
                                         ALU.add).then_inc(b_add, 1)

            def c_rest(b):
                dve.wait_ge(c_hi_s, b + 1)
                dve.tensor_tensor(c_lo[:], blocks(ps_pv), c_hi[:].bitcast(F32), ALU.subtract).then_inc(c_lo_s, 1)
                dve.wait_ge(c_sum, b + 1)
                dve.tensor_scalar(x_sum[:, b, 1:2], x_sum[:, b, 0:1], -1.0, None, ALU.mult).then_inc(c_neg, 1)

            def c_zero_point(b):
                dve.wait_ge(c_neg, b + 1)
                dve.wait_ge(c_mm, b + 1)
                wait_from(dve, c_add, b - 1)
                dve.scalar_tensor_tensor(f_scr[2 + b % 2][:], zero_rows[:], x_sum[:, b, 1:2], ps_o[1][:], ALU.mult,
                                         ALU.add).then_inc(c_zero, 1)

            def c_finish(b):
                dve.wait_ge(c_scaled, b + 1)
                dve.wait_ge(c_bias, b + 1)
                dve.tensor_tensor(acc[:, b, :], f_scr[2 + b % 2][:], f_scr[b % 2][:], ALU.add).then_inc(c_add, 1)

            def ready(b):
                return 2 * (STEPS - 2) if b < 4 else 2 * STEPS

            dve.wait_ge(vec_mm, 1)
            normalise(0, 0, o_added, ready(0))
            g_evac(0)
            normalise_end(0, 0)
            g_evac(1)
            attention_rest(STEPS - 1)
            g_evac(2)
            add_output(STEPS - 1, LOOP_STEPS - 1)
            dve.wait_ge(vec_out, 1)
            dve.wait_ge(o_done, 2 * STEPS)
            for c in range(NC):
                dve.tensor_scalar(ww_f[:, c, :], ones[:], uw[:, NC + c:NC + c + 1], None, ALU.mult).then_inc(ww_s, 1)
            g_evac(3)
            for w in range(BATCH + 5):
                a, b, b_end, c, c_end = w, w - 1, w - 2, w - 3, w - 4
                has_a, has_b, has_b_end, has_c, has_c_end = (0 <= t < BATCH for t in (a, b, b_end, c, c_end))
                if has_b:
                    normalise(1, b, a_add, b + 1)
                if has_c:
                    normalise(2, c, b_add, c + 1)
                if has_c_end:
                    if c_end == 0:
                        dve.wait_ge(rows_in, 48)
                    c_zero_point(c_end)
                if w < 2:
                    unpack_code(2 * w)
                if has_a:
                    a_rest(a)
                if has_b_end:
                    b_finish(b_end)
                if has_b:
                    normalise_end(1, b)
                if has_a:
                    a_route(a)
                if has_c:
                    normalise_end(2, c)
                if has_a:
                    a_mix(a)
                if w < 3:
                    g_evac(4 + (0, 1, 3)[w])
                if w < 2:
                    unpack_code(2 * w + 1)
                if has_c_end:
                    c_finish(c_end)
                if a + 1 < BATCH:
                    normalise(0, a + 1, o_added, ready(a + 1))
                if has_c:
                    c_rest(c)
                if has_b:
                    b_softmax(b)
                if a + 1 < BATCH:
                    normalise_end(0, a + 1)
                if has_a:
                    a_finish(a)
                if w == 0:
                    r_evac(0)
                if w == 1:
                    g_evac(6)
                if w == 2:
                    r_evac(1)

        @block.tensor
        def _(pe):
            def project_k(t, c, first_use=False):
                head, half = c % 2, c // 2 % 2
                cols = slice(half * HALF, (half + 1) * HALF)
                for m in range(NC):
                    if first_use:
                        pe.wait_ge(ct_lo_done, NC * half + m + 1)
                    last = three(pe, ps_k[:], wk_hi[:, head, m, :], wk_lo[:, head, m, :], ct_hi[:, m, cols],
                                 ct_lo[:, m, cols], m == 0, m == NC - 1)
                last.then_inc(k_done, 1)

            def project_q(t, c):
                head, half = c % 2, c // 2 % 2
                cols = slice(half * HALF, (half + 1) * HALF)
                for m in range(NC):
                    last = three(pe, ps_q[:], wq_hi[:, head, m, :], wq_lo[:, head, m, :], xt_hi[:, m, cols],
                                 xt_lo[:, m, cols], m == 0, m == NC - 1)
                last.then_inc(q_done, 1)

            def project_v(t, c):
                n, first = c // 4 % 2, 4 * (c // 2 % 2) + 2 * (c % 2)
                for j in range(2):
                    cols = slice((first + j) * P, (first + j + 1) * P)
                    for m in range(NC):
                        last = three(pe, ps_v[:, j * 2 * P:(j + 1) * 2 * P], ct_hi[:, m, cols], ct_lo[:, m, cols],
                                     wv_hi[n][:, m, :], wv_lo[n][:, m, :], m == 0, m == NC - 1)
                last.then_inc(v_done, 1)

            def x_transpose(b):
                pe.wait_ge(x_h, b + 1)
                wait_from(pe, x_lo, b - 1)
                for m in range(NC):
                    last = pe.transpose(ps_o[b % 2][:, m * P:(m + 1) * P], rms_in[b % 2][:, m * P:(m + 1) * P], ident[:])
                last.then_inc(x_t, 1)

            pe.wait_ge(wk_lo_s, 1)
            project_k(0, 0, first_use=True)
            pe.wait_ge(wv_lo_s, 1)
            project_v(0, 0)
            pe.wait_ge(wk_lo_s, 2)
            pe.wait_ge(k_out, 1)
            project_k(1, 1)
            pe.wait_ge(v_out, 1)
            project_v(1, 1)
            pe.wait_ge(k_out, 2)
            project_k(2, 2, first_use=True)
            pe.wait_ge(ident_done, 1)
            x_transpose(0)
            x_transpose(1)
            pe.wait_ge(k_out, 3)
            project_k(3, 3)
            x_transpose(2)
            x_transpose(3)
            pe.wait_ge(v_out, 2)
            project_v(2, 2)
            x_transpose(4)
            pe.wait_ge(v_out, 3)
            project_v(3, 3)
            x_transpose(5)
            pe.wait_ge(x_lo, 4)
            pe.wait_ge(wq_lo_s, 1)
            project_q(0, 0)
            x_transpose(6)
            pe.wait_ge(wq_lo_s, 2)
            pe.wait_ge(q_out, 1)
            project_q(1, 1)
            x_transpose(7)

            def output(s, c, g=None):
                wait_from(pe, att_lo_s, s + 1)
                if g is not None:
                    pe.wait_ge(wo_lo_s, g + 1)
                n = c // 4 % 2
                for j in range(2):
                    wait_from(pe, o_added, 2 * s + j - 1)
                    for h in range(2):
                        last = three(pe, ps_o[j][:], att_hi[:, 2 * j + h, :], att_lo[:, 2 * j + h, :],
                                     wo_hi[n][:, h, :], wo_lo[n][:, h, :], h == 0, h == 1)
                    last.then_inc(o_done, 1)

            def step_scores(s, c):
                u0 = s - c % 2
                pe.wait_ge(q_out, u0 + 2)
                pe.wait_ge(k_out, u0 + 2)
                wait_from(pe, s_shifted, s)
                n = c // 2 % 2
                for j in range(2):
                    cols = slice((2 * (c % 2) + j) * P, (2 * (c % 2) + j + 1) * P)
                    for h in range(2):
                        m = 2 * j + h
                        last = pe.matmul(ps_s[:, m * P:(m + 1) * P], qt[n][:, h, cols], kt[n][:, h, cols],
                                         start=True, stop=True)
                last.then_inc(s_done, 1)

            def step_transpose(s, c):
                pe.wait_ge(p_done, s + 1)
                wait_from(pe, pt_out, s)
                for m in range(4):
                    last = pe.transpose(ps_t[:, m * P:(m + 1) * P], probs[c % 2][:, m, :], ident[:])
                last.then_inc(pt_done, 1)

            def step_values(s, c):
                pe.wait_ge(pt_out, s + 1)
                pe.wait_ge(v_out, s - c % 2 + 2)
                wait_from(pe, att_lo_s, s)
                n = c // 2 % 2
                for j in range(2):
                    for h in range(2):
                        m = 2 * j + h
                        last = pe.matmul(ps_pv[:, m * P:(m + 1) * P], vv[n][:, 2 * (c % 2) + j, h * P:(h + 1) * P],
                                         probs_t[:, m, :], start=True, stop=True)
                last.then_inc(pv_done, 1)

            def step(i, c):
                s = LOOP_STEPS * i + c
                t, tc = s + 2, (c + 2) % LOOP_STEPS
                gt = 2 * i + (c + 2) // 4
                step_scores(s, c)
                if isinstance(i, int) and s == 0:
                    pe.wait_ge(x_lo, 8)
                ahead = not isinstance(i, int) or s > 1
                pe.wait_ge(wq_lo_s, 2 * gt + c % 2 + 1)
                pe.wait_ge(q_out, t)
                project_q(t, tc)
                if c > 0 or not isinstance(i, int) or i > 0:
                    output(s - 1, (c - 1) % LOOP_STEPS, 2 * i + c // 4 if c % 4 == 1 else None)
                if ahead:
                    pe.wait_ge(wk_lo_s, 2 * gt + c % 2 + 1)
                    pe.wait_ge(k_out, t)
                    project_k(t, tc)
                step_transpose(s, c)
                if ahead:
                    pe.wait_ge(wv_lo_s, gt + 1)
                    pe.wait_ge(v_out, t)
                    project_v(t, tc)
                step_values(s, c)

            for c in range(LOOP_STEPS):
                step(0, c)
            with pe.Fori(1, TURNS - 1) as i:
                for c in range(LOOP_STEPS):
                    step(i, c)
            for c in range(6):
                step(TURNS - 1, c)

            def product_m(m):
                if m == 0:
                    pe.wait_ge(w1_lo_s, NC)
                    pe.wait_ge(q_out, STEPS)
                    pe.wait_ge(k_out, STEPS)
                wait_from(pe, mm_out, m - 1)
                cols = slice(m * P, (m + 1) * P)
                for c in range(NC):
                    if m == 0:
                        pe.wait_ge(w1_lo_s, NC + c + 1)
                    last = three(pe, (ps_q, ps_k)[m % 2][:], wk1_hi[:, c, cols], wk1_lo[:, c, cols], wq1_hi[:, c, :],
                                 wq1_lo[:, c, :], c == 0, c == NC - 1)
                last.then_inc(mm_done, 1)

            def product_g(n):
                m, half = n % NC, n // NC
                if n == 0:
                    pe.wait_ge(mm_out, NC)
                if n == 2:
                    pe.wait_ge(lb_out, 1)
                if n == 3:
                    pe.wait_ge(pt_out, STEPS)
                if n == 4:
                    pe.wait_ge(att_lo_s, STEPS)
                if n == 5:
                    pe.wait_ge(o_added, 2 * STEPS)
                if n > 5:
                    pe.wait_ge(g_out, n - 1)
                cols, rows = slice(m * P, (m + 1) * P), slice(half * HALF, (half + 1) * HALF)
                for c in range(NC):
                    last = three(pe, g_banks[n][:], mm_hi[:, c, cols], mm_lo[:, c, cols], ct_hi[:, c, rows],
                                 ct_lo[:, c, rows], c == 0, c == NC - 1)
                last.then_inc(g_done, 1)

            def product_r(half):
                pe.wait_ge(ww_lo_s, 1)
                pe.wait_ge(g_out, (3, 7)[half])
                rows = slice(half * HALF, (half + 1) * HALF)
                for c in range(NC):
                    last = three(pe, r_banks[half][:], ww_hi[:, c, :], ww_lo[:, c, :], ct_hi[:, c, rows], ct_lo[:, c, rows],
                                 c == 0, c == NC - 1)
                last.then_inc(r_done, 1)

            s = STEPS - 2
            step_scores(s, 6)
            product_m(0)
            pe.wait_ge(v_out, STEPS)
            pe.wait_ge(vec_acc, 2 * NC)
            pe.wait_ge(vec_sum, 1)
            pe.wait_ge(const_done, 4)
            for k in range(2):
                for m in range(NC):
                    pe.matmul(ps_v[:, NC * k + m:NC * k + m + 1], normed[:, k, m * P:(m + 1) * P], ones[:, 0:1],
                              start=True, stop=True)
            pe.matmul(ps_v[:, 2 * NC:2 * NC + 1], ones[:], bqk_sum[:], start=True, stop=True).then_inc(vec_mm, 1)
            output(s - 1, 5)
            pe.wait_ge(vec_out, 1)
            pe.wait_ge(act_chain, 10)
            pe.matmul(ps_v[:, 0:ZL], ones[0:1, :], targets[:], start=True, stop=True).then_inc(tgt_mm, 1)
            product_m(1)
            step_transpose(s, 6)
            product_m(2)
            step_values(s, 6)
            pe.wait_ge(sel_s, 1)
            pe.wait_ge(rbc_s, 2)
            pe.wait_ge(lora_in, 48)
            for c in range(NC):
                cols = slice(c * P, (c + 1) * P)
                pe.matmul(ps_v[:, c * ZL:c * ZL + ACTIVE * RANK], lora_a_sb[:, cols], select[:, 0:ACTIVE * RANK],
                          start=True, stop=True)
                pe.matmul(ps_v[:, c * ZL + ACTIVE * RANK:(c + 1) * ZL], router_sb[:, cols],
                          select[0:EXPERTS, ACTIVE * RANK:ZL], start=True, stop=True)
            for n in range(2):
                last = pe.matmul(ps_v[:, NC * ZL + ACTIVE * n:NC * ZL + ACTIVE * (n + 1)], rb_cols[:, n, :],
                                 select[0:EXPERTS, ACTIVE * RANK:ZL], start=True, stop=True)
            last.then_inc(lr_mm, 1)
            product_m(3)
            s = STEPS - 1
            step_scores(s, 7)
            output(s - 1, 6)
            pe.wait_ge(lr_out, 2)
            pe.matmul(ps_v[0:ACTIVE * RANK, :], select[:, 0:ACTIVE * RANK], lora_b_sb[:], start=True,
                      stop=True).then_inc(lb_mm, 1)
            product_g(0)
            step_transpose(s, 7)
            product_g(1)
            step_values(s, 7)
            product_g(2)
            output(s, 7)
            product_g(3)

            banks = (ps_s, ps_t, ps_pv)

            def transpose(stage, b, freed):
                pe.wait_ge(n_xn[stage], b + 1)
                wait_from(pe, freed, b)
                if b == 0 and stage == 0:
                    pe.wait_ge(s_shifted, STEPS)
                if b == 0 and stage == 1:
                    pe.wait_ge(g_out, 4)
                if b == 0 and stage == 2:
                    pe.wait_ge(r_out, 2)
                for m in range(NC):
                    src = normed[:, stage, m * P:(m + 1) * P] if stage < 2 else normed[:, stage, m:D:NC]
                    last = pe.transpose(banks[stage][:, m * P:(m + 1) * P], src, ident[:])
                last.then_inc(n_t[stage], 1)

            def a_low_rank(b):
                pe.wait_ge(a_full_s, b + 1)
                if b == 0:
                    pe.wait_ge(g_out, 2)
                wait_from(pe, zt_out, b)
                wait_from(pe, z_mixed, 3 * b)
                for c in range(NC):
                    last = pe.matmul(ps_k[:, 0:ZL], a_full[:, c, :], low_rank_in[:, c, :], start=(c == 0),
                                     stop=(c == NC - 1))
                last.then_inc(z_mm, 1)

            def a_base(b):
                pe.wait_ge(a_lo_s, b + 1)
                if b == 0:
                    pe.wait_ge(base_lo_s, NC)
                    pe.wait_ge(g_out, 1)
                wait_from(pe, a_add, b)
                for c in range(NC):
                    three(pe, ps_q[:], a_hi[:, c, :], a_lo[:, c, :], base_hi[:, c, :], base_lo[:, c, :], c == 0, False)

            def a_mix_t(b):
                pe.wait_ge(z_mixed, 3 * b + 3)
                pe.transpose(ps_k[0:ACTIVE * RANK + 1, P:2 * P], z_mix[:, b % 2, :], ident[:]).then_inc(zt_mm, 1)

            def a_end(b):
                pe.wait_ge(zt_out, b + 1)
                pe.matmul(ps_q[:], z_mix_t[:], low_rank_out[:], start=False, stop=True).then_inc(y_mm, 1)

            def b_scores(b):
                pe.wait_ge(b_full_s, b + 1)
                wait_from(pe, bt_out, b)
                pe.wait_ge(g_out, NC if b < 4 else 2 * NC)
                pe.wait_ge(r_out, 1 if b < 4 else 2)
                cols = slice(b * P, (b + 1) * P)
                for c in range(NC):
                    pe.matmul(ps_v[:, 0:P], b_full[:, c, :], gg[:, c, cols], start=(c == 0), stop=False)
                pe.matmul(ps_v[:, 0:P], ones[0:1, :], r_row[0:1, cols], start=False, stop=True).then_inc(bs_mm, 1)

            def b_transpose(b):
                pe.wait_ge(b_exp, b + 1)
                pe.transpose(ps_v[:, 2 * P:3 * P], b_probs[:], ident[:]).then_inc(bt_mm, 1)

            def b_attend(b):
                pe.wait_ge(bt_out, b + 1)
                if b == 0:
                    pe.wait_ge(ctx_in, 16)
                    pe.wait_ge(o_added, 2 * STEPS)
                wait_from(pe, b_add, b)
                pe.matmul(ps_o[0][:], b_probs_t[:], ctx_sb[:, b, :], start=True, stop=True).then_inc(at_mm, 1)

            def c_product(b):
                pe.wait_ge(c_lo_s, b + 1)
                if b == 0:
                    pe.wait_ge(codes_s, 4)
                    pe.wait_ge(g_out, 2 * NC)
                wait_from(pe, c_zero, b)
                for c in range(NC):
                    pe.matmul(ps_o[1][:], c_hi[:, c, :], codes[:, c, :], start=(c == 0), stop=False)
                    last = pe.matmul(ps_o[1][:], c_lo[:, c, :], codes[:, c, :], start=False, stop=(c == NC - 1))
                last.then_inc(c_mm, 1)

            for w in range(BATCH + 3):
                a, b, b_end, c = w, w - 1, w - 2, w - 3
                has_a, has_b, has_b_end, has_c = (0 <= t < BATCH for t in (a, b, b_end, c))
                if has_b_end:
                    b_transpose(b_end)
                if has_a:
                    transpose(0, a, a_lo_s)
                if has_b_end:
                    b_attend(b_end)
                if has_a:
                    a_low_rank(a)
                    a_base(a)
                if w < 3:
                    product_g(4 + (0, 1, 3)[w])
                if has_b:
                    transpose(1, b, b_full_s)
                if has_c:
                    transpose(2, c, c_lo_s)
                if has_a:
                    a_mix_t(a)
                if has_b:
                    b_scores(b)
                if has_a:
                    a_end(a)
                if has_c:
                    c_product(c)
                if w == 0:
                    product_r(0)
                if w == 1:
                    product_g(6)
                if w == 2:
                    product_r(1)


def kernel(**inputs):
    import numpy as np
    import concourse.bacc as bacc
    from concourse.bass_utils import run_bass_kernel_spmd

    def get(name):
        return np.asarray(inputs[name])

    def keep(a):
        return np.ascontiguousarray(a)

    g = GROUPS
    arrays = {
        "x": keep(get("x").reshape(TOK, D)),
        "ctx_nat": keep(get("ctx_4096").reshape(TOK, D)),
        "ctx_t": keep(get("ctx_4096").reshape(TOK, NC, P).transpose(2, 1, 0)),
        "mask": keep(get("mask_BxSxS2_bk0").transpose(1, 0, 2)),
        "bias": keep(get("L0_xattn_position_bias").reshape(g, 2, P, P).transpose(0, 2, 1, 3)),
        "ln_w": keep(get("L0_xattn_ln_weight").reshape(1, D)),
        "w_q": keep(get("L0_xattn_w_q").reshape(g, 2, P, NC, P).transpose(0, 4, 1, 3, 2).reshape(g, P, 2 * D)),
        "w_k": keep(get("L0_xattn_w_k").reshape(g, 2, P, NC, P).transpose(0, 4, 1, 3, 2).reshape(g, P, 2 * D)),
        "w_v": keep(get("L0_xattn_w_v").reshape(g, 2 * P, NC, P).transpose(0, 3, 2, 1).reshape(g, P, 2 * D)),
        "w_o": keep(get("L0_xattn_w_out").reshape(D, g, 2, P).transpose(1, 3, 2, 0).reshape(g, P, 2 * D)),
        "w_base": keep(get("L0_ffn_W_base").reshape(D, NC, P).transpose(2, 1, 0)),
        "b_base": keep(get("L0_ffn_b_base").reshape(1, D)),
        "lora_a": keep(get("L0_ffn_lora_A").reshape(EXPERTS * RANK, D)),
        "lora_b": keep(get("L0_ffn_lora_B").transpose(0, 2, 1).reshape(EXPERTS * RANK, D)),
        "router_w": keep(get("L0_ffn_router_W")),
        "router_b": keep(get("L0_ffn_router_b").reshape(EXPERTS, 1)),
        "prior": keep(get("L0_ffn_domain_prior").reshape(EXPERTS, 1)),
        "active": keep(get("L0_ffn_active").reshape(1, ACTIVE)),
        "wq1": keep(get("L1_xattn_Wq").reshape(NC, P, D).transpose(1, 0, 2)),
        "bq1": keep(get("L1_xattn_bq").reshape(NC, P).T),
        "wk1": keep(get("L1_xattn_Wk").reshape(NC, P, D).transpose(1, 0, 2)),
        "bk1": keep(get("L1_xattn_bk").reshape(NC, P).T),
        "qweight": keep(get("L1_ffn_qweight").reshape(D, P, 3).transpose(1, 2, 0)),
        "w_scale": keep(get("L1_ffn_weight_scale").reshape(1, D)),
        "w_zero": keep(get("L1_ffn_weight_zero_point").reshape(1, D)),
        "ffn_bias": keep(get("L1_ffn_bias").reshape(1, D)),
    }
    nc = bacc.Bacc("TRN2", target_bir_lowering=False, num_devices=1)
    args = [nc.dram_tensor(f"in_{name}", a.shape, mybir.dt.from_np(a.dtype), kind="ExternalInput").ap()
            for name, a in arrays.items()]
    args.append(nc.dram_tensor("out_x", (TOK, D), F32, kind="ExternalOutput").ap())
    build(nc, *args)
    done = run_bass_kernel_spmd(nc, [{f"in_{name}": a for name, a in arrays.items()}], core_ids=[0])
    return done.results[0]["out_x"].reshape(BATCH, P, D)
```

```python
from contextlib import ExitStack

import concourse.bass as bass
from concourse import mybir

F32 = mybir.dt.float32
F32R = mybir.dt.float32r
I32 = mybir.dt.int32
U8 = mybir.dt.uint8
ALU = mybir.AluOpType
ACT = mybir.ActivationFunctionType
AX_X = mybir.AxisListType.X

P = 128
BATCH, D, HEADS = 8, 512, 32
NC = D // P
TOK = BATCH * P
HALF = TOK // 2
GROUPS = HEADS // 2
STEPS = 4 * GROUPS
LOOP_STEPS = 8
TURNS = STEPS // LOOP_STEPS
EXPERTS, ACTIVE, RANK = 16, 4, 8
ZL = ACTIVE * RANK + ACTIVE
LORA_SCALE = 16.0 / 8.0
EPS = 1e-5
PRIOR_EPS = 1e-12
MASKED = 3e38
SCORE_SCALE = float(D) ** -0.5


def wait_from(eng, sem, value):
    if not isinstance(value, int) or value > 0:
        eng.wait_ge(sem, value)


def build(nc, x, ctx_nat, ctx_t, mask, bias, ln_w, w_q, w_k, w_v, w_o, w_base, b_base, lora_a, lora_b,
          router_w, router_b, prior, active, wq1, bq1, wk1, bk1, qweight, w_scale, w_zero, ffn_bias, out):
    with ExitStack() as stack:
        top = [(nc.sbuf_base + 63) // 64 * 64]
        sizes = {F32: 4, F32R: 4, I32: 4, U8: 1}

        def place(name, shape, dt, at=None):
            size = sizes[dt]
            for n in shape[1:]:
                size *= n
            if at is None:
                at = top[0]
                top[0] += (size + 31) // 32 * 32
                assert top[0] <= nc.sbuf_usable_end, (name, top)
            return nc.alloc_sbuf_tensor_at(name, shape, dt, offset=at), at

        xt_hi, at_xt_hi = place("xt_hi", [P, NC, TOK], F32R)
        xt_lo, at_xt_lo = place("xt_lo", [P, NC, TOK], F32R)
        ct_hi, at_ct_hi = place("ct_hi", [P, NC, TOK], F32R)
        ct_lo, at_ct_lo = place("ct_lo", [P, NC, TOK], F32R)
        acc, _ = place("acc", [P, BATCH, D], F32)
        wq_hi, at_wq = place("wq_hi", [P, 2, NC, P], F32R)
        wq_lo, _ = place("wq_lo", [P, 2, NC, P], F32R)
        wk_hi, _ = place("wk_hi", [P, 2, NC, P], F32R)
        wk_lo, _ = place("wk_lo", [P, 2, NC, P], F32R)
        wv_hi, wv_lo, wo_hi, wo_lo, at_wv, at_wo = [0, 0], [0, 0], [0, 0], [0, 0], [0, 0], [0, 0]
        for n in range(2):
            wv_hi[n], at_wv[n] = place(f"wv_hi{n}", [P, NC, 2 * P], F32R)
            wv_lo[n], _ = place(f"wv_lo{n}", [P, NC, 2 * P], F32R)
            wo_hi[n], at_wo[n] = place(f"wo_hi{n}", [P, 2, D], F32R)
            wo_lo[n], _ = place(f"wo_lo{n}", [P, 2, D], F32R)
        raw_q, at_raw = place("raw_q", [P, 2, NC, P], F32)
        raw_k, _ = place("raw_k", [P, 2, NC, P], F32)
        raw_v, _ = place("raw_v", [P, NC, 2 * P], F32)
        raw_o, _ = place("raw_o", [P, 2, D], F32)
        qt, kt, vv, at_qkv = [0, 0], [0, 0], [0, 0], [0, 0]
        for n in range(2):
            qt[n], at_qkv[n] = place(f"qt{n}", [P, 2, HALF], F32)
            kt[n], _ = place(f"kt{n}", [P, 2, HALF], F32)
            vv[n], _ = place(f"vv{n}", [P, 4, 2 * P], F32)
        scores, probs, shift, at_scores, at_probs = [0, 0], [0, 0], [0, 0], [0, 0], [0, 0]
        for n in range(2):
            scores[n], at_scores[n] = place(f"scores{n}", [P, 4, P], F32)
            probs[n], at_probs[n] = place(f"probs{n}", [P, 4, P], F32)
            shift[n], _ = place(f"shift{n}", [P, 4, P], F32)
        probs_t, _ = place("probs_t", [P, 4, P], F32)
        att_hi, at_att_hi = place("att_hi", [P, 4, P], F32R)
        att_lo, _ = place("att_lo", [P, 4, P], F32R)
        bias_sb, _ = place("bias_sb", [P, 2, 2, P], F32)
        mask_sb, _ = place("mask_sb", [P, BATCH, P], F32)
        ident, _ = place("ident", [P, P], F32)
        ones, _ = place("ones", [P, P], F32)
        low_rank_in, _ = place("low_rank_in", [P, NC, ZL], F32)
        low_rank_out, _ = place("low_rank_out", [ACTIVE * RANK + 1, D], F32)
        normed, _ = place("normed", [P, 3, D], F32)
        row_max, _ = place("row_max", [P, 2, 4], F32)
        neg_max, _ = place("neg_max", [P, 2, 4], F32)
        row_sum, _ = place("row_sum", [P, 2, 4], F32)
        row_inv, _ = place("row_inv", [P, 2, 4], F32)
        row_fac, _ = place("row_fac", [P, 2, 4], F32)
        stats, _ = place("stats", [P, BATCH, 6], F32)
        mean_var, _ = place("mean_var", [P, BATCH, 2], F32)
        var_eps, _ = place("var_eps", [P, BATCH], F32)
        rstd, _ = place("rstd", [P, BATCH], F32)
        neg_mean, _ = place("neg_mean", [P, BATCH], F32)
        nmr, _ = place("nmr", [P, BATCH], F32)
        ms_a, _ = place("ms_a", [P, BATCH], F32)
        ms_b, _ = place("ms_b", [P, BATCH], F32)
        ms_eps, _ = place("ms_eps", [P, BATCH], F32)
        rms, _ = place("rms", [P, BATCH], F32)
        minus_half, _ = place("minus_half", [P, BATCH], F32)
        t_stats, _ = place("t_stats", [P, 3, BATCH, 6], F32)
        t_mv, _ = place("t_mv", [P, 3, BATCH, 2], F32)
        t_ve, _ = place("t_ve", [P, 3, BATCH], F32)
        t_rstd, _ = place("t_rstd", [P, 3, BATCH], F32)
        t_nmr, _ = place("t_nmr", [P, 3, BATCH], F32)
        uw, _ = place("uw", [P, NC + 1], F32)
        r_col, _ = place("r_col", [P, 2, BATCH], F32)
        bqk, _ = place("bqk", [P, 2, NC], F32)
        bqk_mul, _ = place("bqk_mul", [P, NC], F32)
        bqk_sum, _ = place("bqk_sum", [P, 1], F32)
        act_i, _ = place("act_i", [1, ACTIVE], I32)
        act_f, _ = place("act_f", [1, 3, ACTIVE], F32)
        targets, _ = place("targets", [1, ZL], F32)
        iota_r, _ = place("iota_r", [1, RANK], I32)
        iota_p, _ = place("iota_p", [P, 1], I32)
        iota_rf, _ = place("iota_rf", [1, RANK], F32)
        iota_pf, _ = place("iota_pf", [P, 1], F32)
        select, _ = place("select", [P, ZL], F32)
        rb_sb, _ = place("rb_sb", [EXPERTS, 2], F32)
        logit_bias, _ = place("logit_bias", [P, 3, ACTIVE], F32)
        logits, _ = place("logits", [P, BATCH, ACTIVE], F32)
        l_max, _ = place("l_max", [P, BATCH, 2], F32)
        l_exp, _ = place("l_exp", [P, BATCH, ACTIVE], F32)
        l_sum, _ = place("l_sum", [P, BATCH, 2], F32)
        alpha, _ = place("alpha", [P, BATCH, ACTIVE], F32)
        z_mix, _ = place("z_mix", [P, 2, ACTIVE * RANK + 1], F32)
        b_max, _ = place("b_max", [P, BATCH, 2], F32)
        b_sum, _ = place("b_sum", [P, BATCH, 2], F32)
        x_sum, _ = place("x_sum", [P, BATCH], F32)
        prior_eps, _ = place("prior_eps", [P, 1], F32)

        raw_ct = [place(f"raw_ct{n}", [P, NC, HALF], F32, at=at_wo[n])[0] for n in range(2)]
        mask_raw, _ = place("mask_raw", [P, BATCH, P], U8, at=at_scores[0])
        ln_w_rows, _ = place("ln_w_rows", [P, D], F32, at=at_att_hi)
        rms_in = [place(f"rms_in{n}", [P, D], F32, at=(*at_probs, at_scores[1])[n])[0] for n in range(3)]

        wk1_raw, _ = place("wk1_raw", [P, NC, D], F32, at=at_raw)
        wq1_raw, _ = place("wq1_raw", [P, NC, D], F32, at=at_raw + 8192)
        wk1_hi, _ = place("wk1_hi", [P, NC, D], F32R, at=at_wv[0])
        wk1_lo, _ = place("wk1_lo", [P, NC, D], F32R, at=at_wo[0])
        wq1_hi, _ = place("wq1_hi", [P, NC, D], F32R, at=at_wq)
        wq1_lo, _ = place("wq1_lo", [P, NC, D], F32R, at=at_wq + 8192)
        mm_hi, _ = place("mm_hi", [P, NC, D], F32R, at=at_raw)
        mm_lo, _ = place("mm_lo", [P, NC, D], F32R, at=at_raw + 8192)
        gg, _ = place("gg", [P, NC, TOK], F32, at=at_xt_hi)
        base_hi, _ = place("base_hi", [P, NC, D], F32R, at=at_xt_lo)
        base_lo, _ = place("base_lo", [P, NC, D], F32R, at=at_xt_lo + 8192)
        base_raw, _ = place("base_raw", [P, NC, D], F32, at=at_qkv[0])
        lora_a_sb, _ = place("lora_a_sb", [P, D], F32, at=at_wv[1])
        lora_b_sb, _ = place("lora_b_sb", [P, D], F32, at=at_wv[1] + 2048)
        router_sb, _ = place("router_sb", [EXPERTS, D], F32, at=at_wv[1] + 4096)
        rb_cols, _ = place("rb_cols", [EXPERTS, 2, P], F32, at=at_wv[1] + 6144)
        r_junk, _ = place("r_junk", [P, D], F32, at=at_qkv[0] + 8192)
        r_diag = [place(f"r_diag{n}", [P, P], F32, at=at_qkv[0] + 8192 + 2048 + 512 * n)[0] for n in range(2)]
        ctx_sb, _ = place("ctx_sb", [P, BATCH, D], F32, at=at_wv[0])
        codes, _ = place("codes", [P, NC, D], F32R, at=at_wq)
        packed, _ = place("packed", [P, 3, D], I32, at=at_wq + 8192)
        unpack, _ = place("unpack", [P, D], I32, at=at_wq + 8192 + 6144)
        zero_rows, _ = place("zero_rows", [P, D], F32, at=at_ct_lo)
        shift_rows, _ = place("shift_rows", [P, D], F32, at=at_ct_lo + 14336)
        scale_rows, _ = place("scale_rows", [P, D], F32, at=at_ct_lo + 2048)
        bias_rows, _ = place("bias_rows", [P, D], F32, at=at_ct_lo + 4096)
        f_scr = [place(f"f_scr{n}", [P, D], F32, at=at_ct_lo + 6144 + 2048 * n)[0] for n in range(4)]
        a_hi, _ = place("a_hi", [P, NC, P], F32R, at=at_qkv[1])
        a_lo, _ = place("a_lo", [P, NC, P], F32R, at=at_qkv[1] + 2048)
        a_full, _ = place("a_full", [P, NC, P], F32, at=at_qkv[1] + 4096)
        b_full, _ = place("b_full", [P, NC, P], F32, at=at_qkv[1] + 6144)
        c_hi, _ = place("c_hi", [P, NC, P], F32R, at=at_qkv[1] + 8192)
        c_lo, _ = place("c_lo", [P, NC, P], F32R, at=at_qkv[1] + 10240)
        b_probs, _ = place("b_probs", [P, P], F32, at=at_scores[0])
        b_probs_t, _ = place("b_probs_t", [P, P], F32, at=at_scores[0] + 512)
        z_mix_t, _ = place("z_mix_t", [ACTIVE * RANK + 1, P], F32, at=at_scores[0] + 1024)
        c_shift_sb, _ = place("c_shift_sb", [P, D], F32, at=at_scores[1])

        def bank(name):
            return stack.enter_context(nc.psum_tensor(name, [P, D], F32))

        ps_s, ps_t, ps_pv, ps_q, ps_k, ps_v = (bank(f"ps_{n}") for n in "s t pv q k v".split())
        ps_o = [bank("ps_o0"), bank("ps_o1")]

        def blocks(t):
            return t[:].rearrange("p (n c) -> p n c", c=P)

        x_banks = (*ps_o, ps_pv, ps_t)
        g_banks = (ps_q, ps_k, ps_v, ps_t, ps_pv, ps_o[1], ps_pv, ps_o[1])

        def sem(name):
            return stack.enter_context(nc.semaphore(name))

        ct_in = [sem(f"ct_in{n}") for n in range(NC + 1)]
        x_in = [sem(f"x_in{n}") for n in range(2)]
        wq_in, wk_in, wv_in, wo_in = sem("wq_in"), sem("wk_in"), sem("wv_in"), sem("wo_in")
        wk0_in = sem("wk0_in")
        wv0_lo_s = sem("wv0_lo_s")
        bias_in = [sem("bias_in0"), sem("bias_in1")]
        mask_in, ln_in = sem("mask_in"), sem("ln_in")
        const_done, ident_zero, ident_done, mask_done = sem("const_done"), sem("ident_zero"), sem("ident_done"), sem("mask_done")
        ct_hi_done, ct_lo_done = sem("ct_hi_done"), sem("ct_lo_done")
        x_stats, x_mean = sem("x_stats"), sem("x_mean")
        x_chain, x_ve, x_rstd, x_ms, x_rms = sem("x_chain"), sem("x_ve"), sem("x_rstd"), sem("x_ms"), sem("x_rms")
        x_neg, x_nmr = sem("x_neg"), sem("x_nmr")
        x_normed, x_resid, x_h, x_t, x_hi, x_lo = (sem(n) for n in ("x_normed", "x_resid", "x_h", "x_t", "x_hi", "x_lo"))
        wq_hi_s, wq_lo_s, wk_hi_s, wk_lo_s = (sem(n) for n in ("wq_hi_s", "wq_lo_s", "wk_hi_s", "wk_lo_s"))
        wv_hi_s, wv_lo_s, wo_hi_s, wo_lo_s = (sem(n) for n in ("wv_hi_s", "wv_lo_s", "wo_hi_s", "wo_lo_s"))
        q_done, k_done, v_done, q_out, k_out, v_out = (sem(n) for n in ("q_done", "k_done", "v_done", "q_out", "k_out", "v_out"))
        s_done, s_shifted, s_max, s_neg, e_done, s_inv, s_fac, p_done = (
            sem(n) for n in ("s_done", "s_shifted", "s_max", "s_neg", "e_done", "s_inv", "s_fac", "p_done"))
        shift_done, pt_done, pt_out, pv_done, att_hi_s, att_lo_s, o_done, o_added = (
            sem(n) for n in ("shift_done", "pt_done", "pt_out", "pv_done", "att_hi_s", "att_lo_s", "o_done", "o_added"))
        w1_in = [sem("wk1_in"), sem("wq1_in")]
        w1_hi_s, w1_lo_s = sem("w1_hi_s"), sem("w1_lo_s")
        vec_in, bqk_s, vec_acc, vec_mm, vec_out = (
            sem(n) for n in ("vec_in", "bqk_s", "vec_acc", "vec_mm", "vec_out"))
        mm_done, mm_hi_s, mm_out = sem("mm_done"), sem("mm_hi_s"), sem("mm_out")
        g_done, g_out = sem("g_done"), sem("g_out")
        kb_mm, kb_s, r_sum, r_col_s, r_diag_s = (sem(n) for n in ("kb_mm", "kb_s", "r_sum", "r_col_s", "r_diag_s"))
        base_in, base_hi_s, base_lo_s = sem("base_in"), sem("base_hi_s"), sem("base_lo_s")
        act_in, lora_in, act_chain, iota_s, tgt_mm, sel_s, rbc_s = (
            sem(n) for n in ("act_in", "lora_in", "act_chain", "iota_s", "tgt_mm", "sel_s", "rbc_s"))
        lr_mm, lr_out, lb_mm, lb_out, lbias = (sem(n) for n in ("lr_mm", "lr_out", "lb_mm", "lb_out", "lbias"))
        ctx_in, packed_in, rows_in, shift_s, unp, codes_s = (
            sem(n) for n in ("ctx_in", "packed_in", "rows_in", "shift_s", "unp", "codes_s"))
        n_st = [sem(f"n_st{k}") for k in range(3)]
        n_mv = [sem(f"n_mv{k}") for k in range(3)]
        n_ve = [sem(f"n_ve{k}") for k in range(3)]
        n_rs = [sem(f"n_rs{k}") for k in range(3)]
        n_nmr = [sem("n_nmr0"), None, sem("n_nmr2")]
        n_xn = [sem(f"n_xn{k}") for k in range(3)]
        n_t = [sem(f"n_t{k}") for k in range(3)]
        a_full_s, a_hi_s, a_lo_s, z_mm, y_mm, zt_mm, zt_out, a_add = (
            sem(n) for n in ("a_full_s", "a_hi_s", "a_lo_s", "z_mm", "y_mm", "zt_mm", "zt_out", "a_add"))
        lg_c, lg_exp, z_mixed = sem("lg_c"), sem("lg_exp"), sem("z_mixed")
        b_full_s, bs_mm, b_c, b_exp, bt_mm, bt_out, at_mm, b_inv, b_add = (
            sem(n) for n in ("b_full_s", "bs_mm", "b_c", "b_exp", "bt_mm", "bt_out", "at_mm", "b_inv", "b_add"))
        c_hi_s, c_lo_s, c_mm, c_bias, c_shift, c_rest_s, c_scaled, c_add = (
            sem(n) for n in ("c_hi_s", "c_lo_s", "c_mm", "c_bias", "c_shift", "c_rest_s", "c_scaled", "c_add"))
        stored = sem("stored")

        block = stack.enter_context(nc.Block())

        def three(pe, dst, hi_l, lo_l, hi_r, lo_r, first, last):
            pe.matmul(dst, hi_l, hi_r, start=first, stop=False)
            pe.matmul(dst, hi_l, lo_r, start=False, stop=False)
            return pe.matmul(dst, lo_l, hi_r, start=False, stop=last)

        @block.sync
        def _(sp):
            def by_batch(t):
                return t.rearrange("(b p) d -> p b d", p=P)

            sp.dma_start(raw_k[:, 0].rearrange("p c d -> p (c d)"), w_k[0, :, 0:D]).then_inc(wk0_in, 16)
            for c in range(NC):
                sp.dma_start(raw_ct[0][:, c, :], ctx_t[:, c, 0:HALF]).then_inc(ct_in[c], 16)
            sp.dma_start(raw_k[:, 1].rearrange("p c d -> p (c d)"), w_k[0, :, D:2 * D]).then_inc(wk_in, 16)
            sp.dma_start(acc[:, 0:4, :], by_batch(x)[:, 0:4, :]).then_inc(x_in[0], 16)
            sp.dma_start(raw_v[:].rearrange("p c d -> p (c d)"), w_v[0]).then_inc(wv_in, 16)
            sp.dma_start(raw_ct[1][:], ctx_t[:, :, HALF:TOK]).then_inc(ct_in[NC], 16)
            sp.dma_start(ln_w_rows[:], ln_w.broadcast_to([P, D])).then_inc(ln_in, 16)
            sp.dma_start(acc[:, 4:8, :], by_batch(x)[:, 4:8, :]).then_inc(x_in[1], 16)
            sp.dma_start(raw_q[:].rearrange("p h c d -> p (h c d)"), w_q[0]).then_inc(wq_in, 16)
            sp.dma_start(mask_raw[:], mask).then_inc(mask_in, 16)
            sp.dma_start(bias_sb[:, 0], bias[0]).then_inc(bias_in[0], 16)
            sp.dma_start(raw_o[:].rearrange("p h d -> p (h d)"), w_o[0]).then_inc(wo_in, 16)
            sp.dma_start(act_i[:], active).then_inc(act_in, 16)
            sp.dma_start(rb_sb[:, 0:1], router_b).then_inc(act_in, 16)
            sp.dma_start(rb_sb[:, 1:2], prior).then_inc(act_in, 16)
            sp.dma_start(low_rank_out[ACTIVE * RANK:ACTIVE * RANK + 1, :], b_base).then_inc(act_in, 16)
            sp.dma_start(bqk[:, 0, :], bq1).then_inc(vec_in, 16)
            sp.dma_start(bqk[:, 1, :], bk1).then_inc(vec_in, 16)
            sp.wait_ge(wv_lo_s, 1)
            sp.wait_ge(wv0_lo_s, 1)
            sp.dma_start(raw_v[:].rearrange("p c d -> p (c d)"), w_v[1]).then_inc(wv_in, 16)

            def load_group(g, more, parity):
                sp.wait_ge(wq_lo_s, 2 * g)
                sp.dma_start(raw_q[:].rearrange("p h c d -> p (h c d)"), w_q[g]).then_inc(wq_in, 16)
                sp.wait_ge(wk_lo_s, 2 * g)
                sp.dma_start(raw_k[:].rearrange("p h c d -> p (h c d)"), w_k[g]).then_inc(wk_in, 16)
                wait_from(sp, shift_done, 4 * g - 4)
                sp.dma_start(bias_sb[:, parity], bias[g]).then_inc(bias_in[parity], 16)
                sp.wait_ge(wo_lo_s, g)
                sp.dma_start(raw_o[:].rearrange("p h d -> p (h d)"), w_o[g]).then_inc(wo_in, 16)
                if more:
                    sp.wait_ge(wv_lo_s, g + 1)
                    sp.dma_start(raw_v[:].rearrange("p c d -> p (c d)"), w_v[g + 1]).then_inc(wv_in, 16)

            load_group(1, True, 1)
            with sp.Fori(1, TURNS - 1) as i:
                load_group(2 * i, True, 0)
                load_group(2 * i + 1, True, 1)
            load_group(GROUPS - 2, True, 0)
            load_group(GROUPS - 1, False, 1)

            sp.wait_ge(wq_lo_s, 2 * GROUPS)
            sp.wait_ge(wk_lo_s, 2 * GROUPS)
            sp.dma_start(wk1_raw[:], wk1).then_inc(w1_in[0], 16)
            sp.wait_ge(wv_lo_s, GROUPS)
            sp.wait_ge(wo_lo_s, GROUPS)
            sp.dma_start(wq1_raw[:], wq1).then_inc(w1_in[1], 16)
            sp.wait_ge(v_done, STEPS)
            sp.dma_start(lora_a_sb[:], lora_a).then_inc(lora_in, 16)
            sp.dma_start(lora_b_sb[:], lora_b).then_inc(lora_in, 16)
            sp.dma_start(router_sb[:], router_w).then_inc(lora_in, 16)
            sp.wait_ge(pv_done, STEPS - 2)
            sp.dma_start(base_raw[:], w_base).then_inc(base_in, 16)
            sp.wait_ge(mm_done, NC)
            sp.dma_start(ctx_sb[:], ctx_nat.rearrange("(b p) d -> p b d", p=P)).then_inc(ctx_in, 16)
            sp.dma_start(packed[:], qweight).then_inc(packed_in, 16)
            sp.wait_ge(g_done, 2 * NC)
            sp.dma_start(zero_rows[:], w_zero.broadcast_to([P, D])).then_inc(rows_in, 16)
            sp.dma_start(scale_rows[:], w_scale.broadcast_to([P, D])).then_inc(rows_in, 16)
            sp.dma_start(bias_rows[:], ffn_bias.broadcast_to([P, D])).then_inc(rows_in, 16)
            for b in range(BATCH):
                sp.wait_ge(c_add, b + 1)
                sp.dma_start(out[b * P:(b + 1) * P, :], acc[:, b, :]).then_inc(stored, 16)
            sp.wait_ge(stored, 16 * BATCH)

        @block.scalar
        def _(act):
            def split_ct(half, c):
                act.wait_ge(ct_in[NC if half else c], 16)
                act.copy(ct_hi[:, c, half * HALF:(half + 1) * HALF], raw_ct[half][:, c, :]).then_inc(ct_hi_done, 1)

            def split_qk(g, head):
                wait_from(act, wq_in, 16 * (g + 1))
                wait_from(act, q_done, 4 * g - 1 + head)
                act.copy(wq_hi[:, head], raw_q[:, head]).then_inc(wq_hi_s, 1)
                wait_from(act, wk_in, 16 * (g + 1))
                wait_from(act, k_done, 4 * g - 1 + head)
                act.copy(wk_hi[:, head], raw_k[:, head]).then_inc(wk_hi_s, 1)

            def split_v(g, n):
                wait_from(act, wv_in, 16 * (g + 1))
                wait_from(act, v_done, 4 * g - 4)
                act.copy(wv_hi[n][:], raw_v[:]).then_inc(wv_hi_s, 1)

            def split_o(g, n):
                wait_from(act, wo_in, 16 * (g + 1))
                wait_from(act, o_done, 8 * g - 8)
                act.copy(wo_hi[n][:], raw_o[:]).then_inc(wo_hi_s, 1)

            def k_evac(t, n, part, bank=ps_k):
                wait_from(act, k_done, t + 1)
                act.copy(kt[n][:, part, :], bank[:]).then_inc(k_out, 1)

            def q_evac(t, n, part, bank=ps_q):
                wait_from(act, q_done, t + 1)
                act.copy(qt[n][:, part, :], bank[:]).then_inc(q_out, 1)

            def x_high(b):
                act.wait_ge(x_t, b + 1)
                act.copy(xt_hi[:, :, b * P:(b + 1) * P], blocks(x_banks[b % 4])).then_inc(x_hi, 1)

            def x_norm(b):
                act.wait_ge(x_nmr, b // 4 + 1)
                if b > 2:
                    act.wait_ge(x_resid, b - 2)
                    act.wait_ge(x_h, b - 2)
                act.activation(normed[:, b % 3, :], acc[:, b, :], ACT.Identity, bias=nmr[:, b:b + 1],
                               scale=rstd[:, b:b + 1]).then_inc(x_normed, 1)

            act.wait_ge(wk0_in, 16)
            act.copy(wk_hi[:, 0], raw_k[:, 0]).then_inc(wk_hi_s, 1)
            for c in range(NC):
                split_ct(0, c)
            act.wait_ge(wk_in, 16)
            act.copy(wk_hi[:, 1], raw_k[:, 1]).then_inc(wk_hi_s, 1)
            k_evac(0, 0, 0)
            split_v(0, 0)
            k_evac(1, 0, 1, ps_q)
            for c in range(NC):
                split_ct(1, c)
            x_norm(0)
            x_norm(1)
            x_norm(2)
            act.wait_ge(wq_in, 16)
            act.copy(wq_hi[:, 0], raw_q[:, 0]).then_inc(wq_hi_s, 1)
            x_high(0)
            x_norm(3)
            x_high(1)
            act.copy(wq_hi[:, 1], raw_q[:, 1]).then_inc(wq_hi_s, 1)
            k_evac(2, 1, 0)
            x_norm(4)
            x_high(2)
            x_norm(5)
            x_high(3)
            k_evac(3, 1, 1)
            x_norm(6)
            x_high(4)
            x_norm(7)
            x_high(5)
            q_evac(0, 0, 0)
            x_high(6)
            q_evac(1, 0, 1, ps_k)
            x_high(7)
            act.wait_ge(ct_lo_done, NC)
            split_o(0, 0)
            split_v(1, 1)

            def attention_high(s):
                wait_from(act, pv_done, s + 1)
                act.copy(att_hi[:], blocks(ps_pv)).then_inc(att_hi_s, 1)

            def exponentials(s, n):
                act.wait_ge(s_neg, s + 1)
                wait_from(act, pt_done, s - 1)
                for m in range(4):
                    e = act.activation(probs[n][:, m, :], scores[n][:, m, :], ACT.Exp,
                                       bias=neg_max[:, n, m:m + 1], accum_out=row_sum[:, n, m:m + 1])
                e.then_inc(e_done, 1)

            def pt_evac(s):
                act.wait_ge(pt_done, s + 1)
                act.copy(probs_t[:], blocks(ps_t)).then_inc(pt_out, 1)

            def step(i, c):
                s = LOOP_STEPS * i + c
                g = 2 * i + c // 4
                n = c % 2
                if c > 0 or not isinstance(i, int) or i > 0:
                    attention_high(s - 1)
                exponentials(s, n)
                q_evac(s + 2, (c // 2 + 1) % 2, n)
                if not isinstance(i, int) or s > 1:
                    k_evac(s + 2, (c // 2 + 1) % 2, n)
                pt_evac(s)
                last = isinstance(i, int) and i == TURNS - 1
                if c % 4 < 2 and not (last and c >= 4):
                    split_qk(g + 1, c % 4)
                if c % 4 == 2 and not (last and c >= 4):
                    split_o(g + 1, (c // 4 + 1) % 2)
                if c % 4 == 3 and not last:
                    split_v(g + 2, (c // 4) % 2)

            for c in range(LOOP_STEPS):
                step(0, c)
            with act.Fori(1, TURNS - 1) as i:
                for c in range(LOOP_STEPS):
                    step(i, c)
            for c in range(LOOP_STEPS - 4):
                step(TURNS - 1, c)
            step(TURNS - 1, 4)
            act.wait_ge(w1_in[0], 16)
            act.wait_ge(v_done, 4 * (GROUPS - 1))
            for c in range(NC):
                act.copy(wk1_hi[:, c, :], wk1_raw[:, c, :]).then_inc(w1_hi_s, 1)
            attention_high(STEPS - 4)
            exponentials(STEPS - 3, 1)
            q_evac(STEPS - 1, 1, 1)
            act.wait_ge(w1_in[1], 16)
            for c in range(NC):
                act.copy(wq1_hi[:, c, :], wq1_raw[:, c, :]).then_inc(w1_hi_s, 1)
            k_evac(STEPS - 1, 1, 1)
            pt_evac(STEPS - 3)
            attention_high(STEPS - 3)

            def mm_high(m):
                act.wait_ge(mm_done, m + 1)
                if m == 0:
                    act.wait_ge(w1_lo_s, 2 * NC)
                    act.wait_ge(vec_mm, 1)
                act.copy(mm_hi[:, m, :], (ps_q, ps_k)[m % 2][:]).then_inc(mm_hi_s, 1)

            exponentials(STEPS - 2, 0)
            mm_high(0)
            mm_high(1)
            act.wait_ge(kb_mm, 1)
            act.copy(normed[:, 2, :], ps_v[:]).then_inc(kb_s, 1)
            pt_evac(STEPS - 2)
            mm_high(2)
            attention_high(STEPS - 2)
            act.wait_ge(lr_mm, 1)
            act.activation(logit_bias[:, 0, :], ps_v[:, 148:152], ACT.Ln, bias=prior_eps[:, 0:1]).then_inc(lbias, 1)
            mm_high(3)
            exponentials(STEPS - 1, 1)
            act.wait_ge(base_in, 16)
            for c in range(NC):
                act.copy(base_hi[:, c, :], base_raw[:, c, :]).then_inc(base_hi_s, 1)
            pt_evac(STEPS - 1)
            attention_high(STEPS - 1)

            def code(v):
                act.wait_ge(unp, v + 1)
                act.copy(codes[:, v, :], unpack[:]).then_inc(codes_s, 1)

            def stage_a(b):
                act.wait_ge(n_t[0], b + 1)
                wait_from(act, z_mm, b)
                act.copy(a_full[:], blocks(ps_s)).then_inc(a_full_s, 1)
                wait_from(act, y_mm, b)
                act.copy(a_hi[:], blocks(ps_s)).then_inc(a_hi_s, 1)

            def stage_a_exp(b):
                act.wait_ge(lg_c, 3 * b + 3)
                act.activation(l_exp[:, b, :], logits[:, b, :], ACT.Exp, bias=l_max[:, b, 1:2],
                               accum_out=l_sum[:, b, 0:1]).then_inc(lg_exp, 1)

            def stage_a_zt(b):
                act.wait_ge(zt_mm, b + 1)
                wait_from(act, y_mm, b)
                act.copy(z_mix_t[:], ps_k[0:ACTIVE * RANK + 1, P:2 * P]).then_inc(zt_out, 1)

            def stage_b(b):
                act.wait_ge(n_t[1], b + 1)
                wait_from(act, bs_mm, b)
                act.copy(b_full[:], blocks(ps_t)).then_inc(b_full_s, 1)

            def stage_b_exp(b):
                act.wait_ge(b_c, 2 * b + 2)
                wait_from(act, bt_mm, b)
                act.activation(b_probs[:], ps_v[:, 0:P], ACT.Exp, bias=b_max[:, b, 1:2], scale=SCORE_SCALE,
                               accum_out=b_sum[:, b, 0:1]).then_inc(b_exp, 1)

            def stage_b_pt(b):
                act.wait_ge(bt_mm, b + 1)
                wait_from(act, at_mm, b)
                act.copy(b_probs_t[:], ps_v[:, 2 * P:3 * P]).then_inc(bt_out, 1)

            def normalise_end(stage, b):
                act.wait_ge(n_nmr[stage], b + 1)
                wait_from(act, n_t[stage], b)
                if stage == 2 and b == 0:
                    act.wait_ge(r_sum, BATCH)
                act.activation(normed[:, stage, :], acc[:, b, :], ACT.Identity, bias=t_nmr[:, stage, b:b + 1],
                               scale=t_rstd[:, stage, b:b + 1],
                               accum_out=x_sum[:, b:b + 1] if stage == 2 else None).then_inc(n_xn[stage], 1)

            def stage_c_shift(b):
                act.wait_ge(shift_s, 1)
                act.wait_ge(n_xn[2], b + 1)
                wait_from(act, c_rest_s, b)
                act.mul(c_shift_sb[:], shift_rows[:], x_sum[:, b:b + 1]).then_inc(c_shift, 1)

            def stage_c(b):
                act.wait_ge(n_t[2], b + 1)
                wait_from(act, c_mm, b)
                act.copy(c_hi[:], blocks(ps_pv)).then_inc(c_hi_s, 1)

            normalise_end(0, 0)
            for w in range(BATCH + 3):
                a, b, b_end, c = w, w - 1, w - 2, w - 3
                if a < BATCH:
                    stage_a(a)
                if c >= 0:
                    stage_c_shift(c)
                if 0 <= b < BATCH:
                    stage_b(b)
                if a < BATCH:
                    stage_a_exp(a)
                if w < 2:
                    code(2 * w)
                if w == BATCH:
                    stage_b_exp(b)
                if 0 <= b_end < BATCH:
                    normalise_end(2, b_end)
                if 0 <= b < BATCH and w != BATCH:
                    stage_b_exp(b)
                if a < BATCH:
                    stage_a_zt(a)
                if a + 1 < BATCH:
                    normalise_end(0, a + 1)
                if 0 <= b < BATCH:
                    stage_b_pt(b)
                if 0 <= b_end < BATCH:
                    stage_c(b_end)
                if w < 2:
                    code(2 * w + 1)

        @block.gpsimd
        def _(pool):
            pool.memset(ident[:], 0.0).then_inc(ident_zero, 1)
            pool.memset(ones[:], 1.0).then_inc(const_done, 1)
            pool.memset(minus_half[:], -0.5).then_inc(const_done, 1)
            pool.memset(prior_eps[:], PRIOR_EPS).then_inc(const_done, 1)
            pool.memset(z_mix[:, :, ACTIVE * RANK:ACTIVE * RANK + 1], 1.0).then_inc(const_done, 1)
            pool.iota(iota_r[:], pattern=[[1, RANK]], base=0, channel_multiplier=0).then_inc(iota_s, 1)
            pool.iota(iota_p[:], pattern=[[1, 1]], base=0, channel_multiplier=1).then_inc(iota_s, 1)
            pool.wait_ge(ident_zero, 1)
            pool.affine_select(out=ident[:], in_=ident[:], compare_op=ALU.not_equal, fill=1.0, base=0,
                               pattern=[[-1, P]], channel_multiplier=1).then_inc(ident_done, 1)

            def rest_qk(head, g):
                wait_from(pool, wq_hi_s, 2 * g + head + 1)
                pool.tensor_tensor(wq_lo[:, head], raw_q[:, head], wq_hi[:, head].bitcast(F32),
                                   ALU.subtract).then_inc(wq_lo_s, 1)
                wait_from(pool, wk_hi_s, 2 * g + head + 1)
                pool.tensor_tensor(wk_lo[:, head], raw_k[:, head], wk_hi[:, head].bitcast(F32),
                                   ALU.subtract).then_inc(wk_lo_s, 1)

            def rest_v(g, n):
                wait_from(pool, wv_hi_s, g + 1)
                pool.tensor_tensor(wv_lo[n][:], raw_v[:], wv_hi[n][:].bitcast(F32), ALU.subtract).then_inc(wv_lo_s, 1)

            def rest_o(g, n):
                wait_from(pool, wo_hi_s, g + 1)
                pool.tensor_tensor(wo_lo[n][:], raw_o[:], wo_hi[n][:].bitcast(F32), ALU.subtract).then_inc(wo_lo_s, 1)

            def make_shift(s, c):
                n = c % 2
                first = 4 * (c // 2 % 2) + 2 * n
                wait_from(pool, s_shifted, s - 1)
                bias_b = bias_sb[:, c // 4 % 2].unsqueeze(1).broadcast_to([P, 2, 2, P])
                mask_b = mask_sb[:, first:first + 2, :].unsqueeze(2).broadcast_to([P, 2, 2, P])
                pool.tensor_tensor(shift[n][:].rearrange("p (b h) k -> p b h k", b=2), bias_b, mask_b,
                                   ALU.add).then_inc(shift_done, 1)

            def x_scale(half):
                cols = slice(4 * half, 4 * half + 4)
                pool.wait_ge(x_ve, half + 1)
                pool.tensor_tensor(rstd[:, cols], var_eps[:, cols], minus_half[:, 0:4], ALU.pow).then_inc(x_rstd, 1)
                pool.wait_ge(x_neg, half + 1)
                pool.wait_ge(x_rstd, half + 1)
                pool.tensor_tensor(nmr[:, cols], neg_mean[:, cols], rstd[:, cols], ALU.mult).then_inc(x_nmr, 1)

            def x_scale_rms(half):
                cols = slice(4 * half, 4 * half + 4)
                pool.wait_ge(x_ms, half + 1)
                pool.tensor_tensor(rms[:, cols], ms_eps[:, cols], minus_half[:, 0:4], ALU.pow).then_inc(x_rms, 1)

            def x_residual(b):
                pool.wait_ge(x_normed, b + 1)
                pool.tensor_tensor(acc[:, b, :], acc[:, b, :], normed[:, b % 3, :], ALU.add).then_inc(x_resid, 1)

            pool.wait_ge(const_done, 2)
            pool.wait_ge(wv_hi_s, 1)
            pool.tensor_tensor(wv_lo[0][:, 0:2], raw_v[:, 0:2], wv_hi[0][:, 0:2].bitcast(F32),
                               ALU.subtract).then_inc(wv_lo_s, 1)
            def rest_q(head):
                pool.wait_ge(wq_hi_s, head + 1)
                pool.tensor_tensor(wq_lo[:, head], raw_q[:, head], wq_hi[:, head].bitcast(F32),
                                   ALU.subtract).then_inc(wq_lo_s, 1)

            x_scale(0)
            x_scale_rms(0)
            x_residual(0)
            x_residual(1)
            rest_q(0)
            x_scale(1)
            x_residual(2)
            x_scale_rms(1)
            x_residual(3)
            rest_q(1)
            x_residual(4)
            pool.wait_ge(mask_done, 1)
            pool.wait_ge(bias_in[0], 16)
            make_shift(0, 0)
            for b in range(5, BATCH):
                x_residual(b)
            rest_o(0, 0)
            rest_v(1, 1)

            def step(i, c):
                s = LOOP_STEPS * i + c
                g = 2 * i + c // 4
                last = isinstance(i, int) and i == TURNS - 1
                if not (last and c == LOOP_STEPS - 1):
                    if c == 3:
                        pool.wait_ge(bias_in[1], 16 * (i + 1))
                    if c == 7:
                        pool.wait_ge(bias_in[0], 16 * (i + 2))
                    make_shift(s + 1, (c + 1) % LOOP_STEPS)
                if c % 4 < 2 and not (last and c >= 4):
                    rest_qk(c % 4, g + 1)
                if c % 4 == 2 and not (last and c >= 4):
                    rest_o(g + 1, (c // 4 + 1) % 2)
                if c % 4 == 3 and not last:
                    rest_v(g + 2, (c // 4) % 2)

            for c in range(LOOP_STEPS):
                step(0, c)
            with pool.Fori(1, TURNS - 1) as i:
                for c in range(LOOP_STEPS):
                    step(i, c)
            for c in range(LOOP_STEPS):
                step(TURNS - 1, c)
            for c in range(NC):
                pool.wait_ge(base_hi_s, c + 1)
                pool.tensor_tensor(base_lo[:, c, :], base_raw[:, c, :], base_hi[:, c, :].bitcast(F32),
                                   ALU.subtract).then_inc(base_lo_s, 1)

            def inv_std(stage, b):
                pool.wait_ge(n_mv[stage], b + 1)
                pool.tensor_scalar(t_ve[:, stage, b:b + 1], t_mv[:, stage, b, 1:2], EPS, None,
                                   ALU.add).then_inc(n_ve[stage], 1)
                pool.wait_ge(n_ve[stage], b + 1)
                pool.tensor_tensor(t_rstd[:, stage, b:b + 1], t_ve[:, stage, b:b + 1], minus_half[:, 0:1],
                                   ALU.pow).then_inc(n_rs[stage], 1)
                if stage != 1:
                    pool.wait_ge(n_rs[stage], b + 1)
                    pool.tensor_scalar(t_nmr[:, stage, b:b + 1], t_mv[:, stage, b, 0:1], t_rstd[:, stage, b:b + 1], -1.0,
                                       ALU.mult, ALU.mult).then_inc(n_nmr[stage], 1)

            def r_diagonal(b):
                pool.wait_ge(r_col_s, 1)
                wait_from(pool, bs_mm, b - 1)
                pool.tensor_scalar(r_diag[b % 2][:], ident[:], r_col[:, 1, b:b + 1], None, ALU.mult).then_inc(r_diag_s, 1)

            inv_std(0, 0)
            for w in range(BATCH + 3):
                b, b_end, c = w - 1, w - 2, w - 3
                if 0 <= b < BATCH:
                    inv_std(1, b)
                if c >= 1:
                    pool.wait_ge(c_scaled, c)
                    pool.wait_ge(c_rest_s, c)
                    pool.tensor_tensor(acc[:, c - 1, :], f_scr[3 - c % 2][:], f_scr[1 - c % 2][:],
                                       ALU.add).then_inc(c_add, 1)
                if w < BATCH:
                    r_diagonal(w)
                if 0 <= b_end < BATCH:
                    if b_end == 0:
                        pool.wait_ge(rows_in, 48)
                    inv_std(2, b_end)
                if w + 1 < BATCH:
                    inv_std(0, w + 1)
                if 0 <= b_end < BATCH:
                    wait_from(pool, c_add, b_end - 1)
                    pool.tensor_tensor(f_scr[b_end % 2][:], acc[:, b_end, :], bias_rows[:], ALU.add).then_inc(c_bias, 1)
                if c >= 0:
                    pool.wait_ge(c_shift, c + 1)
                    pool.wait_ge(c_bias, c + 1)
                    pool.tensor_tensor(f_scr[c % 2][:], f_scr[c % 2][:], c_shift_sb[:], ALU.add).then_inc(c_rest_s, 1)

        @block.vector
        def _(dve):
            def ct_rest(half, c):
                cols = slice(half * HALF, (half + 1) * HALF)
                dve.wait_ge(ct_hi_done, NC * half + c + 1)
                dve.tensor_tensor(ct_lo[:, c, cols], raw_ct[half][:, c, :], ct_hi[:, c, cols].bitcast(F32),
                                  ALU.subtract).then_inc(ct_lo_done, 1)

            def x_statistics(half):
                dve.wait_ge(x_in[half], 16)
                tiles = range(4 * half, 4 * half + 4)
                for b in tiles:
                    dve.bn_stats(stats[:, b, :], acc[:, b, :]).then_inc(x_stats, 1)
                for b in tiles:
                    dve.wait_ge(x_stats, b + 1)
                    dve.bn_aggr(mean_var[:, b, :], stats[:, b, :]).then_inc(x_mean, 1)
                cols = slice(4 * half, 4 * half + 4)
                dve.wait_ge(x_mean, 4 * half + 4)
                dve.tensor_scalar(var_eps[:, cols], mean_var[:, cols, 1], EPS, None, ALU.add).then_inc(x_ve, 1)
                dve.tensor_scalar(neg_mean[:, cols], mean_var[:, cols, 0], -1.0, None, ALU.mult).then_inc(x_neg, 1)

            def x_mean_square(half):
                cols = slice(4 * half, 4 * half + 4)
                dve.wait_ge(x_rstd, half + 1)
                dve.tensor_tensor(ms_a[:, cols], mean_var[:, cols, 1], rstd[:, cols], ALU.mult).then_inc(x_chain, 1)
                dve.wait_ge(x_chain, 2 * half + 1)
                dve.tensor_tensor(ms_b[:, cols], ms_a[:, cols], rstd[:, cols], ALU.mult).then_inc(x_chain, 1)
                dve.wait_ge(x_chain, 2 * half + 2)
                dve.tensor_scalar(ms_eps[:, cols], ms_b[:, cols], EPS, None, ALU.add).then_inc(x_ms, 1)

            def x_tile(b):
                if b % 4 == 0:
                    dve.wait_ge(x_rms, b // 4 + 1)
                dve.wait_ge(x_normed, b + 1)
                wait_from(dve, x_t, b - 2)
                dve.scalar_tensor_tensor(rms_in[b % 3][:], normed[:, b % 3, :], rms[:, b:b + 1], ln_w_rows[:],
                                         ALU.mult, ALU.mult).then_inc(x_h, 1)

            def x_rest(b):
                dve.wait_ge(x_hi, b + 1)
                cols = slice(b * P, (b + 1) * P)
                dve.tensor_tensor(xt_lo[:, :, cols], blocks(x_banks[b % 4]), xt_hi[:, :, cols].bitcast(F32),
                                  ALU.subtract).then_inc(x_lo, 1)

            def v_evac(t, n, part, bank=ps_v):
                wait_from(dve, v_done, t + 1)
                dve.tensor_copy(vv[n][:, 2 * part:2 * part + 2, :],
                                bank[:].rearrange("p (b c) -> p b c", b=2)).then_inc(v_out, 1)

            def wk_rest(head):
                dve.wait_ge(wk_hi_s, head + 1)
                dve.tensor_tensor(wk_lo[:, head], raw_k[:, head], wk_hi[:, head].bitcast(F32),
                                  ALU.subtract).then_inc(wk_lo_s, 1)

            wk_rest(0)
            for c in range(NC):
                ct_rest(0, c)
            wk_rest(1)
            x_statistics(0)
            dve.wait_ge(wv_hi_s, 1)
            dve.tensor_tensor(wv_lo[0][:, 2:4], raw_v[:, 2:4], wv_hi[0][:, 2:4].bitcast(F32),
                              ALU.subtract).then_inc(wv0_lo_s, 1)
            x_mean_square(0)
            for c in range(NC):
                ct_rest(1, c)
            v_evac(0, 0, 0)
            dve.wait_ge(ln_in, 16)
            x_tile(0)
            x_tile(1)
            x_tile(2)
            x_statistics(1)
            x_tile(3)
            x_rest(0)
            x_mean_square(1)
            v_evac(1, 0, 1, ps_s)
            x_rest(1)
            x_tile(4)
            x_rest(2)
            x_tile(5)
            x_rest(3)
            dve.wait_ge(mask_in, 16)
            dve.tensor_scalar(mask_sb[:], mask_raw[:], 1.0, MASKED, ALU.subtract, ALU.mult).then_inc(mask_done, 1)
            x_tile(6)
            x_rest(4)
            x_tile(7)
            x_rest(5)
            x_rest(6)
            x_rest(7)

            def attention_rest(s):
                wait_from(dve, att_hi_s, s + 1)
                dve.tensor_tensor(att_lo[:], blocks(ps_pv), att_hi[:].bitcast(F32), ALU.subtract).then_inc(att_lo_s, 1)

            def add_output(s, c):
                for j in range(2):
                    b = 4 * (c // 2 % 2) + 2 * (c % 2) + j
                    wait_from(dve, o_done, 2 * s + j + 1)
                    if isinstance(s, int) and s < 4:
                        dve.wait_ge(x_resid, b + 1)
                    else:
                        dve.wait_ge(o_added, 2 * s - 6)
                    dve.tensor_tensor(acc[:, b, :], ps_o[j][:], acc[:, b, :], ALU.add).then_inc(o_added, 1)

            def step(i, c, drain=False):
                s = LOOP_STEPS * i + c
                n = c % 2
                start = isinstance(i, int) and i == 0 and c == 0
                if not start and not drain:
                    attention_rest(s - 1)
                dve.wait_ge(s_done, s + 1)
                dve.wait_ge(shift_done, s + 1)
                wait_from(dve, e_done, s - 1)
                dve.tensor_tensor(scores[n][:], blocks(ps_s), shift[n][:], ALU.add).then_inc(s_shifted, 1)
                dve.wait_ge(s_shifted, s + 1)
                dve.tensor_reduce(row_max[:, n, :], scores[n][:], AX_X, ALU.max).then_inc(s_max, 1)
                dve.wait_ge(s_max, s + 1)
                dve.tensor_scalar(neg_max[:, n, :], row_max[:, n, :], -1.0, None, ALU.mult).then_inc(s_neg, 1)
                if not drain and (not isinstance(i, int) or s > 0):
                    v_evac(s + 1, ((c + 1) // 2) % 2, (c + 1) % 2)
                dve.wait_ge(e_done, s + 1)
                dve.reciprocal(row_inv[:, n, :], row_sum[:, n, :]).then_inc(s_inv, 1)
                dve.wait_ge(s_inv, s + 1)
                dve.scalar_tensor_tensor(row_fac[:, n, :], row_max[:, n, :], -MASKED / 3.0, row_inv[:, n, :],
                                         ALU.is_gt, ALU.mult).then_inc(s_fac, 1)
                dve.wait_ge(s_fac, s + 1)
                dve.tensor_tensor(probs[n][:], probs[n][:], row_fac[:, n, :].unsqueeze(2).broadcast_to([P, 4, P]),
                                  ALU.mult).then_inc(p_done, 1)
                if not start:
                    add_output(s - 1, (c - 1) % LOOP_STEPS)

            for c in range(LOOP_STEPS):
                step(0, c)
            dve.wait_ge(act_in, 64)
            dve.wait_ge(iota_s, 2)
            dve.tensor_copy(act_f[:, 0, :], act_i[:]).then_inc(act_chain, 1)
            dve.tensor_copy(iota_rf[:], iota_r[:]).then_inc(act_chain, 1)
            dve.tensor_copy(iota_pf[:], iota_p[:]).then_inc(act_chain, 1)
            dve.wait_ge(act_chain, 3)
            dve.tensor_scalar(act_f[:, 1, :], act_f[:, 0, :], 0.0, float(EXPERTS), ALU.is_lt, ALU.mult).then_inc(act_chain, 1)
            dve.wait_ge(act_chain, 4)
            dve.tensor_tensor(act_f[:, 2, :], act_f[:, 0, :], act_f[:, 1, :], ALU.add).then_inc(act_chain, 1)
            dve.wait_ge(act_chain, 5)
            dve.tensor_scalar(targets[:, ACTIVE * RANK:ZL], act_f[:, 2, :], 0.0, float(EXPERTS - 1), ALU.max,
                              ALU.min).then_inc(act_chain, 1)
            dve.wait_ge(act_chain, 6)
            for j in range(ACTIVE):
                dve.scalar_tensor_tensor(targets[:, j * RANK:(j + 1) * RANK],
                                         targets[:, ACTIVE * RANK + j:ACTIVE * RANK + j + 1].broadcast_to([1, RANK]),
                                         float(RANK), iota_rf[:], ALU.mult, ALU.add).then_inc(act_chain, 1)
            dve.wait_ge(vec_in, 32)
            dve.tensor_tensor(bqk_mul[:], bqk[:, 0, :], bqk[:, 1, :], ALU.mult).then_inc(bqk_s, 1)
            dve.wait_ge(bqk_s, 1)
            dve.tensor_reduce(bqk_sum[:], bqk_mul[:], AX_X, ALU.add).then_inc(bqk_s, 1)

            with dve.Fori(1, TURNS - 1) as i:
                for c in range(LOOP_STEPS):
                    step(i, c)
            for c in range(5):
                step(TURNS - 1, c)

            def weighted_rows(k, w_raw, vec):
                dve.tensor_scalar(normed[:, k, :], w_raw[:, 0, :], bqk[:, vec, 0:1], None, ALU.mult).then_inc(vec_acc, 1)
                for c in range(1, NC):
                    dve.wait_ge(vec_acc, NC * (1 - k) + c)
                    dve.scalar_tensor_tensor(normed[:, k, :], w_raw[:, c, :], bqk[:, vec, c:c + 1], normed[:, k, :],
                                             ALU.mult, ALU.add).then_inc(vec_acc, 1)

            dve.wait_ge(w1_in[0], 16)
            weighted_rows(1, wk1_raw, 0)
            dve.wait_ge(o_done, 2 * (STEPS - 4))
            for c in range(NC):
                dve.wait_ge(w1_hi_s, c + 1)
                dve.tensor_tensor(wk1_lo[:, c, :], wk1_raw[:, c, :], wk1_hi[:, c, :].bitcast(F32),
                                  ALU.subtract).then_inc(w1_lo_s, 1)
            step(TURNS - 1, 5)
            dve.wait_ge(w1_in[1], 16)
            weighted_rows(0, wq1_raw, 1)
            dve.wait_ge(k_done, STEPS)
            for c in range(NC):
                dve.wait_ge(w1_hi_s, NC + c + 1)
                dve.tensor_tensor(wq1_lo[:, c, :], wq1_raw[:, c, :], wq1_hi[:, c, :].bitcast(F32),
                                  ALU.subtract).then_inc(w1_lo_s, 1)

            def mm_rest(m):
                dve.wait_ge(mm_hi_s, m + 1)
                dve.tensor_tensor(mm_lo[:, m, :], (ps_q, ps_k)[m % 2][:], mm_hi[:, m, :].bitcast(F32),
                                  ALU.subtract).then_inc(mm_out, 1)

            def g_evac(n):
                dve.wait_ge(g_done, n + 1)
                m, half = n % NC, n // NC
                dve.tensor_scalar(gg[:, m, half * HALF:(half + 1) * HALF], g_banks[n][:], uw[:, m:m + 1], None,
                                  ALU.add).then_inc(g_out, 1)

            def r_batch(b):
                if b == 0:
                    dve.wait_ge(ctx_in, 16)
                    dve.wait_ge(kb_s, 1)
                    dve.wait_ge(pv_done, STEPS - 2)
                wait_from(dve, r_sum, b)
                dve.scalar_tensor_tensor(r_junk[:], ctx_sb[:, b, :], 1.0, normed[:, 2, :], ALU.mult, ALU.mult,
                                         accum_out=r_col[:, 0, b:b + 1]).then_inc(r_sum, 1)

            def unpack_code(v):
                word, down = ((0, 0), (0, 6), (1, 0), (2, 0))[v]
                dve.wait_ge(packed_in, 16)
                wait_from(dve, codes_s, v)
                dve.tensor_scalar(unpack[:], packed[:, word, :], down, 63, ALU.logical_shift_right,
                                  ALU.bitwise_and).then_inc(unp, 1)

            v_evac(STEPS - 1, 1, 1)
            attention_rest(STEPS - 3)
            step(TURNS - 1, 6, drain=True)
            dve.wait_ge(vec_mm, 1)
            dve.tensor_copy(uw[:], ps_v[:, 0:NC + 1]).then_inc(vec_out, 1)
            mm_rest(0)
            dve.wait_ge(tgt_mm, 1)
            dve.wait_ge(act_chain, 10)
            dve.tensor_scalar(select[:], ps_v[:, 0:ZL], iota_pf[:, 0:1], None, ALU.is_equal).then_inc(sel_s, 1)
            for n in range(2):
                dve.tensor_scalar(rb_cols[:, n, :], ones[0:EXPERTS, :], rb_sb[:, n:n + 1], None,
                                  ALU.mult).then_inc(rbc_s, 1)
            mm_rest(1)
            mm_rest(2)
            attention_rest(STEPS - 2)
            dve.wait_ge(lr_mm, 1)
            dve.wait_ge(lbias, 1)
            dve.tensor_copy(low_rank_in[:], ps_v[:, 0:NC * ZL].rearrange("p (c z) -> p c z", z=ZL)).then_inc(lr_out, 1)
            dve.wait_ge(lr_out, 1)
            dve.tensor_tensor(logit_bias[:, 1, :], logit_bias[:, 0, :], ps_v[:, 144:148], ALU.add).then_inc(lr_out, 1)
            mm_rest(3)
            step(TURNS - 1, 7, drain=True)
            dve.wait_ge(lb_mm, 1)
            dve.tensor_copy(low_rank_out[0:ACTIVE * RANK, :], ps_v[0:ACTIVE * RANK, :]).then_inc(lb_out, 1)

            def statistics(stage, b, before, count):
                dve.wait_ge(before, count)
                dve.bn_stats(t_stats[:, stage, b, :], acc[:, b, :]).then_inc(n_st[stage], 1)
                dve.wait_ge(n_st[stage], b + 1)
                dve.bn_aggr(t_mv[:, stage, b, :], t_stats[:, stage, b, :]).then_inc(n_mv[stage], 1)

            def normalise_end(b):
                dve.wait_ge(n_rs[1], b + 1)
                wait_from(dve, n_t[1], b)
                if b == 0:
                    dve.wait_ge(kb_mm, 1)
                dve.tensor_scalar(normed[:, 1, :], acc[:, b, :], t_mv[:, 1, b, 0:1], t_rstd[:, 1, b:b + 1],
                                  ALU.subtract, ALU.mult).then_inc(n_xn[1], 1)

            def a_rest(b):
                dve.wait_ge(a_hi_s, b + 1)
                dve.tensor_tensor(a_lo[:], blocks(ps_s), a_hi[:].bitcast(F32), ALU.subtract).then_inc(a_lo_s, 1)

            def a_route(b):
                dve.wait_ge(z_mm, b + 1)
                dve.tensor_tensor(logits[:, b, :], ps_k[:, ACTIVE * RANK:ZL], logit_bias[:, 1, :],
                                  ALU.add).then_inc(lg_c, 1)
                dve.wait_ge(lg_c, 3 * b + 1)
                dve.tensor_reduce(l_max[:, b, 0:1], logits[:, b, :], AX_X, ALU.max).then_inc(lg_c, 1)
                dve.wait_ge(lg_c, 3 * b + 2)
                dve.tensor_scalar(l_max[:, b, 1:2], l_max[:, b, 0:1], -1.0, None, ALU.mult).then_inc(lg_c, 1)

            def a_mix(b):
                dve.wait_ge(lg_exp, b + 1)
                dve.reciprocal(l_sum[:, b, 1:2], l_sum[:, b, 0:1]).then_inc(z_mixed, 1)
                dve.wait_ge(z_mixed, 3 * b + 1)
                dve.tensor_scalar(alpha[:, b, :], l_exp[:, b, :], l_sum[:, b, 1:2], LORA_SCALE, ALU.mult,
                                  ALU.mult).then_inc(z_mixed, 1)
                dve.wait_ge(z_mixed, 3 * b + 2)
                wait_from(dve, zt_mm, b - 1)
                dve.tensor_tensor(z_mix[:, b % 2, 0:ACTIVE * RANK].rearrange("p (e r) -> p e r", r=RANK),
                                  ps_k[:, 0:ACTIVE * RANK].rearrange("p (e r) -> p e r", r=RANK),
                                  alpha[:, b, :].unsqueeze(2).broadcast_to([P, ACTIVE, RANK]),
                                  ALU.mult).then_inc(z_mixed, 1)

            def a_finish(b):
                dve.wait_ge(y_mm, b + 1)
                dve.wait_ge(n_xn[0], b + 1)
                dve.tensor_tensor(acc[:, b, :], ps_q[:], acc[:, b, :], ALU.add).then_inc(a_add, 1)

            def b_softmax(b):
                dve.wait_ge(bs_mm, b + 1)
                dve.tensor_reduce(b_max[:, b, 0:1], ps_v[:, 0:P], AX_X, ALU.max).then_inc(b_c, 1)
                dve.wait_ge(b_c, 2 * b + 1)
                dve.tensor_scalar(b_max[:, b, 1:2], b_max[:, b, 0:1], -SCORE_SCALE, None, ALU.mult).then_inc(b_c, 1)

            def b_finish(b):
                dve.wait_ge(b_exp, b + 1)
                dve.reciprocal(b_sum[:, b, 1:2], b_sum[:, b, 0:1]).then_inc(b_inv, 1)
                dve.wait_ge(b_inv, b + 1)
                dve.wait_ge(at_mm, b + 1)
                dve.scalar_tensor_tensor(acc[:, b, :], ps_o[0][:], b_sum[:, b, 1:2], acc[:, b, :], ALU.mult,
                                         ALU.add).then_inc(b_add, 1)

            def c_rest(b):
                dve.wait_ge(c_hi_s, b + 1)
                dve.tensor_tensor(c_lo[:], blocks(ps_pv), c_hi[:].bitcast(F32), ALU.subtract).then_inc(c_lo_s, 1)

            def c_scale(b):
                dve.wait_ge(c_mm, b + 1)
                wait_from(dve, c_add, b - 1)
                dve.tensor_tensor(f_scr[2 + b % 2][:], ps_o[1][:], scale_rows[:], ALU.mult).then_inc(c_scaled, 1)

            def ready(b):
                return 2 * (STEPS - 2) if b < 4 else 2 * STEPS

            statistics(0, 0, o_added, ready(0))
            g_evac(0)
            r_batch(0)
            r_batch(1)
            g_evac(1)
            attention_rest(STEPS - 1)
            r_batch(2)
            r_batch(3)
            g_evac(2)
            add_output(STEPS - 1, LOOP_STEPS - 1)
            for b in range(4, BATCH):
                r_batch(b)
            g_evac(3)
            dve.wait_ge(r_sum, BATCH)
            dve.wait_ge(vec_out, 1)
            dve.tensor_scalar(r_col[:, 1, :], r_col[:, 0, :], uw[:, NC:NC + 1], None, ALU.add).then_inc(r_col_s, 1)
            for w in range(BATCH + 3):
                a, b, b_end, c = w, w - 1, w - 2, w - 3
                has_a, has_b, has_b_end, has_c = (0 <= t < BATCH for t in (a, b, b_end, c))
                if has_b:
                    statistics(1, b, a_add, b + 1)
                if has_a:
                    a_rest(a)
                if has_b:
                    normalise_end(b)
                if w < 2:
                    unpack_code(2 * w)
                if has_b_end:
                    b_finish(b_end)
                if w < 2:
                    g_evac(4 + 2 * w)
                if has_a:
                    a_route(a)
                if has_b_end:
                    statistics(2, b_end, b_add, b_end + 1)
                if has_c:
                    c_scale(c)
                if has_a:
                    a_mix(a)
                if a + 1 < BATCH:
                    statistics(0, a + 1, o_added, ready(a + 1))
                if has_b:
                    b_softmax(b)
                if w < 2:
                    unpack_code(2 * w + 1)
                if b_end == 0:
                    dve.wait_ge(rows_in, 48)
                    dve.scalar_tensor_tensor(shift_rows[:], zero_rows[:], -1.0, scale_rows[:], ALU.mult,
                                             ALU.mult).then_inc(shift_s, 1)
                if w < 2:
                    g_evac(5 + 2 * w)
                if has_a:
                    a_finish(a)
                if has_b_end:
                    c_rest(b_end)
            dve.wait_ge(c_scaled, BATCH)
            dve.wait_ge(c_rest_s, BATCH)
            dve.wait_ge(c_add, BATCH - 1)
            dve.tensor_tensor(acc[:, BATCH - 1, :], f_scr[2 + (BATCH - 1) % 2][:], f_scr[(BATCH - 1) % 2][:],
                              ALU.add).then_inc(c_add, 1)

        @block.tensor
        def _(pe):
            def project_k(t, c, first_use=False, bank=ps_k):
                head, half = c % 2, c // 2 % 2
                cols = slice(half * HALF, (half + 1) * HALF)
                for m in range(NC):
                    if first_use:
                        pe.wait_ge(ct_lo_done, NC * half + m + 1)
                    last = three(pe, bank[:], wk_hi[:, head, m, :], wk_lo[:, head, m, :], ct_hi[:, m, cols],
                                 ct_lo[:, m, cols], m == 0, m == NC - 1)
                last.then_inc(k_done, 1)

            def project_q(t, c, bank=ps_q):
                head, half = c % 2, c // 2 % 2
                cols = slice(half * HALF, (half + 1) * HALF)
                for m in range(NC):
                    last = three(pe, bank[:], wq_hi[:, head, m, :], wq_lo[:, head, m, :], xt_hi[:, m, cols],
                                 xt_lo[:, m, cols], m == 0, m == NC - 1)
                last.then_inc(q_done, 1)

            def project_v(t, c, bank=ps_v):
                n, first = c // 4 % 2, 4 * (c // 2 % 2) + 2 * (c % 2)
                for j in range(2):
                    cols = slice((first + j) * P, (first + j + 1) * P)
                    for m in range(NC):
                        last = three(pe, bank[:, j * 2 * P:(j + 1) * 2 * P], ct_hi[:, m, cols], ct_lo[:, m, cols],
                                     wv_hi[n][:, m, :], wv_lo[n][:, m, :], m == 0, m == NC - 1)
                last.then_inc(v_done, 1)

            def x_transpose(b):
                pe.wait_ge(x_h, b + 1)
                wait_from(pe, x_lo, b - 3)
                for m in range(NC):
                    last = pe.transpose(x_banks[b % 4][:, m * P:(m + 1) * P], rms_in[b % 3][:, m * P:(m + 1) * P],
                                        ident[:])
                last.then_inc(x_t, 1)

            pe.wait_ge(wk_lo_s, 1)
            project_k(0, 0, first_use=True)
            pe.wait_ge(wk_lo_s, 2)
            project_k(1, 1, bank=ps_q)
            pe.wait_ge(wv_lo_s, 1)
            pe.wait_ge(wv0_lo_s, 1)
            project_v(0, 0)
            project_v(1, 1, bank=ps_s)
            pe.wait_ge(ident_done, 1)
            x_transpose(0)
            x_transpose(1)
            pe.wait_ge(k_out, 1)
            project_k(2, 2, first_use=True)
            x_transpose(2)
            x_transpose(3)
            pe.wait_ge(k_out, 3)
            project_k(3, 3)
            x_transpose(4)
            x_transpose(5)
            pe.wait_ge(x_lo, 4)
            pe.wait_ge(wq_lo_s, 1)
            project_q(0, 0)
            x_transpose(6)
            pe.wait_ge(wq_lo_s, 2)
            pe.wait_ge(k_out, 4)
            project_q(1, 1, bank=ps_k)
            x_transpose(7)

            def output(s, c, g=None):
                wait_from(pe, att_lo_s, s + 1)
                if g is not None:
                    pe.wait_ge(wo_lo_s, g + 1)
                n = c // 4 % 2
                for j in range(2):
                    wait_from(pe, o_added, 2 * s + j - 1)
                    for h in range(2):
                        last = three(pe, ps_o[j][:], att_hi[:, 2 * j + h, :], att_lo[:, 2 * j + h, :],
                                     wo_hi[n][:, h, :], wo_lo[n][:, h, :], h == 0, h == 1)
                    last.then_inc(o_done, 1)

            def step_scores(s, c):
                u0 = s - c % 2
                pe.wait_ge(q_out, u0 + 2)
                pe.wait_ge(k_out, u0 + 2)
                wait_from(pe, s_shifted, s)
                n = c // 2 % 2
                for j in range(2):
                    cols = slice((2 * (c % 2) + j) * P, (2 * (c % 2) + j + 1) * P)
                    for h in range(2):
                        m = 2 * j + h
                        last = pe.matmul(ps_s[:, m * P:(m + 1) * P], qt[n][:, h, cols], kt[n][:, h, cols],
                                         start=True, stop=True)
                last.then_inc(s_done, 1)

            def step_transpose(s, c):
                pe.wait_ge(p_done, s + 1)
                wait_from(pe, pt_out, s)
                for m in range(4):
                    last = pe.transpose(ps_t[:, m * P:(m + 1) * P], probs[c % 2][:, m, :], ident[:])
                last.then_inc(pt_done, 1)

            def step_values(s, c):
                pe.wait_ge(pt_out, s + 1)
                pe.wait_ge(v_out, s - c % 2 + 2)
                wait_from(pe, att_lo_s, s)
                n = c // 2 % 2
                for j in range(2):
                    for h in range(2):
                        m = 2 * j + h
                        last = pe.matmul(ps_pv[:, m * P:(m + 1) * P], vv[n][:, 2 * (c % 2) + j, h * P:(h + 1) * P],
                                         probs_t[:, m, :], start=True, stop=True)
                last.then_inc(pv_done, 1)

            def step(i, c):
                s = LOOP_STEPS * i + c
                t, tc = s + 2, (c + 2) % LOOP_STEPS
                gt = 2 * i + (c + 2) // 4
                step_scores(s, c)
                if isinstance(i, int) and s == 0:
                    pe.wait_ge(x_lo, 8)
                ahead = not isinstance(i, int) or s > 1
                pe.wait_ge(wq_lo_s, 2 * gt + c % 2 + 1)
                pe.wait_ge(q_out, t)
                project_q(t, tc)
                if c > 0 or not isinstance(i, int) or i > 0:
                    output(s - 1, (c - 1) % LOOP_STEPS, 2 * i + c // 4 if c % 4 == 1 else None)
                if ahead:
                    pe.wait_ge(wk_lo_s, 2 * gt + c % 2 + 1)
                    pe.wait_ge(k_out, t)
                    project_k(t, tc)
                first = isinstance(i, int) and s == 0
                if not first:
                    step_transpose(s, c)
                pe.wait_ge(wv_lo_s, gt + 1)
                pe.wait_ge(v_out, t)
                project_v(t, tc)
                if first:
                    step_transpose(s, c)
                step_values(s, c)

            for c in range(LOOP_STEPS):
                step(0, c)
            with pe.Fori(1, TURNS - 1) as i:
                for c in range(LOOP_STEPS):
                    step(i, c)
            for c in range(6):
                step(TURNS - 1, c)

            def product_m(m):
                if m == 0:
                    pe.wait_ge(w1_lo_s, NC)
                    pe.wait_ge(q_out, STEPS)
                    pe.wait_ge(k_out, STEPS)
                wait_from(pe, mm_out, m - 1)
                cols = slice(m * P, (m + 1) * P)
                for c in range(NC):
                    if m == 0:
                        pe.wait_ge(w1_lo_s, NC + c + 1)
                    last = three(pe, (ps_q, ps_k)[m % 2][:], wk1_hi[:, c, cols], wk1_lo[:, c, cols], wq1_hi[:, c, :],
                                 wq1_lo[:, c, :], c == 0, c == NC - 1)
                last.then_inc(mm_done, 1)

            def product_g(n):
                m, half = n % NC, n // NC
                if n == 0:
                    pe.wait_ge(mm_out, NC)
                if n == 2:
                    pe.wait_ge(lb_out, 1)
                if n == 3:
                    pe.wait_ge(pt_out, STEPS)
                if n == 4:
                    pe.wait_ge(att_lo_s, STEPS)
                if n == 5:
                    pe.wait_ge(o_added, 2 * STEPS)
                if n > 5:
                    pe.wait_ge(g_out, n - 1)
                cols, rows = slice(m * P, (m + 1) * P), slice(half * HALF, (half + 1) * HALF)
                for c in range(NC):
                    last = three(pe, g_banks[n][:], mm_hi[:, c, cols], mm_lo[:, c, cols], ct_hi[:, c, rows],
                                 ct_lo[:, c, rows], c == 0, c == NC - 1)
                last.then_inc(g_done, 1)

            def spread_kb():
                pe.wait_ge(sel_s, 1)
                pe.matmul(ps_v[:], ones[:], normed[:, 1, :], start=True, stop=True).then_inc(kb_mm, 1)

            s = STEPS - 2
            step_scores(s, 6)
            product_m(0)
            pe.wait_ge(v_out, STEPS)
            pe.wait_ge(vec_acc, 2 * NC)
            pe.wait_ge(bqk_s, 2)
            pe.wait_ge(const_done, 4)
            for m in range(NC):
                pe.matmul(ps_v[:, m:m + 1], normed[:, 0, m * P:(m + 1) * P], ones[:, 0:1], start=True, stop=True)
            pe.matmul(ps_v[:, NC:NC + 1], ones[:], bqk_sum[:], start=True, stop=True).then_inc(vec_mm, 1)
            output(s - 1, 5)
            pe.wait_ge(vec_out, 1)
            pe.wait_ge(act_chain, 10)
            pe.matmul(ps_v[:, 0:ZL], ones[0:1, :], targets[:], start=True, stop=True).then_inc(tgt_mm, 1)
            product_m(1)
            spread_kb()
            step_transpose(s, 6)
            product_m(2)
            step_values(s, 6)
            pe.wait_ge(kb_s, 1)
            pe.wait_ge(rbc_s, 2)
            pe.wait_ge(lora_in, 48)
            for c in range(NC):
                cols = slice(c * P, (c + 1) * P)
                pe.matmul(ps_v[:, c * ZL:c * ZL + ACTIVE * RANK], lora_a_sb[:, cols], select[:, 0:ACTIVE * RANK],
                          start=True, stop=True)
                pe.matmul(ps_v[:, c * ZL + ACTIVE * RANK:(c + 1) * ZL], router_sb[:, cols],
                          select[0:EXPERTS, ACTIVE * RANK:ZL], start=True, stop=True)
            for n in range(2):
                last = pe.matmul(ps_v[:, NC * ZL + ACTIVE * n:NC * ZL + ACTIVE * (n + 1)], rb_cols[:, n, :],
                                 select[0:EXPERTS, ACTIVE * RANK:ZL], start=True, stop=True)
            last.then_inc(lr_mm, 1)
            product_m(3)
            s = STEPS - 1
            step_scores(s, 7)
            output(s - 1, 6)
            pe.wait_ge(lr_out, 2)
            pe.matmul(ps_v[0:ACTIVE * RANK, :], select[:, 0:ACTIVE * RANK], lora_b_sb[:], start=True,
                      stop=True).then_inc(lb_mm, 1)
            product_g(0)
            step_transpose(s, 7)
            product_g(1)
            step_values(s, 7)
            product_g(2)
            output(s, 7)
            product_g(3)

            banks = (ps_s, ps_t, ps_pv)

            def transpose(stage, b, freed):
                pe.wait_ge(n_xn[stage], b + 1)
                wait_from(pe, freed, b)
                if b == 0 and stage == 0:
                    pe.wait_ge(s_shifted, STEPS)
                if b == 0 and stage == 1:
                    pe.wait_ge(g_out, 4)
                if b == 0 and stage == 2:
                    pe.wait_ge(g_out, 2 * NC - 1)
                for m in range(NC):
                    src = normed[:, stage, m * P:(m + 1) * P] if stage < 2 else normed[:, stage, m:D:NC]
                    last = pe.transpose(banks[stage][:, m * P:(m + 1) * P], src, ident[:])
                last.then_inc(n_t[stage], 1)

            def a_low_rank(b):
                pe.wait_ge(a_full_s, b + 1)
                if b == 0:
                    pe.wait_ge(g_out, 2)
                wait_from(pe, zt_out, b)
                wait_from(pe, z_mixed, 3 * b)
                for c in range(NC):
                    last = pe.matmul(ps_k[:, 0:ZL], a_full[:, c, :], low_rank_in[:, c, :], start=(c == 0),
                                     stop=(c == NC - 1))
                last.then_inc(z_mm, 1)

            def a_base(b, part):
                if part == 0:
                    pe.wait_ge(a_lo_s, b + 1)
                    if b == 0:
                        pe.wait_ge(base_lo_s, NC)
                        pe.wait_ge(g_out, 1)
                    wait_from(pe, a_add, b)
                for c in (2 * part, 2 * part + 1):
                    three(pe, ps_q[:], a_hi[:, c, :], a_lo[:, c, :], base_hi[:, c, :], base_lo[:, c, :], c == 0, False)

            def a_mix_t(b):
                pe.wait_ge(z_mixed, 3 * b + 3)
                pe.transpose(ps_k[0:ACTIVE * RANK + 1, P:2 * P], z_mix[:, b % 2, :], ident[:]).then_inc(zt_mm, 1)

            def a_end(b):
                pe.wait_ge(zt_out, b + 1)
                pe.matmul(ps_q[:], z_mix_t[:], low_rank_out[:], start=False, stop=True).then_inc(y_mm, 1)

            def b_scores(b):
                pe.wait_ge(b_full_s, b + 1)
                wait_from(pe, bt_out, b)
                pe.wait_ge(g_out, NC if b < 4 else 2 * NC)
                pe.wait_ge(r_diag_s, b + 1)
                cols = slice(b * P, (b + 1) * P)
                for c in range(NC):
                    pe.matmul(ps_v[:, 0:P], b_full[:, c, :], gg[:, c, cols], start=(c == 0), stop=False)
                pe.matmul(ps_v[:, 0:P], ones[:], r_diag[b % 2][:], start=False, stop=True).then_inc(bs_mm, 1)

            def b_transpose(b):
                pe.wait_ge(b_exp, b + 1)
                pe.transpose(ps_v[:, 2 * P:3 * P], b_probs[:], ident[:]).then_inc(bt_mm, 1)

            def b_attend(b):
                pe.wait_ge(bt_out, b + 1)
                if b == 0:
                    pe.wait_ge(ctx_in, 16)
                    pe.wait_ge(o_added, 2 * STEPS)
                wait_from(pe, b_add, b)
                pe.matmul(ps_o[0][:], b_probs_t[:], ctx_sb[:, b, :], start=True, stop=True).then_inc(at_mm, 1)

            def c_product(b):
                pe.wait_ge(c_lo_s, b + 1)
                if b == 0:
                    pe.wait_ge(codes_s, 4)
                    pe.wait_ge(g_out, 2 * NC)
                wait_from(pe, c_scaled, b)
                for c in range(NC):
                    pe.matmul(ps_o[1][:], c_hi[:, c, :], codes[:, c, :], start=(c == 0), stop=False)
                    last = pe.matmul(ps_o[1][:], c_lo[:, c, :], codes[:, c, :], start=False, stop=(c == NC - 1))
                last.then_inc(c_mm, 1)

            for w in range(BATCH + 3):
                a, b, b_end, c = w, w - 1, w - 2, w - 3
                has_a, has_b, has_b_end, has_c = (0 <= t < BATCH for t in (a, b, b_end, c))
                if has_a:
                    transpose(0, a, a_lo_s)
                if has_b_end:
                    b_attend(b_end)
                if has_c:
                    c_product(c)
                if w < 2:
                    product_g(4 + 2 * w)
                if has_a:
                    a_low_rank(a)
                if has_b:
                    transpose(1, b, b_full_s)
                if has_a:
                    a_base(a, 0)
                if has_b:
                    b_scores(b)
                if has_a:
                    a_base(a, 1)
                    a_mix_t(a)
                if w < 2:
                    product_g(5 + 2 * w)
                if w == BATCH:
                    b_transpose(b)
                if has_b_end:
                    transpose(2, b_end, c_lo_s)
                if has_b and w < BATCH:
                    b_transpose(b)
                if has_a:
                    a_end(a)


def kernel(**inputs):
    import numpy as np
    import concourse.bacc as bacc
    from concourse.bass_utils import run_bass_kernel_spmd

    def get(name):
        return np.asarray(inputs[name])

    def keep(a):
        return np.ascontiguousarray(a)

    g = GROUPS
    arrays = {
        "x": keep(get("x").reshape(TOK, D)),
        "ctx_nat": keep(get("ctx_4096").reshape(TOK, D)),
        "ctx_t": keep(get("ctx_4096").reshape(TOK, NC, P).transpose(2, 1, 0)),
        "mask": keep(get("mask_BxSxS2_bk0").transpose(1, 0, 2)),
        "bias": keep(get("L0_xattn_position_bias").reshape(g, 2, P, P).transpose(0, 2, 1, 3)),
        "ln_w": keep(get("L0_xattn_ln_weight").reshape(1, D)),
        "w_q": keep(get("L0_xattn_w_q").reshape(g, 2, P, NC, P).transpose(0, 4, 1, 3, 2).reshape(g, P, 2 * D)),
        "w_k": keep(get("L0_xattn_w_k").reshape(g, 2, P, NC, P).transpose(0, 4, 1, 3, 2).reshape(g, P, 2 * D)),
        "w_v": keep(get("L0_xattn_w_v").reshape(g, 2 * P, NC, P).transpose(0, 3, 2, 1).reshape(g, P, 2 * D)),
        "w_o": keep(get("L0_xattn_w_out").reshape(D, g, 2, P).transpose(1, 3, 2, 0).reshape(g, P, 2 * D)),
        "w_base": keep(get("L0_ffn_W_base").reshape(D, NC, P).transpose(2, 1, 0)),
        "b_base": keep(get("L0_ffn_b_base").reshape(1, D)),
        "lora_a": keep(get("L0_ffn_lora_A").reshape(EXPERTS * RANK, D)),
        "lora_b": keep(get("L0_ffn_lora_B").transpose(0, 2, 1).reshape(EXPERTS * RANK, D)),
        "router_w": keep(get("L0_ffn_router_W")),
        "router_b": keep(get("L0_ffn_router_b").reshape(EXPERTS, 1)),
        "prior": keep(get("L0_ffn_domain_prior").reshape(EXPERTS, 1)),
        "active": keep(get("L0_ffn_active").reshape(1, ACTIVE)),
        "wq1": keep(get("L1_xattn_Wq").reshape(NC, P, D).transpose(1, 0, 2)),
        "bq1": keep(get("L1_xattn_bq").reshape(NC, P).T),
        "wk1": keep(get("L1_xattn_Wk").reshape(NC, P, D).transpose(1, 0, 2)),
        "bk1": keep(get("L1_xattn_bk").reshape(NC, P).T),
        "qweight": keep(get("L1_ffn_qweight").reshape(D, P, 3).transpose(1, 2, 0)),
        "w_scale": keep(get("L1_ffn_weight_scale").reshape(1, D)),
        "w_zero": keep(get("L1_ffn_weight_zero_point").reshape(1, D)),
        "ffn_bias": keep(get("L1_ffn_bias").reshape(1, D)),
    }
    nc = bacc.Bacc("TRN2", target_bir_lowering=False, num_devices=1)
    args = [nc.dram_tensor(f"in_{name}", a.shape, mybir.dt.from_np(a.dtype), kind="ExternalInput").ap()
            for name, a in arrays.items()]
    args.append(nc.dram_tensor("out_x", (TOK, D), F32, kind="ExternalOutput").ap())
    build(nc, *args)
    done = run_bass_kernel_spmd(nc, [{f"in_{name}": a for name, a in arrays.items()}], core_ids=[0])
    return done.results[0]["out_x"].reshape(BATCH, P, D)
```
